# Optimizing a Trainium2 kernel written in Bass

```python
import numpy as np
import jax
import jax.numpy as jnp

def _softmax(x, axis=-1):
    return jax.nn.softmax(x, axis=axis)

def _gelu(x):
    return jax.nn.gelu(x, approximate=True)

def _silu(x):
    return jax.nn.silu(x)

def _sigmoid(x):
    return jax.nn.sigmoid(x)

def _layernorm(x, axis=-1, eps=1e-05):
    m = jnp.mean(x, axis=axis, keepdims=True)
    v = jnp.var(x, axis=axis, keepdims=True)
    return (x - m) / jnp.sqrt(v + eps)

def _scatter_add(tgt, idx, src, axis=0):
    return tgt.at[idx].add(src)

def _segment_sum(src, seg, n):
    return jax.ops.segment_sum(src, seg, n)
kernel_name = 'mk_gnn_resnorm_d2_gnn_r8_679d80'

def setup_inputs(seed: int=0):
    np.random.seed(seed)
    _w = jnp.asarray

    def _rec_inputs():
        import jax
        import jax.numpy as jnp
        _gk = jax.random.key(seed)
        x = -0.0005121 + 1.001 * jax.random.normal(jax.random.fold_in(_gk, 1), (12500, 64), jnp.float32)
        src = jax.random.randint(jax.random.fold_in(_gk, 2), (400000,), 0, 12500, jnp.int32)
        dst = jax.random.randint(jax.random.fold_in(_gk, 3), (400000,), 0, 12500, jnp.int32)
        _o = jnp.argsort(dst, stable=True)
        src = src[_o]
        dst = dst[_o]
        return (x, src, dst)
    x, src, dst = _rec_inputs()

    def _L0_gnn_setup():
        import jax, jax.numpy as jnp
        import numpy as np
        N_NODES = 6250
        N_EDGES = 100000
        D_IN = 64
        D_HID = 128
        D_OUT = 64
        key = jax.random.key(seed)
        k0, k1, k2, k3 = jax.random.split(key, 4)
        x = jax.random.normal(k0, (N_NODES, D_IN), dtype=jnp.float32)
        edge_index = jax.random.randint(k1, (2, N_EDGES), 0, N_NODES, dtype=jnp.int32)
        W1 = jax.random.normal(k2, (2 * D_IN, D_HID), dtype=jnp.float32) * 0.05
        b1 = jnp.zeros((D_HID,), dtype=jnp.float32)
        W2 = jax.random.normal(k3, (D_HID, D_OUT), dtype=jnp.float32) * 0.05
        b2 = jnp.zeros((D_OUT,), dtype=jnp.float32)
        return {'x': x, 'edge_index': edge_index, 'W1': W1, 'b1': b1, 'W2': W2, 'b2': b2}
    _L0_gnn_all = _L0_gnn_setup()
    _L0_gnn_in = {k: v for k, v in _L0_gnn_all.items() if k in ('W1', 'b1', 'W2', 'b2')}
    del _L0_gnn_all

    def _L1_gnn_setup():
        import jax, jax.numpy as jnp
        import numpy as np
        N_NODES = 12500
        N_EDGES = 200000
        HIDDEN = 64

        def gcn_conv(x, edge_index, W, b):
            n = x.shape[0]
            h = x @ W
            loop = jnp.arange(n, dtype=edge_index.dtype)
            src = jnp.concatenate([edge_index[0], loop])
            dst = jnp.concatenate([edge_index[1], loop])
            deg = jax.ops.segment_sum(jnp.ones_like(dst, dtype=h.dtype), dst, num_segments=n)
            dinv = jnp.where(deg > 0, jax.lax.rsqrt(jnp.maximum(deg, 1e-12)), 0.0)
            norm = dinv[src] * dinv[dst]
            msg = h[src] * norm[:, None]
            out = jax.ops.segment_sum(msg, dst, num_segments=n)
            return out + b
        key = jax.random.key(seed)
        k = jax.random.split(key, 6)
        x = jax.random.normal(k[0], (N_NODES, HIDDEN), dtype=jnp.float32)
        edge_index = jax.random.randint(k[1], (2, N_EDGES), 0, N_NODES, dtype=jnp.int32)
        s = 1.0 / np.sqrt(HIDDEN)
        W1 = jax.random.normal(k[2], (HIDDEN, HIDDEN), dtype=jnp.float32) * s
        b1 = jnp.zeros((HIDDEN,), dtype=jnp.float32)
        W2 = jax.random.normal(k[3], (HIDDEN, HIDDEN), dtype=jnp.float32) * s
        b2 = jnp.zeros((HIDDEN,), dtype=jnp.float32)
        return {'x': x, 'edge_index': edge_index, 'W1': W1, 'b1': b1, 'W2': W2, 'b2': b2}
    _L1_gnn_all = _L1_gnn_setup()
    _L1_gnn_in = {k: v for k, v in _L1_gnn_all.items() if k in ('W1', 'b1', 'W2', 'b2')}
    del _L1_gnn_all
    return {'x': x, 'src': src, 'dst': dst, 'L0_gnn_W1': _L0_gnn_in['W1'], 'L0_gnn_b1': _L0_gnn_in['b1'], 'L0_gnn_W2': _L0_gnn_in['W2'], 'L0_gnn_b2': _L0_gnn_in['b2'], 'L1_gnn_W1': _L1_gnn_in['W1'], 'L1_gnn_b1': _L1_gnn_in['b1'], 'L1_gnn_W2': _L1_gnn_in['W2'], 'L1_gnn_b2': _L1_gnn_in['b2']}

def reference(x, src, dst, L0_gnn_W1, L0_gnn_b1, L0_gnn_W2, L0_gnn_b2, L1_gnn_W1, L1_gnn_b1, L1_gnn_W2, L1_gnn_b2):
    import jax
    import jax.numpy as jnp

    def _L0_gnn_ref(x, edge_index, W1, b1, W2, b2):
        import jax, jax.numpy as jnp
        import numpy as np
        N_NODES = 6250
        N_EDGES = 100000
        D_IN = 64
        D_HID = 128
        D_OUT = 64
        row, col = (edge_index[0], edge_index[1])
        x_row = x[row]
        x_col = x[col]
        h = jnp.concatenate([x_row, x_col - x_row], axis=1)
        h = jax.nn.relu(h @ W1 + b1)
        h = h @ W2 + b2
        out = jax.ops.segment_max(h, row, num_segments=x.shape[0])
        out = jnp.where(jnp.isfinite(out), out, jnp.zeros_like(out))
        return out

    def _L1_gnn_ref(x, edge_index, W1, b1, W2, b2):
        import jax, jax.numpy as jnp
        import numpy as np
        N_NODES = 12500
        N_EDGES = 200000
        HIDDEN = 64

        def gcn_conv(x, edge_index, W, b):
            n = x.shape[0]
            h = x @ W
            loop = jnp.arange(n, dtype=edge_index.dtype)
            src = jnp.concatenate([edge_index[0], loop])
            dst = jnp.concatenate([edge_index[1], loop])
            deg = jax.ops.segment_sum(jnp.ones_like(dst, dtype=h.dtype), dst, num_segments=n)
            dinv = jnp.where(deg > 0, jax.lax.rsqrt(jnp.maximum(deg, 1e-12)), 0.0)
            norm = dinv[src] * dinv[dst]
            msg = h[src] * norm[:, None]
            out = jax.ops.segment_sum(msg, dst, num_segments=n)
            return out + b
        h = gcn_conv(x, edge_index, W1, b1)
        h = jax.nn.relu(gcn_conv(h, edge_index, W1, b1))
        h = gcn_conv(h, edge_index, W2, b2)
        return jax.nn.log_softmax(h, axis=1)
    edge_index = jnp.stack([src, dst])
    x = _layernorm(x + _L0_gnn_ref(x, edge_index, L0_gnn_W1, L0_gnn_b1, L0_gnn_W2, L0_gnn_b2), axis=-1)
    x = _layernorm(x + _L1_gnn_ref(x, edge_index, L1_gnn_W1, L1_gnn_b1, L1_gnn_W2, L1_gnn_b2), axis=-1)
    return x

_drawn_inputs = setup_inputs


def setup_inputs(seed=0):
    import zlib

    import numpy as np

    out = dict(_drawn_inputs(seed))
    spreads = {'L0_gnn_b1': (0.0, 0.1),
     'L0_gnn_b2': (0.0, 0.1),
     'L1_gnn_b1': (0.0, 0.1),
     'L1_gnn_b2': (0.0, 0.1)}
    factors = {}
    for name, (base, spread) in spreads.items():
        noise = np.random.default_rng([zlib.crc32(name.encode()), seed]).standard_normal(out[name].shape)
        drawn = base * np.exp(spread * noise) if base else spread * noise
        out[name] = jnp.asarray(drawn.astype(out[name].dtype))
    for name, factor in factors.items():
        out[name] = (out[name] * factor).astype(out[name].dtype)
    return out
```

```python
import concourse.bass as bass
from concourse import mybir
from contextlib import ExitStack

P = 128
N_NODES, CH, HID = 12500, 64, 128
N_EDGES = 400000
NBLK = -(-N_NODES // P)
LAST = N_NODES - (NBLK - 1) * P
NC = NBLK * CH
LOGW = 12
W = 1 << LOGW
SORTED = P * W
NODE_BITS = 14
LOW = (1 << NODE_BITS) - 1
REAL = 0x20000000
PAD = 0x30000000
TILES = 16
NCH = -(-N_EDGES // (P * TILES))
NCH += NCH % 2
NT = NCH * TILES
HALF = TILES // 2
GROUPS = TILES // 4
CREDIT = 8
BIG = 1.5e38
EPS = 1e-5
PAIRS = NBLK // 2
PPI = 7
SIGNS = 8


def gnn(nc, x, src, dst, w1, b1, w2, b2, cw1, cb1, cw2, cb2, out):
    f32, bf16, i32 = mybir.dt.float32, mybir.dt.bfloat16, mybir.dt.int32
    ALU, ACT, AX = mybir.AluOpType, mybir.ActivationFunctionType, mybir.AxisListType

    ctx = ExitStack()
    with ctx:
        def sb(name, shape, dt):
            return ctx.enter_context(nc.sbuf_tensor(name, shape, dt))

        def sem(name):
            return ctx.enter_context(nc.semaphore(name))

        def dram(name, shape, dt):
            return nc.dram_tensor(name, shape, dt, kind="Internal").ap()

        d_edge = dram("edges", (4, N_EDGES), i32)
        d_a = dram("table_a", (NBLK * P, HID), f32)
        d_b = dram("table_b", (NBLK * P, HID), f32)
        d_h = dram("table_h", (NBLK * P, CH), f32)
        d_keys = dram("sorted_keys", (SORTED // CH, CH), f32)
        d_sub = dram("sub_heads", (P, CH), f32)
        d_head = dram("heads", (P, 1), f32)
        d_last = dram("last_keys", (P, 1), f32)
        d_keep = dram("keep", (2, SORTED), bf16)
        d_pen = dram("penalty", (2, SORTED), bf16)
        d_rows = dram("scan_rows", (NT * P, CH), f32)

        X = sb("X", [P, NC], f32)
        NE = N_EDGES // P
        EX = sb("EX", [P, NC], f32)
        HP = sb("HP", [P, NC], f32)
        arena = sb("arena", [P, 2 * W], f32)
        keyb = [arena[:, 0:W], arena[:, W:2 * W]]
        TMP = arena[:, 0:NC]
        idx_lo = sb("idx_lo", [P, 2 * NT], i32)
        idx_hi = sb("idx_hi", [P, NT], i32)
        keep = sb("keep_sb", [P, W], bf16)
        pen = sb("pen_sb", [P, W], bf16)
        msk = [keep[0:CH, k * TILES * P:(k + 1) * TILES * P] for k in range(2)]
        stage = sb("stage", [P, PPI * P], f32)
        stageT = sb("stageT", [P, PPI * P], f32)
        outr = sb("outr", [P, 2, TILES * CH], f32)
        R = sb("R", [P, 2, 512], f32)
        S = sb("S", [CH, 2, 512], f32)
        stg = sb("stg", [P, 2, 2 * TILES], i32)
        ident = sb("ident", [P, P], f32)
        shift = sb("shift", [P, P], f32)
        wrap = sb("wrap", [P, P], f32)
        w_ab = sb("w_ab", [P, 4 * P], f32)
        w1b = sb("w1b", [P, HID], f32)
        w2s = sb("w2s", [HID, CH], f32)
        b1r = sb("b1r", [1, 4 * P], f32)
        ones1 = sb("ones1", [1, P], f32)
        b2b = sb("b2b", [P, CH], f32)
        w_cv = sb("w_cv", [P, 3 * P], f32)
        b_cv = sb("b_cv", [P, 3 * CH], f32)
        low_cv = sb("low_cv", [P, 3], f32)
        pcol = sb("pcol", [P, 1], i32)
        bit = sb("bit", [P, SIGNS], i32)
        sgn = sb("sgn", [P, SIGNS], f32)
        flip = sb("flip", [P, SIGNS], f32)
        qi = sb("qi", [P, NBLK], i32)
        q = qi[:, :].bitcast(f32)
        subh = sb("subh", [P, CH], f32)
        headb = sb("headb", [P, P], f32)
        prevk = sb("prevk", [P, 1], f32)
        prevh = sb("prevh", [P, 1], i32)
        r1 = sb("r1", [P, NBLK], f32)
        i1 = sb("i1", [P, NBLK], i32)
        i2 = sb("i2", [P, NBLK], i32)
        cle = sb("cle", [P, NBLK + 1], f32)
        cnt = sb("cnt", [P, 2 * NBLK], f32)
        some = sb("some", [P, 2 * NBLK], f32)
        endr = sb("endr", [P, 2 * NBLK], i32)
        e0 = sb("e0", [P, NBLK], i32)
        e1 = sb("e1", [P, NBLK], i32)
        e2 = sb("e2", [P, NBLK], i32)
        e3 = sb("e3", [P, NBLK], i32)
        dinv = sb("dinv", [P, NBLK], f32)
        e_deg = sb("e_deg", [P, NBLK], f32)
        mu = sb("mu", [P, NBLK], f32)
        sd = sb("sd", [P, NBLK], f32)

        ps = ctx.enter_context(nc.psum_tensor("ps", [P, 8, 512], f32))
        psf = ps[:, :, :].rearrange("p b n -> p (b n)")

        cleared, made, setup_done = sem("cleared"), sem("constants_made"), sem("setup_done")
        ld_x, ld_e, ld_w, ld_cw = sem("x_loaded"), sem("edges_loaded"), sem("weights_loaded"), sem("conv_weights_loaded")
        e_copied = sem("edges_copied")
        staged, t_turned, t_evac, t_proj, t_copied, t_stored = (sem(n) for n in (
            "nodes_staged", "nodes_turned", "turned_copied", "projected", "projection_copied", "tables_stored"))
        turn_in, turned, odd_copied = sem("keys_to_turn"), sem("keys_turned"), sem("odd_banks_copied")
        heads_ready, masks_ready = sem("heads_ready"), sem("masks_ready")
        keys_out, back_in, masks_out = sem("keys_stored"), sem("heads_loaded"), sem("masks_stored")
        rows1_chosen, rows2_chosen, counts_ready, shifted = (sem(n) for n in (
            "sub_head_rows_chosen", "key_rows_chosen", "counts_ready", "counts_shifted"))
        g_sub, g_key, order_done = sem("sub_heads_gathered"), sem("key_rows_gathered"), sem("order_done")
        gath = [[sem(f"message_rows_gathered_{k}_{h}") for h in range(2)] for k in range(2)]
        gath_cv = [[sem(f"feature_rows_gathered_{k}_{h}") for h in range(2)] for k in range(2)]
        staged_idx = sem("indices_staged")
        t_ready, relu_done, m_ready, scan_done, o_ready, out_copied, out_free = (sem(n) for n in (
            "messages_summed", "relu_done", "columns_ready", "scanned", "rows_turned", "rows_copied", "rows_stored"))
        msk_in = [sem("mask_loaded_0"), sem("mask_loaded_1")]
        outd = [sem("rows_out_0"), sem("rows_out_1")]
        h_staged = sem("conv_nodes_staged")
        g_end, h_ready, h_out = sem("ends_gathered"), sem("features_ready"), sem("features_stored")
        var_ready, deg_ready, rooted = sem("variance_ready"), sem("degree_ready"), sem("rooted")
        shifted_down, exped, sum_ready, logged, out_ready = (sem(n) for n in (
            "logits_shifted", "exponentiated", "sum_ready", "logarithm_done", "output_ready"))
        stored = sem("output_stored")
        passed = {e.engine: sem(f"passed_{n}") for n, e in (("sp", nc.sync), ("pool", nc.gpsimd), ("pe", nc.tensor))}

        plan = [("both", L, 1 << d) for L in range(1, LOGW) for d in range(L - 1, -1, -1)]
        plan.append(("flip", LOGW, 0))
        plan += [("up", LOGW, 1 << d) for d in range(LOGW - 1, -1, -1)]
        for L in range(LOGW + 1, LOGW + 8):
            plan += [("flip", L, 0), ("turn", L, 0)]
            plan += [("up", L, 1 << d) for d in range(L - LOGW - 1, -1, -1)]
            plan.append(("turn", L, 0))
            plan += [("up", L, 1 << d) for d in range(LOGW - 1, -1, -1)]
        turn_from = [n % 2 for n, e in enumerate(plan) if e[0] == "turn"]
        KEY_BUF = len(plan) % 2
        NTURN = len(turn_from) + 1
        STEPS = PAIRS // PPI

        by_tile = keyb[1 - KEY_BUF].rearrange("p (q f) -> p q f", q=P)
        def hold(eng, *waits):
            for signal, value in waits:
                eng.wait_ge(signal, value)
            eng.sem_inc(passed[eng.engine], 1)

        block = ctx.enter_context(nc.Block())

        @block.sync
        def _(sp):
            sp.wait_ge(cleared, 1)
            for row, e in enumerate((dst, src, dst, src)):
                sp.dma_start(d_edge[row:row + 1, :], e[None, :]).then_inc(e_copied, 16)
            sp.dma_start(X[:, 0:(NBLK - 1) * CH].rearrange("p (c d) -> p c d", d=CH),
                         x[0:(NBLK - 1) * P, :].rearrange("(c p) d -> p c d", p=P)).then_inc(ld_x, 16)
            sp.dma_start(X[0:LAST, (NBLK - 1) * CH:NC], x[(NBLK - 1) * P:, :]).then_inc(ld_x, 16)
            for h in range(2):
                sp.dma_start(w_ab[h * CH:(h + 1) * CH, h * P:(h + 1) * P], w1[0:CH, :]).then_inc(ld_w, 16)
                sp.dma_start(w1b[h * CH:(h + 1) * CH, :], w1[CH:2 * CH, :]).then_inc(ld_w, 16)
                sp.dma_start(b1r[0:1, h * P:(h + 1) * P], b1[None, :]).then_inc(ld_w, 16)
            sp.dma_start(w2s[:], w2).then_inc(ld_w, 16)
            sp.dma_start(b2b[:], b2.partition_broadcast(P)).then_inc(ld_w, 16)
            for k, (w, b) in enumerate(((cw1, cb1), (cw1, cb1), (cw2, cb2))):
                for h in range(2):
                    sp.dma_start(w_cv[h * CH:(h + 1) * CH, k * P + h * CH:k * P + (h + 1) * CH], w).then_inc(ld_cw, 16)
                sp.dma_start(b_cv[:, k * CH:(k + 1) * CH], b.partition_broadcast(P)).then_inc(ld_cw, 16)

            def load_edges(r):
                for n in range(2):
                    row = d_edge[bass.ds(r + n, 1), :] if not isinstance(r, int) else d_edge[r + n:r + n + 1, :]
                    sp.dma_start(EX[:, n * NE:(n + 1) * NE],
                                 row.rearrange("o (p w) -> (o p) w", p=P).bitcast(f32)).then_inc(ld_e, 16)

            sp.wait_ge(e_copied, 64)
            load_edges(0)
            A_v = d_a.rearrange("(k c p) d -> k p c d", p=P, c=2 * PPI)
            B_v = d_b.rearrange("(k c p) d -> k p c d", p=P, c=2 * PPI)
            nA = 2 * PPI * HID
            with sp.Fori(0, STEPS, 1) as k:
                for n, table in enumerate((A_v, B_v)):
                    sp.wait_ge(t_copied, k * 2 + (n + 1))
                    sp.dma_start(table[bass.ds(k, 1)].rearrange("o p c d -> (o p) c d"),
                                 HP[:, n * nA:(n + 1) * nA].rearrange("p (c d) -> p c d", d=HID)).then_inc(t_stored, 16)
            with sp.Fori(0, 2, 1) as r:
                sp.wait_ge(heads_ready, r + 1)
                sp.dma_start(d_keys.rearrange("(p a) b -> p (a b)", p=P), keyb[KEY_BUF]).then_inc(keys_out, 16)
                sp.dma_start(d_sub, subh[:]).then_inc(keys_out, 16)
                sp.dma_start(d_head, subh[:, 0:1]).then_inc(keys_out, 16)
                sp.dma_start(d_last, keyb[KEY_BUF][:, W - 1:W]).then_inc(keys_out, 16)
                sp.wait_ge(keys_out, r * 64 + 64)
                sp.dma_start(prevk[1:P, :], d_last[0:P - 1, :]).then_inc(back_in, 16)
                sp.dma_start(headb[:], d_head.rearrange("p o -> (p o)").partition_broadcast(P)).then_inc(back_in, 16)
                sp.wait_ge(masks_ready, r + 1)
                for rows, t in ((d_keep, keep), (d_pen, pen)):
                    sp.dma_start(rows[bass.ds(r, 1), :].rearrange("o (p w) -> (o p) w", p=P), t[:]).then_inc(masks_out, 16)
                sp.wait_ge(masks_out, r * 32 + 32)
                sp.wait_ge(order_done, r + 1)
                load_edges(r + 1)

            def pass_io(mask_row, chunks_before):
                def load(c, k):
                    cols = mask_row[bass.ds(c * (TILES * P), TILES * P)]
                    sp.dma_start(msk[k], cols.partition_broadcast(CH)).then_inc(msk_in[k], 16)
                load(0, 0)
                load(1, 1)
                rows = d_rows.rearrange("(c p k) d -> c p (k d)", p=P, k=TILES)
                with sp.Fori(0, NCH // 2, 1) as i:
                    for k in range(2):
                        c = i * 2 + k
                        g = (chunks_before + c) * GROUPS
                        sp.wait_ge(scan_done, g + (CREDIT + GROUPS))
                        load(c + 2, k)
                        if k == 1:
                            sp.wait_ge(outd[0], (chunks_before + c + 1) * 8)
                            sp.sem_inc(out_free, 1)
                        sp.wait_ge(out_copied, g + (CREDIT + GROUPS))
                        sp.dma_start(rows[bass.ds(c, 1)].rearrange("o p n -> (o p) n"), outr[:, k, :]).then_inc(outd[k], 16)
                    sp.wait_ge(outd[1], (i * 2 + (chunks_before + 2)) * 8)
                    sp.sem_inc(out_free, 1)
                landed = (chunks_before + NCH) * 8 + (chunks_before + NCH) // NCH * 16
                if isinstance(landed, int):
                    sp.wait_ge(msk_in[0], landed)
                    sp.wait_ge(msk_in[1], landed)
                else:
                    hold(sp, (msk_in[0], landed), (msk_in[1], landed))

            sp.sem_inc(out_free, CREDIT)
            sp.wait_ge(ld_e, 96)
            pass_io(d_pen[1, :], 0)
            with sp.Fori(0, 3, 1) as r:
                sp.wait_ge(h_ready, r + 1)
                sp.dma_start(d_h.rearrange("(c p) d -> p c d", p=P),
                             HP[:, :].rearrange("p (c d) -> p c d", d=CH)).then_inc(h_out, 16)
                pass_io(d_keep[0, :], (r + 1) * NCH)
            sp.wait_ge(stored, 32)

        @block.gpsimd
        def _(pool):
            pool.wait_ge(cleared, 1)
            nc.gpsimd.iota(pcol[:], [[0, 1]], base=0, channel_multiplier=1).then_inc(made, 1)
            nc.gpsimd.iota(qi[:], [[P, NBLK]], base=0, channel_multiplier=1).then_inc(made, 1)
            for t, base, step in ((ident, 0, -1), (shift, 1, -1)):
                nc.gpsimd.affine_select(out=t[:], in_=t[:], compare_op=ALU.not_equal, fill=1.0, base=base,
                                        pattern=[[step, P]], channel_multiplier=1).then_inc(made, 1)
            nc.gpsimd.affine_select(out=wrap[:], in_=wrap[:], compare_op=ALU.not_equal, fill=1.0, base=-(P - 1),
                                    pattern=[[P, P]], channel_multiplier=1).then_inc(made, 1)

            def gather(dst, table, index, signal):
                nc.gpsimd.indirect_dma_start(dst, None, table, bass.IndirectOffsetOnAxis(ap=index, axis=0)).then_inc(signal, 16)

            pool.wait_ge(t_stored, 32 * STEPS)
            with pool.Fori(0, 2, 1) as r:
                hold(pool, (rows1_chosen, r + 1), (keys_out, r * 64 + 64))
                for c in range(NBLK):
                    gather(HP[:, c * CH:(c + 1) * CH], d_sub, i1[:, c:c + 1], g_sub)
                hold(pool, (rows2_chosen, r + 1))
                for c in range(NBLK):
                    gather(HP[:, c * CH:(c + 1) * CH], d_keys, i2[:, c:c + 1], g_key)

            def pass_gather(chunks_before, lots, width, per):
                with pool.Fori(0, NCH // 2, 1) as i:
                    for k in range(2):
                        c = i * 2 + k
                        used = t_ready if lots == 2 else m_ready
                        pool.wait_ge(used, (chunks_before + c) * GROUPS + (CREDIT - GROUPS))
                        for n in range(lots):
                            lst = (idx_lo[:, bass.ds(c * TILES + NT, TILES)], idx_hi[:, bass.ds(c * TILES, TILES)])[n] \
                                if lots == 2 else idx_lo[:, bass.ds(c * TILES, TILES)]
                            nc.gpsimd.tensor_copy(stg[:, k, n * TILES:(n + 1) * TILES], lst).then_inc(staged_idx, 1)
                        hold(pool, (staged_idx, c * lots + (lots if lots == 2 else per)))
                        for t in range(TILES):
                            for n in range(lots):
                                at = (k * lots + n) * TILES * width + t * width
                                gather(arena[:, at:at + width], ((d_b, d_a)[n] if lots == 2 else d_h),
                                       stg[:, k, n * TILES + t:n * TILES + t + 1],
                                       (gath if lots == 2 else gath_cv)[k][t // HALF])

            def ends(order, passes):
                stored_rows = passes * NCH + CREDIT
                if isinstance(stored_rows, int):
                    pool.wait_ge(out_free, stored_rows)
                else:
                    hold(pool, (out_free, stored_rows))
                for c in range(NBLK):
                    gather(EX[:, c * CH:(c + 1) * CH], d_rows, endr[:, order * NBLK + c:order * NBLK + c + 1], g_end)

            pool.wait_ge(order_done, 2)
            pass_gather(0, 2, HID, 0)
            ends(1, 1)
            with pool.Fori(0, 3, 1) as r:
                hold(pool, (h_out, r * 16 + 16))
                pass_gather((r + 1) * NCH, 1, CH, r * NCH + (2 * NCH + 1))
                ends(0, r + 2)

        @block.scalar
        def _(act):
            act.wait_ge(ld_x, 32)
            nA = 2 * PPI * HID
            with act.Fori(0, STEPS, 1) as k:
                nc.scalar.copy(stage[:], X[:, bass.ds(k * (PPI * P), PPI * P)]).then_inc(staged, 1)
                act.wait_ge(t_turned, k + 1)
                nc.scalar.copy(stageT[:], psf[:, 0:PPI * P]).then_inc(t_evac, 1)
                for h in range(2):
                    act.wait_ge(t_proj, k * 2 + (h + 1))
                    nc.scalar.copy(HP[:, h * nA:(h + 1) * nA], psf[:, h * 2048:h * 2048 + nA]).then_inc(t_copied, 1)
                act.wait_ge(t_stored, k * 32 + 32)
            with act.Fori(0, 2, 1) as r:
                for n in range(NTURN):
                    for b in range(1, 8, 2):
                        act.wait_ge(turned, r * (8 * NTURN) + (8 * n + b + 1))
                        if n < NTURN - 1:
                            dst_cols = keyb[1 - turn_from[n]][:, b * 512:(b + 1) * 512]
                            nc.scalar.copy(dst_cols, ps[:, b, :]).then_inc(odd_copied, 1)
                        else:
                            dst_cols = by_tile[:, :, 4 * b:4 * b + 4]
                            nc.scalar.copy(dst_cols, ps[:, b, :].rearrange("p (j q) -> p q j", j=4)).then_inc(odd_copied, 1)

            def copy_rows(c, k, g, before):
                G = (before + c) * GROUPS + g
                act.wait_ge(o_ready, G + (CREDIT + 1))
                if g == 0:
                    act.wait_ge(out_free, before + c + (CREDIT - 1))
                nc.scalar.copy(outr[:, k, g * 4 * CH:(g + 1) * 4 * CH], ps[:, 4 + g % 2, 0:4 * CH]).then_inc(out_copied, 1)

            act.sem_inc(relu_done, CREDIT)
            act.sem_inc(out_copied, CREDIT)
            with act.Fori(0, NCH // 2, 1) as i:
                for k in range(2):
                    c = i * 2 + k
                    for g in range(GROUPS + 2):
                        if g < GROUPS:
                            G = c * GROUPS + g
                            act.wait_ge(t_ready, G + (CREDIT + 1))
                            act.wait_ge(m_ready, G + (CREDIT - 1))
                            nc.scalar.activation(R[:, g % 2, :], ps[:, g % 2, :], ACT.Relu).then_inc(relu_done, 1)
                        if g >= 2:
                            copy_rows(c, k, g - 2, 0)
            act.wait_ge(var_ready, 1)
            nc.scalar.activation(sd[:], mu[:], ACT.Sqrt).then_inc(rooted, 1)
            act.wait_ge(deg_ready, 1)
            nc.scalar.activation(dinv[:], e_deg[:], ACT.Sqrt).then_inc(rooted, 1)
            with act.Fori(0, 3, 1) as r:
                with act.Fori(0, STEPS, 1) as k:
                    act.wait_ge(t_turned, r * STEPS + k + (STEPS + 1))
                    nc.scalar.copy(stageT[:], psf[:, 0:PPI * P]).then_inc(t_evac, 1)
                with act.Fori(0, NCH // 2, 1) as i:
                    for k in range(2):
                        for g in range(GROUPS):
                            copy_rows(i * 2 + k, k, g, (r + 1) * NCH)
            act.wait_ge(shifted_down, 1)
            nc.scalar.activation(TMP, EX[:], ACT.Exp).then_inc(exped, 1)
            act.wait_ge(sum_ready, 1)
            nc.scalar.activation(mu[:], sd[:], ACT.Ln).then_inc(logged, 1)
            act.wait_ge(var_ready, 2)
            nc.scalar.activation(sd[:], mu[:], ACT.Sqrt).then_inc(rooted, 1)
            act.wait_ge(out_ready, 1)
            act.dma_start(out[0:(NBLK - 1) * P, :].rearrange("(c p) d -> p c d", p=P),
                          X[:, 0:(NBLK - 1) * CH].rearrange("p (c d) -> p c d", d=CH)).then_inc(stored, 16)
            act.dma_start(out[(NBLK - 1) * P:, :], X[0:LAST, (NBLK - 1) * CH:NC]).then_inc(stored, 16)
            act.wait_ge(stored, 32)

        @block.tensor
        def _(pe):
            pe.wait_ge(made, 5)
            pe.wait_ge(setup_done, 1)
            nA = 2 * PPI * HID
            with pe.Fori(0, STEPS, 1) as k:
                pe.wait_ge(staged, k + 1)
                for j in range(PPI):
                    last = nc.tensor.transpose(psf[:, j * P:(j + 1) * P], stage[:, j * P:(j + 1) * P], ident[:])
                last.then_inc(t_turned, 1)
                pe.wait_ge(t_evac, k + 1)
                for h in range(2):
                    for j in range(PPI):
                        o = psf[:, h * 2048 + j * 2 * P:h * 2048 + (j + 1) * 2 * P]
                        nc.tensor.matmul(o, ones1[:], b1r[:, h * 2 * P:(h + 1) * 2 * P], start=True, stop=False)
                        last = nc.tensor.matmul(o, stageT[:, j * P:(j + 1) * P], w_ab[:, h * 2 * P:(h + 1) * 2 * P],
                                                start=False, stop=True)
                    last.then_inc(t_proj, 1)
            pe.wait_ge(t_copied, 2 * STEPS)
            with pe.Fori(0, 2, 1) as r:
                for n in range(NTURN):
                    pe.wait_ge(turn_in, r * NTURN + (n + 1))
                    from_buf = keyb[turn_from[n] if n < NTURN - 1 else KEY_BUF]
                    for b in range(8):
                        for j in range(4):
                            f = 4 * b + j
                            last = nc.tensor.transpose(ps[:, b, j * P:(j + 1) * P], from_buf[:, f * P:(f + 1) * P], ident[:])
                        last.then_inc(turned, 1)
                pe.wait_ge(counts_ready, r + 1)
                nc.tensor.matmul(ps[:, 0, 0:NBLK], shift[:], cle[:, 1:NBLK + 1], start=True, stop=False)
                nc.tensor.matmul(ps[:, 0, 0:NBLK], wrap[:], cle[:, 0:NBLK], start=False, stop=True).then_inc(shifted, 1)

            pe.wait_ge(order_done, 2)
            pe.sem_inc(t_ready, CREDIT)
            pe.sem_inc(m_ready, CREDIT)
            pe.sem_inc(o_ready, CREDIT)

            def sum_messages(c, k, g):
                G = c * GROUPS + g
                pe.wait_ge(relu_done, G + (CREDIT - 1))
                for t in range(4):
                    o = ps[:, g % 2, t * P:(t + 1) * P]
                    for n in range(2):
                        a = (k * 2 + n) * TILES * HID + (4 * g + t) * HID
                        last = nc.tensor.matmul(o, arena[:, a:a + HID], ident[:], start=n == 0, stop=n == 1)
                last.then_inc(t_ready, 1)

            def rows_back(c, g, before):
                G = (before + c) * GROUPS + g
                hold(pe, (scan_done, G + (CREDIT + 1)), (out_copied, G + (CREDIT - 1)))
                for t in range(4):
                    last = nc.tensor.transpose(ps[:, 4 + g % 2, t * CH:(t + 1) * CH], S[:, g % 2, t * P:(t + 1) * P],
                                               ident[0:CH, 0:CH])
                last.then_inc(o_ready, 1)

            with pe.Fori(0, NCH // 2, 1) as i:
                for k in range(2):
                    c = i * 2 + k
                    for g in range(GROUPS + 2):
                        if g in (0, GROUPS // 2):
                            pe.wait_ge(gath[k][g * 2 // GROUPS], i * (32 * HALF) + 32 * HALF)
                        if g < GROUPS:
                            sum_messages(c, k, g)
                        if 0 <= g - 1 < GROUPS:
                            G = c * GROUPS + g - 1
                            pe.wait_ge(relu_done, G + (CREDIT + 1))
                            pe.wait_ge(scan_done, G + (CREDIT - 1))
                            nc.tensor.matmul(ps[0:CH, 2 + (g - 1) % 2, :], w2s[:], R[:, (g - 1) % 2, :],
                                             start=True, stop=True).then_inc(m_ready, 1)
                        if g >= 2:
                            rows_back(c, g - 2, 0)

            pe.wait_ge(ld_cw, 144)
            with pe.Fori(0, 3, 1) as r:
                with pe.Fori(0, STEPS, 1) as k:
                    pe.wait_ge(h_staged, r * STEPS + k + 1)
                    for j in range(PPI):
                        last = nc.tensor.transpose(psf[:, j * P:(j + 1) * P], stage[:, j * P:(j + 1) * P], ident[:])
                    last.then_inc(t_turned, 1)
                    pe.wait_ge(t_evac, r * STEPS + k + (STEPS + 1))
                    for j in range(PPI):
                        last = nc.tensor.matmul(psf[:, 1024 + j * P:1024 + (j + 1) * P], stageT[:, j * P:(j + 1) * P],
                                                w_cv[:, bass.ds(r * P, P)], start=True, stop=True)
                    last.then_inc(t_proj, 1)
                with pe.Fori(0, NCH // 2, 1) as i:
                    for k in range(2):
                        c = i * 2 + k
                        for g in range(GROUPS + 1):
                            if g in (0, GROUPS // 2):
                                pe.wait_ge(gath_cv[k][g * 2 // GROUPS], (r * (NCH // 2) + i) * (16 * HALF) + 16 * HALF)
                            if g < GROUPS:
                                G = ((r + 1) * NCH + c) * GROUPS + g
                                hold(pe, (scan_done, G + (CREDIT - 1)))
                                for t in range(4):
                                    a = k * TILES * CH + (4 * g + t) * CH
                                    last = nc.tensor.transpose(ps[0:CH, 2 + g % 2, t * P:(t + 1) * P],
                                                               arena[:, a:a + CH], ident[:])
                                last.then_inc(m_ready, 1)
                            if g >= 1:
                                rows_back(c, g - 1, (r + 1) * NCH)

        @block.vector
        def _(dve):
            def bc_in(t, n=CH):
                return t[:, :, None].to_broadcast([P, NBLK, n])

            def bc_out(t):
                return t[:, None, :].to_broadcast([P, NBLK, CH])

            def nodes(t):
                return t[:, :].rearrange("p (c d) -> p c d", d=CH)

            for t in (X[:, (NBLK - 1) * CH:NC], w_ab[:], w_cv[:], b1r[:], ident[:], shift[:], wrap[:], cle[:],
                      prevk[:], S[:]):
                nc.vector.memset(t, 0.0)
            nc.vector.memset(ones1[:], 1.0).then_inc(cleared, 1)
            nc.vector.memset(low_cv[:], -2.0 * BIG)
            nc.vector.memset(sgn[:], 1.0)
            dve.drain()
            nc.vector.memset(low_cv[:, 1:2], 0.0)
            dve.wait_ge(made, 5)
            nc.vector.tensor_scalar(qi[:], qi[:], NODE_BITS, REAL | LOW, ALU.logical_shift_left, ALU.bitwise_or)
            for j in range(SIGNS - 1):
                nc.vector.tensor_scalar(bit[:, j:j + 1], pcol[:], j, 1, ALU.logical_shift_right, ALU.bitwise_and)
            dve.drain()
            nc.vector.tensor_scalar(sgn[:, 0:SIGNS - 1], bit[:, 0:SIGNS - 1], -2.0, 1.0, ALU.mult, ALU.add)
            dve.drain()
            nc.vector.tensor_copy(flip[:, 0:1], sgn[:, 0:1])
            nc.vector.tensor_tensor(flip[:, 1:SIGNS], sgn[:, 0:SIGNS - 1], sgn[:, 1:SIGNS], ALU.mult)
            dve.wait_ge(ld_w, 128)
            for h in range(2):
                hs = slice(h * CH, (h + 1) * CH)
                nc.vector.tensor_copy(w_ab[hs, (2 + h) * P:(3 + h) * P], w1b[hs, :])
                last = nc.vector.tensor_tensor(w_ab[hs, h * P:(h + 1) * P], w_ab[hs, h * P:(h + 1) * P], w1b[hs, :],
                                               ALU.subtract)
            last.then_inc(setup_done, 1)

            def network_step(kind, L, d, a, b):
                if kind == "flip":
                    return nc.vector.tensor_scalar(b, a, flip[:, L - LOGW:L - LOGW + 1], None, ALU.mult)
                if kind == "up":
                    av, bv = (t.rearrange("p (m h d) -> p m h d", h=2, d=d) for t in (a, b))
                    nc.vector.tensor_tensor(bv[:, :, 0, :], av[:, :, 0, :], av[:, :, 1, :], ALU.min)
                    return nc.vector.tensor_tensor(bv[:, :, 1, :], av[:, :, 0, :], av[:, :, 1, :], ALU.max)
                av, bv = (t.rearrange("p (n r m h d) -> p n r m h d", r=2, h=2, d=d, m=(1 << L) // (2 * d)) for t in (a, b))
                for way in range(2):
                    lo, hi = av[:, :, way, :, 0, :], av[:, :, way, :, 1, :]
                    nc.vector.tensor_tensor(bv[:, :, way, :, way, :], lo, hi, ALU.min)
                    last = nc.vector.tensor_tensor(bv[:, :, way, :, 1 - way, :], lo, hi, ALU.max)
                return last

            with dve.Fori(0, 2, 1) as r:
                key = keyb[0].bitcast(i32)
                e_hi, e_lo = (EX[:, n * NE:(n + 1) * NE].bitcast(i32) for n in range(2))
                nc.vector.memset(key[:, NE:], PAD)
                dve.wait_ge(ld_e, r * 32 + 32)
                nc.vector.tensor_scalar(key[:, 0:NE], e_hi, NODE_BITS, REAL, ALU.logical_shift_left, ALU.bitwise_or)
                dve.drain()
                nc.vector.tensor_tensor(key[:, 0:NE], key[:, 0:NE], e_lo, ALU.bitwise_or)
                dve.drain()
                turn = 0
                for n, (kind, L, d) in enumerate(plan):
                    if kind == "turn":
                        for b in range(0, 8, 2):
                            dve.wait_ge(turned, r * (8 * NTURN) + (8 * turn + b + 1))
                            nc.vector.tensor_copy(keyb[(n + 1) % 2][:, b * 512:(b + 1) * 512], ps[:, b, :])
                        turn += 1
                        dve.drain()
                        dve.wait_ge(odd_copied, r * (4 * NTURN) + 4 * turn)
                        continue
                    else:
                        last = network_step(kind, L, d, keyb[n % 2], keyb[(n + 1) % 2])
                        if n + 1 < len(plan) and plan[n + 1][0] == "turn":
                            last.then_inc(turn_in, 1)
                    dve.drain()

                ks, kf = keyb[KEY_BUF], keyb[1 - KEY_BUF].bitcast(i32)
                nc.vector.tensor_copy(subh[:], ks.rearrange("p (a b) -> p a b", b=CH)[:, :, 0]).then_inc(heads_ready, 1)
                nc.vector.tensor_scalar(kf, ks.bitcast(i32), NODE_BITS, None, ALU.logical_shift_right)
                dve.wait_ge(back_in, r * 32 + 32)
                nc.vector.tensor_scalar(prevh[:], prevk[:].bitcast(i32), NODE_BITS, None, ALU.logical_shift_right)
                dve.drain()
                nc.vector.tensor_tensor(keep[:, 1:W], kf[:, 1:W], kf[:, 0:W - 1], ALU.is_equal)
                nc.vector.tensor_tensor(keep[:, 0:1], kf[:, 0:1], prevh[:], ALU.is_equal).then_inc(turn_in, 1)
                dve.drain()
                nc.vector.tensor_scalar(pen[:], keep[:], 2 * BIG, -BIG, ALU.mult, ALU.add).then_inc(masks_ready, 1)
                for b in range(0, 8, 2):
                    dve.wait_ge(turned, r * (8 * NTURN) + (8 * (NTURN - 1) + b + 1))
                    nc.vector.tensor_copy(by_tile[:, :, 4 * b:4 * b + 4], ps[:, b, :].rearrange("p (j q) -> p q j", j=4))
                dve.drain()
                dve.wait_ge(odd_copied, r * (4 * NTURN) + 4 * NTURN)
                nc.vector.tensor_scalar(idx_lo[:, bass.ds(r * NT, NT)], kf[:, 0:NT], LOW, None, ALU.bitwise_and)
                nc.vector.tensor_scalar(idx_hi[:], kf[:, 0:NT], NODE_BITS, LOW, ALU.logical_shift_right, ALU.bitwise_and)

                less = EX[:, :].bitcast(bf16)
                less1 = less.rearrange("p (c d) -> p c d", d=P)
                less2 = less[:, 0:NC].rearrange("p (c d) -> p c d", d=CH)
                nc.vector.tensor_tensor(less1, headb[:, None, :].to_broadcast([P, NBLK, P]), bc_in(q, P), ALU.is_le)
                dve.drain()
                nc.vector.tensor_reduce(r1[:], less1, AX.X, ALU.add)
                dve.drain()
                nc.vector.tensor_scalar(r1[:], r1[:], -1.0, 0.0, ALU.add, ALU.max)
                dve.drain()
                nc.vector.tensor_copy(i1[:], r1[:]).then_inc(rows1_chosen, 1)
                dve.wait_ge(g_sub, r * (16 * NBLK) + 16 * NBLK)
                nc.vector.tensor_tensor(less2, nodes(HP), bc_in(q), ALU.is_le)
                dve.drain()
                nc.vector.tensor_reduce(sd[:], less2, AX.X, ALU.add)
                dve.drain()
                nc.vector.tensor_scalar(sd[:], sd[:], -1.0, 0.0, ALU.add, ALU.max)
                dve.drain()
                nc.vector.scalar_tensor_tensor(r1[:], r1[:], float(CH), sd[:], ALU.mult, ALU.add)
                dve.drain()
                nc.vector.tensor_copy(i2[:], r1[:]).then_inc(rows2_chosen, 1)
                dve.wait_ge(g_key, r * (16 * NBLK) + 16 * NBLK)
                nc.vector.tensor_tensor(less2, nodes(HP), bc_in(q), ALU.is_le)
                dve.drain()
                nc.vector.tensor_reduce(sd[:], less2, AX.X, ALU.add)
                dve.drain()
                nc.vector.scalar_tensor_tensor(cle[:, 1:], r1[:], float(CH), sd[:], ALU.mult, ALU.add).then_inc(counts_ready, 1)
                dve.drain()
                nc.vector.tensor_scalar(mu[:], cle[:, 1:], -1.0, 0.0, ALU.add, ALU.max)
                dve.drain()
                nc.vector.tensor_copy(e0[:], mu[:])
                dve.drain()
                nc.vector.tensor_scalar(e1[:], e0[:], (SORTED - 1) // (TILES * P) * (TILES * P), None, ALU.bitwise_and)
                nc.vector.tensor_scalar(e2[:], e0[:], P - 1, 4, ALU.bitwise_and, ALU.logical_shift_left)
                nc.vector.tensor_scalar(e3[:], e0[:], 7, TILES - 1, ALU.logical_shift_right, ALU.bitwise_and)
                dve.drain()
                nc.vector.tensor_tensor(e1[:], e1[:], e2[:], ALU.bitwise_or)
                dve.drain()
                nc.vector.tensor_tensor(endr[:, bass.ds(r * NBLK, NBLK)], e1[:], e3[:], ALU.bitwise_or)
                dve.wait_ge(shifted, r + 1)
                nc.vector.tensor_tensor(mu[:], cle[:, 1:], ps[:, 0, 0:NBLK], ALU.subtract)
                dve.drain()
                nc.vector.tensor_copy(cnt[:, bass.ds(r * NBLK, NBLK)], mu[:])
                nc.vector.tensor_scalar(some[:, bass.ds(r * NBLK, NBLK)], mu[:], 0.0, None, ALU.is_gt).then_inc(order_done, 1)
                dve.drain()

            def scans(before, op0, op1):
                with dve.Fori(0, NCH // 2, 1) as i:
                    for k in range(2):
                        dve.wait_ge(msk_in[k], (i * 2 + before + 2) * 8 + before // NCH * 16)
                        for g in range(GROUPS):
                            G = (i * 2 + before + k) * GROUPS + g
                            dve.wait_ge(m_ready, G + (CREDIT + 1))
                            dve.wait_ge(o_ready, G + (CREDIT - 1))
                            dve.wait_ge(scan_done, G + CREDIT)
                            nc.vector.tensor_tensor_scan(S[:, g % 2, :], msk[k][:, g * 512:(g + 1) * 512],
                                                         ps[0:CH, 2 + g % 2, :], S[:, 1 - g % 2, 511:512],
                                                         op0, op1).then_inc(scan_done, 1)

            def layer_norm(t, n):
                tv = nodes(t)
                nc.vector.tensor_reduce(mu[:], tv, AX.X, ALU.add)
                dve.drain()
                nc.vector.tensor_scalar(mu[:], mu[:], 1.0 / CH, None, ALU.mult)
                dve.drain()
                nc.vector.tensor_tensor(tv, tv, bc_in(mu), ALU.subtract)
                dve.drain()
                nc.vector.tensor_tensor(TMP, t[:, :], t[:, :], ALU.mult)
                dve.drain()
                nc.vector.tensor_reduce(sd[:], nodes(TMP), AX.X, ALU.add)
                dve.drain()
                nc.vector.tensor_scalar(mu[:], sd[:], 1.0 / CH, EPS, ALU.mult, ALU.add).then_inc(var_ready, 1)
                dve.wait_ge(rooted, n)
                nc.vector.reciprocal(mu[:], sd[:])
                dve.drain()
                return nc.vector.tensor_tensor(tv, tv, bc_in(mu), ALU.mult)

            dve.sem_inc(scan_done, CREDIT)
            scans(0, ALU.min, ALU.max)
            dve.wait_ge(g_end, 16 * NBLK)
            nc.vector.tensor_tensor(nodes(EX), nodes(EX), bc_out(b2b), ALU.add)
            dve.drain()
            nc.vector.tensor_tensor(TMP, EX[:], EX[:], ALU.subtract)
            nc.vector.memset(HP[:], 0.0)
            dve.drain()
            nc.vector.tensor_scalar(TMP, TMP, 0.0, None, ALU.is_equal)
            dve.drain()
            nc.vector.tensor_tensor(nodes(TMP), nodes(TMP), bc_in(some[:, NBLK:2 * NBLK]), ALU.mult)
            dve.drain()
            nc.vector.copy_predicated(HP[:], TMP.bitcast(i32), EX[:])
            dve.drain()
            nc.vector.tensor_tensor(X[:], X[:], HP[:], ALU.add)
            dve.drain()
            layer_norm(X, 1)
            nc.vector.tensor_scalar(e_deg[:], cnt[:, 0:NBLK], 1.0, 1e-12, ALU.add, ALU.max).then_inc(deg_ready, 1)
            dve.wait_ge(rooted, 2)
            nc.vector.reciprocal(dinv[:], dinv[:])
            dve.drain()
            nc.vector.tensor_copy(EX[:], X[:])
            dve.drain()
            n2 = 2 * PPI
            with dve.Fori(0, 3, 1) as r:
                with dve.Fori(0, STEPS, 1) as k:
                    nc.vector.tensor_copy(stage[:], EX[:, bass.ds(k * (PPI * P), PPI * P)]).then_inc(h_staged, 1)
                    dve.wait_ge(t_proj, r * STEPS + k + (2 * STEPS + 1))
                    nc.vector.tensor_tensor(HP[:, bass.ds(k * (PPI * P), PPI * P)].rearrange("p (c d) -> p c d", d=CH),
                                            psf[:, 1024:1024 + PPI * P].rearrange("p (c d) -> p c d", d=CH),
                                            dinv[:, bass.ds(k * n2, n2)][:, :, None].to_broadcast([P, n2, CH]),
                                            ALU.mult)
                    dve.drain()
                dve.drain().then_inc(h_ready, 1)
                scans((r + 1) * NCH, ALU.mult, ALU.add)
                dve.wait_ge(g_end, r * (16 * NBLK) + 32 * NBLK)
                nc.vector.tensor_tensor(nodes(EX), nodes(EX), bc_in(some[:, 0:NBLK]), ALU.mult)
                dve.drain()
                nc.vector.tensor_tensor(EX[:], EX[:], HP[:], ALU.add)
                dve.drain()
                nc.vector.tensor_tensor(nodes(EX), nodes(EX), bc_in(dinv), ALU.mult)
                dve.drain()
                nc.vector.tensor_tensor(nodes(EX), nodes(EX),
                                        b_cv[:, bass.ds(r * CH, CH)][:, None, :].to_broadcast([P, NBLK, CH]), ALU.add)
                dve.drain()
                nc.vector.tensor_scalar(EX[:], EX[:], low_cv[:, bass.ds(r, 1)], None, ALU.max)
                dve.drain()
            nc.vector.tensor_reduce(mu[:], nodes(EX), AX.X, ALU.max)
            dve.drain()
            nc.vector.tensor_tensor(nodes(EX), nodes(EX), bc_in(mu), ALU.subtract).then_inc(shifted_down, 1)
            dve.wait_ge(exped, 1)
            nc.vector.tensor_reduce(sd[:], nodes(TMP), AX.X, ALU.add).then_inc(sum_ready, 1)
            dve.wait_ge(logged, 1)
            nc.vector.tensor_tensor(nodes(EX), nodes(EX), bc_in(mu), ALU.subtract)
            dve.drain()
            nc.vector.tensor_tensor(X[:], X[:], EX[:], ALU.add)
            dve.drain()
            layer_norm(X, 3).then_inc(out_ready, 1)


_INS = ['x', 'src', 'dst', 'L0_gnn_W1', 'L0_gnn_b1', 'L0_gnn_W2', 'L0_gnn_b2',
        'L1_gnn_W1', 'L1_gnn_b1', 'L1_gnn_W2', 'L1_gnn_b2']
_OUTS = [((N_NODES, CH), 'float32')]


def kernel(**inputs):
    import numpy as _np
    import concourse.bacc as _bacc
    from concourse import mybir as _mybir
    from concourse.bass_utils import run_bass_kernel_spmd as _run

    nc = _bacc.Bacc("TRN2", target_bir_lowering=False, num_devices=1)
    arrays, args = {}, []
    for name in _INS:
        a = _np.ascontiguousarray(inputs[name])
        arrays[f"in_{name}_dram"] = a
        args.append(nc.dram_tensor(f"in_{name}_dram", a.shape, _mybir.dt.from_np(a.dtype), kind="ExternalInput").ap())
    for i, (shape, dtype) in enumerate(_OUTS):
        dt = _mybir.dt.from_np(_np.dtype(dtype))
        args.append(nc.dram_tensor(f"out_{i}_dram", shape, dt, kind="ExternalOutput").ap())
    gnn(nc, *args)
    r = _run(nc, [arrays], core_ids=[0])
    return r.results[0]["out_0_dram"]
```

```python
import concourse.bass as bass
from concourse import mybir
from contextlib import ExitStack

P = 128
N_NODES, CH, HID = 12500, 64, 128
N_EDGES = 400000
NBLK = -(-N_NODES // P)
LAST = N_NODES - (NBLK - 1) * P
NC = NBLK * CH
LOGW = 12
W = 1 << LOGW
SORTED = P * W
NODE_BITS = 14
LOW = (1 << NODE_BITS) - 1
REAL = 0x20000000
PAD = 0x30000000
TILES = 16
NCH = -(-N_EDGES // (P * TILES))
NCH += NCH % 2
NT = NCH * TILES
HALF = TILES // 2
GROUPS = TILES // 4
CREDIT = 8
BIG = 1.5e38
PAD_VALUE = 2.0 ** -31
EPS = 1e-5
DB = 256
NDB = NBLK * P // DB
BUCKETS = NBLK * NDB
BCOLS = -(-BUCKETS // P)
MOST = P
MOST_SAME = 16
SB = 7
SRC_GROUP = 14
PARTS = [9, 9] + [8] * 10
SPLIT = 2048.0
PAIRS = NBLK // 2
PPI = 7
SIGNS = 8
WINDOW_END = NBLK * P - P


def gnn(nc, x, src, dst, w1, b1, w2, b2, cw1, cb1, cw2, cb2, out):
    f32, bf16, i32, f16 = mybir.dt.float32, mybir.dt.bfloat16, mybir.dt.int32, mybir.dt.float16
    ALU, ACT, AX = mybir.AluOpType, mybir.ActivationFunctionType, mybir.AxisListType

    ctx = ExitStack()
    with ctx:
        def sb(name, shape, dt):
            return ctx.enter_context(nc.sbuf_tensor(name, shape, dt))

        def sem(name):
            return ctx.enter_context(nc.semaphore(name))

        def dram(name, shape, dt):
            return nc.dram_tensor(name, shape, dt, kind="Internal").ap()

        d_a = dram("table_a", (NBLK * P, HID), f32)
        d_b = dram("table_b", (NBLK * P, HID), f32)
        d_h = dram("table_h", (NBLK * P, CH), f32)
        d_keys = dram("sorted_keys", (SORTED // CH, CH), f32)
        d_sub = dram("sub_heads", (P, CH), f32)
        d_head = dram("heads", (P, 1), f32)
        d_last = dram("last_keys", (P, 1), f32)
        d_keep = dram("keep", (1, SORTED), bf16)
        d_local = dram("local_sources", (1, SORTED), bf16)
        d_first = dram("window_firsts", (P, 2), i32)
        d_pen = dram("penalty", (1, SORTED), bf16)
        d_rows = dram("scan_rows", (NT * P, CH), f32)

        d_count = dram("edge_counts", (NDB, P, NBLK * DB // 2), bf16)

        X = sb("X", [P, NC], f32)
        NE = N_EDGES // P
        EX = sb("EX", [P, NC], f32)
        HP = sb("HP", [P, NC], f32)
        arena = sb("arena", [P, 2 * W], f32)
        keyb = [arena[:, 0:W], arena[:, W:2 * W]]
        TMP = arena[:, 0:NC]
        U = sb("U", [P, 15872], f32)
        idx_lo = U[:, 0:NT].bitcast(i32)
        idx_hi = U[:, NT:2 * NT].bitcast(i32)
        loc = [U[:, NT + k * TILES * P // 2:NT + (k + 1) * TILES * P // 2].bitcast(bf16) for k in range(2)]
        one_a = [U[:, NT + TILES * P + k * 512:NT + TILES * P + (k + 1) * 512] for k in range(2)]
        at = 2 * NT
        msk_all = U[:, at:at + TILES * P].bitcast(bf16)
        msk = [msk_all[0:CH, k * TILES * P:(k + 1) * TILES * P] for k in range(2)]
        at += TILES * P
        keep = U[:, at:at + W // 2].bitcast(bf16)
        pen = U[:, at + W // 2:at + W].bitcast(bf16)
        local = U[:, at + W:at + W + W // 2].bitcast(bf16)
        vS = U[:, at:at + BCOLS * P // 2].bitcast(bf16)
        at += BCOLS * P // 2
        vD = U[:, at:at + BCOLS * P // 2].bitcast(bf16)
        at += BCOLS * P // 2
        one_s = U[:, at:at + 7 * P].bitcast(bf16).rearrange("p (j u n) -> p j u n", j=7, u=2)
        at += 7 * P
        one_d = U[:, at:at + 7 * DB].bitcast(bf16).rearrange("p (j u n) -> p j u n", j=7, u=2)
        assert at + 7 * DB <= 15872
        CT = max(PARTS) * SB * DB // 4
        ct = [U[:, k * CT:(k + 1) * CT].bitcast(mybir.dt.float8e4) for k in range(3)]
        ct_load = [U[:, k * CT:(k + 1) * CT].bitcast(bf16) for k in range(3)]
        ctile = arena[:, 0:7 * SRC_GROUP * DB // 4].bitcast(mybir.dt.float8e4).rearrange("p (g n) -> p g n", g=7)
        ctile_out = arena[:, 0:7 * SRC_GROUP * DB // 4].bitcast(bf16).rearrange("p (g n) -> p g n", g=7)
        rows_b = HP[:, 0:2 * TILES * HID].rearrange("p (k t d) -> p k t d", k=2, t=TILES)
        window = [HP[:, (2 * TILES + k) * HID:(2 * TILES + k + 1) * HID] for k in range(2)]
        parts = arena[:, 0:NC].bitcast(f16).rearrange("p (c n) -> p c n", n=P)
        room = sb("room", [P, 2 * TILES * CH], f32)
        outr = room[:, :].rearrange("p (k n) -> p k n", k=2)
        stage = room[:, 0:PPI * P]
        stageT = room[:, PPI * P:2 * PPI * P]
        sums = room[:, 0:2 * PPI * P]
        R = sb("R", [P, 2, 512], f32)
        S = sb("S", [CH, 2, 512], f32)
        stg = sb("stg", [P, 2, 2 * TILES], i32)
        ident = sb("ident", [P, P], f32)
        shift = sb("shift", [P, P], f32)
        wrap = sb("wrap", [P, P], f32)
        w_ab = sb("w_ab", [P, 4 * P], f32)
        w1b = sb("w1b", [P, HID], f32)
        w2s = sb("w2s", [HID, CH], f32)
        b1r = sb("b1r", [1, 4 * P], f32)
        ones1 = sb("ones1", [1, P], f32)
        b2b = sb("b2b", [P, CH], f32)
        w_cv = sb("w_cv", [P, 3 * P], f32)
        b_cv = sb("b_cv", [P, 3 * CH], f32)
        low_cv = sb("low_cv", [P, 3], f32)
        pcol = sb("pcol", [P, 1], i32)
        pcolf = sb("pcolf", [P, 1], f32)
        bit = sb("bit", [P, SIGNS], i32)
        sgn = sb("sgn", [P, SIGNS], f32)
        flip = sb("flip", [P, SIGNS], f32)
        qi = sb("qi", [P, NBLK], i32)
        q = qi[:, :].bitcast(f32)
        subh = sb("subh", [P, CH], f32)
        headb = sb("headb", [P, P], f32)
        prevk = sb("prevk", [P, 1], f32)
        prevh = sb("prevh", [P, 1], i32)
        r1 = sb("r1", [P, NBLK], f32)
        i1 = sb("i1", [P, NBLK], i32)
        i2 = sb("i2", [P, NBLK], i32)
        cle = sb("cle", [P, NBLK + 1], f32)
        cnt = sb("cnt", [P, NBLK], f32)
        some = sb("some", [P, NBLK], f32)
        endr = sb("endr", [P, NBLK], i32)
        e0 = sb("e0", [P, NBLK], i32)
        e1 = sb("e1", [P, NBLK], i32)
        e2 = sb("e2", [P, NBLK], i32)
        e3 = sb("e3", [P, NBLK], i32)
        dinv = sb("dinv", [P, NBLK], f32)
        deg = sb("deg", [P, NBLK], f32)
        e_deg = sb("e_deg", [P, NBLK], f32)
        qbi = sb("qbi", [P, BCOLS], i32)
        qb = qbi[:, :].bitcast(f32)
        bit_on = sb("bit_on", [P, 7, BCOLS], i32)
        iota_i = sb("iota_i", [P, DB], i32)
        iota_r = sb("iota_r", [P, DB], bf16)
        ones_b = sb("ones_b", [P, 1], bf16)
        ones_c = sb("ones_c", [P, 1], f32)
        zrow = sb("zrow", [1, P], bf16)
        orow = sb("orow", [1, 512], bf16)
        join = sb("join", [P, CH], f32)
        fl = sb("fl", [P, 4], f32)
        win = sb("win", [P, 2], i32)
        win_top = sb("win_top", [P, 2], i32)
        firsts = iota_i[0:1, :]
        flag = sb("flag", [1, 1], i32)
        top = sb("top", [P, 1], f32)
        row1 = sb("row1", [1, P], f32)
        one1 = sb("one1", [1, 1], f32)
        expo = sb("expo", [P, 1], i32)
        scale = sb("scale", [P, 1], f32)
        unscale = sb("unscale", [P, 1], f32)
        mu = sb("mu", [P, NBLK], f32)
        sd = sb("sd", [P, NBLK], f32)

        ps = ctx.enter_context(nc.psum_tensor("ps", [P, 8, 512], f32))
        psf = ps[:, :, :].rearrange("p b n -> p (b n)")

        cleared, made, setup_done = sem("cleared"), sem("constants_made"), sem("setup_done")
        ld_x, ld_e, ld_w, ld_cw = sem("x_loaded"), sem("edges_loaded"), sem("weights_loaded"), sem("conv_weights_loaded")
        e_copied = sem("edges_copied")
        staged, t_turned, t_evac, t_proj, t_copied, t_stored = (sem(n) for n in (
            "nodes_staged", "nodes_turned", "turned_copied", "projected", "projection_copied", "tables_stored"))
        turn_in, turned, odd_copied = sem("keys_to_turn"), sem("keys_turned"), sem("odd_banks_copied")
        heads_ready, masks_ready = sem("heads_ready"), sem("masks_ready")
        keys_out, back_in, masks_out = sem("keys_stored"), sem("heads_loaded"), sem("masks_stored")
        rows1_chosen, rows2_chosen, counts_ready, shifted = (sem(n) for n in (
            "sub_head_rows_chosen", "key_rows_chosen", "counts_ready", "counts_shifted"))
        g_sub, g_key, order_done = sem("sub_heads_gathered"), sem("key_rows_gathered"), sem("order_done")
        gath = [[sem(f"message_rows_gathered_{k}_{h}") for h in range(2)] for k in range(2)]
        gath_cv = [[sem(f"feature_rows_gathered_{k}_{h}") for h in range(2)] for k in range(2)]
        staged_idx = sem("indices_staged")
        t_ready, relu_done, m_ready, scan_done, o_ready, out_copied, out_free = (sem(n) for n in (
            "messages_summed", "relu_done", "columns_ready", "scanned", "rows_turned", "rows_copied", "rows_stored"))
        msk_in = [sem("mask_loaded_0"), sem("mask_loaded_1")]
        outd = [sem("rows_out_0"), sem("rows_out_1")]
        h_staged = sem("conv_nodes_staged")
        g_end, h_ready, h_out = sem("ends_gathered"), sem("features_ready"), sem("features_stored")
        var_ready, deg_ready, rooted = sem("variance_ready"), sem("degree_ready"), sem("rooted")
        shifted_down, exped, sum_ready, logged, out_ready = (sem(n) for n in (
            "logits_shifted", "exponentiated", "sum_ready", "logarithm_done", "output_ready"))
        stored = sem("output_stored")
        ex_free, edges_wanted = sem("ex_free"), sem("edges_wanted")
        firsts_in, one_a_ready = sem("window_firsts_loaded"), sem("one_hot_sources_ready")
        win_in = [sem("window_loaded_0"), sem("window_loaded_1")]
        flag_in, flag_ready = sem("overflows_found"), sem("path_chosen")
        starts_ready, g_pairs, b_shifted, b_turned, b_copied, b_ready = (sem(n) for n in (
            "bucket_rows_chosen", "bucket_rows_gathered", "buckets_aligned", "buckets_turned", "buckets_copied", "bucket_columns_ready"))
        cols_made = sem("bucket_numbers_made")
        hot_ready, count_ready, count_copied, count_free = (sem(n) for n in (
            "one_hots_ready", "counts_summed", "counts_copied", "counts_stored"))
        c_out = [sem(f"counts_out_{g}") for g in range(7)]
        deg_summed, degrees_done = sem("degrees_summed"), sem("degrees_done")
        top_ready, top_row, top_one, top_all = (sem(n) for n in (
            "partition_maxima", "maxima_turned", "maximum_found", "maximum_spread"))
        parts_ready, acc_ready, acc_copied, joined, sb_done = (sem(n) for n in (
            "parts_ready", "block_summed", "block_sums_copied", "block_joined", "block_done"))
        ct_in = [sem(f"counts_in_{k}") for k in range(3)]
        ct_used = sem("counts_used")
        passed = {e.engine: sem(f"passed_{n}") for n, e in (("sp", nc.sync), ("pool", nc.gpsimd), ("pe", nc.tensor), ("act", nc.scalar))}

        plan = [("both", L, 1 << d) for L in range(1, LOGW) for d in range(L - 1, -1, -1)]
        plan.append(("flip", LOGW, 0))
        plan += [("up", LOGW, 1 << d) for d in range(LOGW - 1, -1, -1)]
        for L in range(LOGW + 1, LOGW + 8):
            plan += [("flip", L, 0), ("turn", L, 0)]
            plan += [("up", L, 1 << d) for d in range(L - LOGW - 1, -1, -1)]
            plan.append(("turn", L, 0))
            plan += [("up", L, 1 << d) for d in range(LOGW - 1, -1, -1)]
        turn_from = [n % 2 for n, e in enumerate(plan) if e[0] == "turn"]
        KEY_BUF = len(plan) % 2
        NTURN = len(turn_from)
        TURNS = [0, NTURN + 1, 2 * NTURN + 1]
        QCOLS = [NBLK, BCOLS, NBLK]
        QUERIED = [0, NBLK, NBLK + BCOLS]
        STEPS = PAIRS // PPI
        FUSED = NCH // NDB
        PHASES = GROUPS + 2
        BPAIRS = NBLK // 2

        def share(c, g):
            f = c * PHASES + g
            return range(f * BPAIRS // (FUSED * PHASES), (f + 1) * BPAIRS // (FUSED * PHASES))

        by_tile = keyb[1 - KEY_BUF].rearrange("p (q f) -> p q f", q=P)
        def hold(eng, *waits):
            for signal, value in waits:
                eng.wait_ge(signal, value)
            eng.sem_inc(passed[eng.engine], 1)

        block = ctx.enter_context(nc.Block())

        @block.sync
        def _(sp):
            sp.wait_ge(cleared, 1)
            sp.dma_start(X[:, 0:(NBLK - 1) * CH].rearrange("p (c d) -> p c d", d=CH),
                         x[0:(NBLK - 1) * P, :].rearrange("(c p) d -> p c d", p=P)).then_inc(ld_x, 16)
            sp.dma_start(X[0:LAST, (NBLK - 1) * CH:NC], x[(NBLK - 1) * P:, :]).then_inc(ld_x, 16)
            for h in range(2):
                sp.dma_start(w_ab[h * CH:(h + 1) * CH, h * P:(h + 1) * P], w1[0:CH, :]).then_inc(ld_w, 16)
                sp.dma_start(w1b[h * CH:(h + 1) * CH, :], w1[CH:2 * CH, :]).then_inc(ld_w, 16)
                sp.dma_start(b1r[0:1, h * P:(h + 1) * P], b1[None, :]).then_inc(ld_w, 16)
            sp.dma_start(w2s[:], w2).then_inc(ld_w, 16)
            sp.dma_start(b2b[:], b2.partition_broadcast(P)).then_inc(ld_w, 16)
            for k, (w, b) in enumerate(((cw1, cb1), (cw1, cb1), (cw2, cb2))):
                for h in range(2):
                    sp.dma_start(w_cv[h * CH:(h + 1) * CH, k * P + h * CH:k * P + (h + 1) * CH], w).then_inc(ld_cw, 16)
                sp.dma_start(b_cv[:, k * CH:(k + 1) * CH], b.partition_broadcast(P)).then_inc(ld_cw, 16)

            def load_edges():
                for n, e in enumerate((src, dst)):
                    sp.dma_start(EX[:, n * NE:(n + 1) * NE], e.rearrange("(p w) -> p w", p=P).bitcast(f32)).then_inc(ld_e, 16)

            load_edges()
            A_v = d_a.rearrange("(k c p) d -> k p c d", p=P, c=2 * PPI)
            B_v = d_b.rearrange("(k c p) d -> k p c d", p=P, c=2 * PPI)
            nA = 2 * PPI * HID
            with sp.Fori(0, STEPS, 1) as k:
                for n, table in enumerate((A_v, B_v)):
                    sp.wait_ge(t_copied, k * 2 + (n + 1))
                    sp.dma_start(table[bass.ds(k, 1)].rearrange("o p c d -> (o p) c d"),
                                 HP[:, n * nA:(n + 1) * nA].rearrange("p (c d) -> p c d", d=HID)).then_inc(t_stored, 16)
            def sort_io(k):
                sp.wait_ge(heads_ready, k + 1)
                sp.dma_start(d_keys.rearrange("(p a) b -> p (a b)", p=P), keyb[KEY_BUF]).then_inc(keys_out, 16)
                sp.dma_start(d_sub, subh[:]).then_inc(keys_out, 16)
                sp.dma_start(d_head, subh[:, 0:1]).then_inc(keys_out, 16)
                sp.dma_start(d_last, keyb[KEY_BUF][:, W - 1:W]).then_inc(keys_out, 16)
                sp.wait_ge(keys_out, k * 64 + 64)
                sp.dma_start(headb[:], d_head.rearrange("p o -> (p o)").partition_broadcast(P)).then_inc(back_in, 16)
                if k == 1:
                    later = d_keys.rearrange("a b -> (a b)")[MOST_SAME:MOST_SAME + (P - 1) * W]
                    sp.dma_start(keyb[1 - KEY_BUF][0:P - 1, :], later.rearrange("(p w) -> p w", w=W)).then_inc(back_in, 16)
                else:
                    sp.dma_start(prevk[1:P, :], d_last[0:P - 1, :]).then_inc(back_in, 16)
                    sp.wait_ge(masks_ready, k // 2 + 1)
                    rows, t = (d_pen, pen) if k == 0 else (d_keep, keep)
                    sp.dma_start(rows.rearrange("o (p w) -> (o p) w", p=P), t).then_inc(masks_out, 16)
                    if k == 0:
                        sp.dma_start(d_local.rearrange("o (p w) -> (o p) w", p=P), local).then_inc(masks_out, 16)
                        sp.dma_start(d_first, win[:]).then_inc(masks_out, 16)
                    sp.wait_ge(masks_out, 48 + k // 2 * 16)
                    if k == 0:
                        sp.dma_start(firsts, d_first.rearrange("(o p) k -> o (p k)", o=1)).then_inc(firsts_in, 16)

            sort_io(0)
            sp.wait_ge(edges_wanted, 1)
            load_edges()
            sort_io(1)
            def pass_io(mask_row, chunks_before):
                def load(c, k):
                    cols = mask_row[bass.ds(c * (TILES * P), TILES * P)]
                    sp.dma_start(msk[k], cols.partition_broadcast(CH)).then_inc(msk_in[k], 16)
                load(0, 0)
                load(1, 1)
                rows = d_rows.rearrange("(c p k) d -> c p (k d)", p=P, k=TILES)
                with sp.Fori(0, NCH // 2, 1) as i:
                    for k in range(2):
                        c = i * 2 + k
                        g = (chunks_before + c) * GROUPS
                        sp.wait_ge(scan_done, g + (CREDIT + GROUPS))
                        load(c + 2, k)
                        if k == 1:
                            sp.wait_ge(outd[0], (chunks_before + c + 1) * 8)
                            sp.sem_inc(out_free, 1)
                        sp.wait_ge(out_copied, g + (CREDIT + GROUPS))
                        sp.dma_start(rows[bass.ds(c, 1)].rearrange("o p n -> (o p) n"), outr[:, k, :]).then_inc(outd[k], 16)
                    sp.wait_ge(outd[1], (i * 2 + (chunks_before + 2)) * 8)
                    sp.sem_inc(out_free, 1)
                landed = (chunks_before + NCH) * 8 + (chunks_before + NCH) // NCH * 16
                if isinstance(landed, int):
                    sp.wait_ge(msk_in[0], landed)
                    sp.wait_ge(msk_in[1], landed)
                else:
                    hold(sp, (msk_in[0], landed), (msk_in[1], landed))

            sp.sem_inc(out_free, CREDIT)
            sp.sem_inc(count_free, CREDIT)
            sp.wait_ge(firsts_in, 16)
            sp.wait_ge(flag_ready, 1)
            sp.wait_ge(order_done, 2)
            general = sp.value_load(flag[0:1, 0:1])
            with sp.If(general > 0):
                pass_io(d_pen[0, :], 0)
            with sp.Else():
                rows = d_rows.rearrange("(c p k) d -> c p (k d)", p=P, k=TILES)

                def load(c, k):
                    edges = bass.ds(c * (TILES * P), TILES * P)
                    first = sp.value_load(firsts[:, bass.ds(c, 1)], min_val=0, max_val=WINDOW_END)
                    sp.dma_start(msk[k], d_pen[0, edges].partition_broadcast(CH)).then_inc(msk_in[k], 16)
                    sp.dma_start(loc[k], d_local[0, edges].partition_broadcast(P)).then_inc(win_in[k], 16)
                    sp.dma_start(window[k], d_a[bass.ds(first, P), :]).then_inc(win_in[k], 16)

                load(0, 0)
                load(1, 1)
                with sp.Fori(0, NDB, 1) as d:
                    stored_lots = 0
                    for n in range(FUSED):
                        c, k = d * FUSED + n, n % 2
                        g = c * GROUPS
                        sp.wait_ge(t_ready, g + (CREDIT + GROUPS))
                        sp.wait_ge(scan_done, g + (CREDIT + GROUPS))
                        load(c + 2, k)
                        if n:
                            sp.wait_ge(outd[1 - k], d * (FUSED * 8) + (n + 1) // 2 * 16)
                            sp.sem_inc(out_free, 1)
                        hold(sp, (out_copied, g + (CREDIT + GROUPS)))
                        sp.dma_start(rows[bass.ds(c, 1)].rearrange("o p n -> (o p) n"), outr[:, k, :]).then_inc(outd[k], 16)
                        for lot in range(stored_lots, share(n, PHASES - 1).stop // 7):
                            hold(sp, (count_copied, d * BPAIRS + (lot * 7 + 7 + CREDIT)))
                            half = SRC_GROUP * DB // 2
                            sp.dma_start(d_count[bass.ds(d, 1), :, lot * half:(lot + 1) * half].rearrange("o p n -> (o p) n"),
                                         ctile_out[:, lot, :]).then_inc(c_out[lot], 16)
                            if lot:
                                sp.wait_ge(c_out[lot - 1], d * 16 + 16)
                                sp.sem_inc(count_free, 1)
                            stored_lots = lot + 1
                    sp.wait_ge(outd[1], d * (FUSED * 8) + FUSED * 8)
                    sp.sem_inc(out_free, 1)
                    sp.wait_ge(c_out[6], d * 16 + 16)
                    sp.sem_inc(count_free, 1)
                for k in range(2):
                    sp.wait_ge(msk_in[k], NCH * 8 + 16)
                    sp.wait_ge(win_in[k], NCH * 16 + 32)
            with sp.If(general > 0):
                sp.wait_ge(ex_free, 1)
                load_edges()
                sort_io(2)
                with sp.Fori(0, 3, 1) as r:
                    sp.wait_ge(h_ready, r + 1)
                    sp.dma_start(d_h.rearrange("(c p) d -> p c d", p=P),
                                 HP[:, :].rearrange("p (c d) -> p c d", d=CH)).then_inc(h_out, 16)
                    pass_io(d_keep[0, :], (r + 1) * NCH)
            with sp.Else():
                sp.wait_ge(degrees_done, 1)
                NP = len(PARTS)
                with sp.Fori(0, 3, 1) as r, sp.Fori(0, NDB // SB, 1) as nb:
                    n = r * SB + nb
                    for a, width in enumerate(PARTS):
                        s0 = sum(PARTS[:a])
                        sp.wait_ge(ct_used, n * NP + (a - 2 + CREDIT))
                        row = d_count[bass.ds(nb * SB, SB), :, s0 * DB // 2:(s0 + width) * DB // 2]
                        sp.dma_start(ct_load[a % 3][:, 0:SB * width * DB // 2].rearrange("p (d n) -> p d n", d=SB),
                                     row.rearrange("d p n -> p d n")).then_inc(ct_in[a % 3], 16)
            sp.wait_ge(stored, 32)

        @block.gpsimd
        def _(pool):
            pool.wait_ge(cleared, 1)
            nc.gpsimd.iota(pcol[:], [[0, 1]], base=0, channel_multiplier=1).then_inc(made, 1)
            nc.gpsimd.iota(qi[:], [[P, NBLK]], base=0, channel_multiplier=1).then_inc(made, 1)
            nc.gpsimd.iota(qbi[:], [[P, BCOLS]], base=0, channel_multiplier=1).then_inc(made, 1)
            nc.gpsimd.iota(iota_i[:], [[1, DB]], base=0, channel_multiplier=0).then_inc(made, 1)
            for t, base, step in ((ident, 0, -1), (shift, 1, -1)):
                nc.gpsimd.affine_select(out=t[:], in_=t[:], compare_op=ALU.not_equal, fill=1.0, base=base,
                                        pattern=[[step, P]], channel_multiplier=1).then_inc(made, 1)
            nc.gpsimd.affine_select(out=wrap[:], in_=wrap[:], compare_op=ALU.not_equal, fill=1.0, base=-(P - 1),
                                    pattern=[[P, P]], channel_multiplier=1).then_inc(made, 1)
            for half, fill in ((0, 1.0), (1, 1.0 / SPLIT)):
                pool.wait_ge(made, 7 + half)
                nc.gpsimd.affine_select(out=join[:], in_=join[:], compare_op=ALU.not_equal, fill=fill, base=-half * CH,
                                        pattern=[[-1, CH]], channel_multiplier=1).then_inc(made, 1)

            def gather(dst, table, index, signal):
                nc.gpsimd.indirect_dma_start(dst, None, table, bass.IndirectOffsetOnAxis(ap=index, axis=0)).then_inc(signal, 16)

            def search_rows(k):
                pool.wait_ge(rows1_chosen, k + 1)
                pool.wait_ge(keys_out, k * 64 + 64)
                for c in range(QCOLS[k]):
                    gather(HP[:, c * CH:(c + 1) * CH], d_sub, i1[:, c:c + 1], g_sub)
                pool.wait_ge(rows2_chosen, k + 1)
                for c in range(QCOLS[k]):
                    gather(HP[:, c * CH:(c + 1) * CH], d_keys, i2[:, c:c + 1], g_key)

            pool.wait_ge(t_stored, 32 * STEPS)
            search_rows(0)
            search_rows(1)
            key_rows = d_keys.rearrange("(a t) b -> a (t b)", t=2)
            for h in range(2):
                pool.wait_ge(starts_ready, h + 1)
                for c in range(BCOLS // 2):
                    for n, index in enumerate((i1, i2)):
                        o = c * 2 * P + n * P
                        gather(EX[:, o:o + P], key_rows, index[:, h * BCOLS // 2 + c:h * BCOLS // 2 + c + 1], g_pairs)
            pool.wait_ge(cols_made, 1)
            nc.gpsimd.iota(EX[:, 0:BCOLS * P].bitcast(i32), [[1, BCOLS * P]], base=REAL >> 15,
                           channel_multiplier=0).then_inc(cols_made, 1)

            def pass_gather(chunks_before, lots, width, per):
                with pool.Fori(0, NCH // 2, 1) as i:
                    for k in range(2):
                        c = i * 2 + k
                        used = t_ready if lots == 2 else m_ready
                        pool.wait_ge(used, (chunks_before + c) * GROUPS + (CREDIT - GROUPS))
                        for n in range(lots):
                            lst = (idx_lo[:, bass.ds(c * TILES, TILES)], idx_hi[:, bass.ds(c * TILES, TILES)])[n] \
                                if lots == 2 else idx_lo[:, bass.ds(c * TILES, TILES)]
                            nc.gpsimd.tensor_copy(stg[:, k, n * TILES:(n + 1) * TILES], lst).then_inc(staged_idx, 1)
                        hold(pool, (staged_idx, c * lots + (lots if lots == 2 else per)))
                        for t in range(TILES):
                            for n in range(lots):
                                at = (k * lots + n) * TILES * width + t * width
                                gather(arena[:, at:at + width], ((d_b, d_a)[n] if lots == 2 else d_h),
                                       stg[:, k, n * TILES + t:n * TILES + t + 1],
                                       (gath if lots == 2 else gath_cv)[k][t // HALF])

            def ends(passes):
                stored_rows = passes * NCH + CREDIT
                if isinstance(stored_rows, int):
                    pool.wait_ge(out_free, stored_rows)
                else:
                    hold(pool, (out_free, stored_rows))
                for c in range(NBLK):
                    gather(EX[:, c * CH:(c + 1) * CH], d_rows, endr[:, c:c + 1], g_end)

            pool.wait_ge(order_done, 2)
            pool.wait_ge(flag_ready, 1)
            general = pool.value_load(flag[0:1, 0:1])
            with pool.If(general > 0):
                pass_gather(0, 2, HID, 0)
            with pool.Else():
                with pool.Fori(0, NDB, 1) as d:
                    for n in range(FUSED):
                        c, k = d * FUSED + n, n % 2
                        pool.wait_ge(t_ready, c * GROUPS + (CREDIT - GROUPS))
                        nc.gpsimd.tensor_copy(stg[:, k, 0:TILES], idx_lo[:, bass.ds(c * TILES, TILES)]).then_inc(staged_idx, 1)
                        hold(pool, (staged_idx, c + 1))
                        for t in range(TILES):
                            gather(rows_b[:, k, t, :], d_b, stg[:, k, t:t + 1], gath[k][t // HALF])
            ends(1)
            with pool.If(general > 0):
                search_rows(2)
                pool.wait_ge(order_done, 3)
                with pool.Fori(0, 3, 1) as r:
                    hold(pool, (h_out, r * 16 + 16))
                    pass_gather((r + 1) * NCH, 1, CH, r * NCH + (2 * NCH + 1))
                    ends(r + 2)
            with pool.Else():
                pool.wait_ge(flag_ready, 1)

        @block.scalar
        def _(act):
            act.wait_ge(ld_x, 32)
            nA = 2 * PPI * HID
            with act.Fori(0, STEPS, 1) as k:
                nc.scalar.copy(stage[:], X[:, bass.ds(k * (PPI * P), PPI * P)]).then_inc(staged, 1)
                act.wait_ge(t_turned, k + 1)
                nc.scalar.copy(stageT[:], psf[:, 0:PPI * P]).then_inc(t_evac, 1)
                for h in range(2):
                    act.wait_ge(t_proj, k * 2 + (h + 1))
                    nc.scalar.copy(HP[:, h * nA:(h + 1) * nA], psf[:, h * 2048:h * 2048 + nA]).then_inc(t_copied, 1)
                act.wait_ge(t_stored, k * 32 + 32)
            def odd_banks(k):
                for n in range(NTURN + (k != 1)):
                    for b in range(1, 8, 2):
                        act.wait_ge(turned, 8 * (TURNS[k] + n) + b + 1)
                        if n < NTURN:
                            dst_cols = keyb[1 - turn_from[n]][:, b * 512:(b + 1) * 512]
                            nc.scalar.copy(dst_cols, ps[:, b, :]).then_inc(odd_copied, 1)
                        else:
                            dst_cols = by_tile[:, :, 4 * b:4 * b + 4]
                            nc.scalar.copy(dst_cols, ps[:, b, :].rearrange("p (j q) -> p q j", j=4)).then_inc(odd_copied, 1)

            odd_banks(0)
            odd_banks(1)
            for h in range(2):
                act.wait_ge(b_turned, h + 1)
                half = BCOLS // 2 * P
                nc.scalar.copy(arena[:, h * half:(h + 1) * half], psf[:, 0:half]).then_inc(b_copied, 1)
            def copy_rows(c, k, g, before, bank):
                G = (before + c) * GROUPS + g
                act.wait_ge(o_ready, G + (CREDIT + 1))
                if g == 0:
                    act.wait_ge(out_free, before + c + (CREDIT - 1))
                nc.scalar.copy(outr[:, k, g * 4 * CH:(g + 1) * 4 * CH], ps[:, bank, 0:4 * CH]).then_inc(out_copied, 1)

            act.sem_inc(relu_done, CREDIT)
            act.sem_inc(out_copied, CREDIT)
            act.sem_inc(count_copied, CREDIT)

            def relu(c, g):
                G = c * GROUPS + g
                act.wait_ge(t_ready, G + (CREDIT + 1))
                act.wait_ge(m_ready, G + (CREDIT - 1))
                nc.scalar.activation(R[:, g % 2, :], ps[:, g % 2, :], ACT.Relu).then_inc(relu_done, 1)

            act.wait_ge(b_ready, 1)
            act.wait_ge(flag_ready, 1)
            general = act.value_load(flag[0:1, 0:1])
            with act.If(general > 0):
                with act.Fori(0, NCH // 2, 1) as i:
                    for k in range(2):
                        for g in range(PHASES):
                            if g < GROUPS:
                                relu(i * 2 + k, g)
                            if g >= 2:
                                copy_rows(i * 2 + k, k, g - 2, 0, 4 + g % 2)
            with act.Else():
                with act.Fori(0, NDB, 1) as d:
                    for n in range(FUSED):
                        c, k = d * FUSED + n, n % 2
                        for g in range(PHASES):
                            if g < GROUPS:
                                relu(c, g)
                            if g >= 2:
                                copy_rows(c, k, g - 2, 0, 4)
                            for m in share(n, g):
                                if m % 7 == 0:
                                    act.wait_ge(count_free, d * 7 + (m // 7 + 1 + CREDIT - 7))
                                hold(act, (count_ready, d * BPAIRS + (m + 1 + CREDIT)))
                                nc.scalar.copy(ctile[:, m // 7, m % 7 * 512:(m % 7 + 1) * 512], ps[:, 5 + m % 2, :],
                                               saturate=False).then_inc(count_copied, 1)
            act.wait_ge(var_ready, 1)
            nc.scalar.activation(sd[:], mu[:], ACT.Sqrt).then_inc(rooted, 1)

            def copy_turned(r):
                with act.Fori(0, STEPS, 1) as k:
                    act.wait_ge(t_turned, r * STEPS + k + (STEPS + 1))
                    nc.scalar.copy(stageT[:], psf[:, 0:PPI * P]).then_inc(t_evac, 1)

            with act.If(general > 0):
                odd_banks(2)
                act.wait_ge(deg_ready, 1)
                nc.scalar.activation(dinv[:], e_deg[:], ACT.Sqrt).then_inc(rooted, 1)
                with act.Fori(0, 3, 1) as r:
                    copy_turned(r)
                    with act.Fori(0, NCH // 2, 1) as i:
                        for k in range(2):
                            for g in range(GROUPS):
                                copy_rows(i * 2 + k, k, g, (r + 1) * NCH, 4 + g % 2)
            with act.Else():
                act.wait_ge(deg_ready, 1)
                nc.scalar.activation(dinv[:], e_deg[:], ACT.Sqrt).then_inc(rooted, 1)
                with act.Fori(0, 3, 1) as r:
                    copy_turned(r)
                    with act.Fori(0, NDB // SB, 1) as n:
                        act.wait_ge(acc_ready, r * SB + n + 1)
                        nc.scalar.copy(sums, psf[:, 0:SB * DB]).then_inc(acc_copied, 1)
            act.wait_ge(shifted_down, 1)
            nc.scalar.activation(TMP, EX[:], ACT.Exp).then_inc(exped, 1)
            act.wait_ge(sum_ready, 1)
            nc.scalar.activation(mu[:], sd[:], ACT.Ln).then_inc(logged, 1)
            act.wait_ge(var_ready, 2)
            nc.scalar.activation(sd[:], mu[:], ACT.Sqrt).then_inc(rooted, 1)
            act.wait_ge(out_ready, 1)
            act.dma_start(out[0:(NBLK - 1) * P, :].rearrange("(c p) d -> p c d", p=P),
                          X[:, 0:(NBLK - 1) * CH].rearrange("p (c d) -> p c d", d=CH)).then_inc(stored, 16)
            act.dma_start(out[(NBLK - 1) * P:, :], X[0:LAST, (NBLK - 1) * CH:NC]).then_inc(stored, 16)
            act.wait_ge(stored, 32)

        @block.tensor
        def _(pe):
            pe.wait_ge(made, 9)
            pe.wait_ge(setup_done, 1)
            nA = 2 * PPI * HID
            with pe.Fori(0, STEPS, 1) as k:
                pe.wait_ge(staged, k + 1)
                for j in range(PPI):
                    last = nc.tensor.transpose(psf[:, j * P:(j + 1) * P], stage[:, j * P:(j + 1) * P], ident[:])
                last.then_inc(t_turned, 1)
                pe.wait_ge(t_evac, k + 1)
                for h in range(2):
                    for j in range(PPI):
                        o = psf[:, h * 2048 + j * 2 * P:h * 2048 + (j + 1) * 2 * P]
                        nc.tensor.matmul(o, ones1[:], b1r[:, h * 2 * P:(h + 1) * 2 * P], start=True, stop=False)
                        last = nc.tensor.matmul(o, stageT[:, j * P:(j + 1) * P], w_ab[:, h * 2 * P:(h + 1) * 2 * P],
                                                start=False, stop=True)
                    last.then_inc(t_proj, 1)
            pe.wait_ge(t_copied, 2 * STEPS)
            def turns(k):
                for n in range(NTURN + (k != 1)):
                    pe.wait_ge(turn_in, TURNS[k] + n + 1)
                    from_buf = keyb[turn_from[n] if n < NTURN else KEY_BUF]
                    for b in range(8):
                        for j in range(4):
                            f = 4 * b + j
                            last = nc.tensor.transpose(ps[:, b, j * P:(j + 1) * P], from_buf[:, f * P:(f + 1) * P], ident[:])
                        last.then_inc(turned, 1)
                pe.wait_ge(counts_ready, k + 1)
                n = QCOLS[k]
                nc.tensor.matmul(ps[:, 0, 0:n], shift[:], cle[:, 1:n + 1], start=True, stop=False)
                nc.tensor.matmul(ps[:, 0, 0:n], wrap[:], cle[:, 0:n], start=False, stop=True).then_inc(shifted, 1)

            turns(0)
            turns(1)
            pe.wait_ge(flag_in, 1)
            nc.tensor.matmul(ps[0:1, 1, 0:1], fl[:, 2:3], ones_c[:], start=True, stop=True).then_inc(flag_in, 1)
            for h in range(2):
                pe.wait_ge(b_shifted, h + 1)
                if h:
                    pe.wait_ge(b_copied, h)
                for c in range(BCOLS // 2):
                    last = nc.tensor.transpose(psf[:, c * P:(c + 1) * P], HP[:, c * 2 * P:c * 2 * P + P], ident[:])
                last.then_inc(b_turned, 1)
            pe.wait_ge(order_done, 2)
            pe.sem_inc(count_ready, CREDIT)
            pe.sem_inc(t_ready, CREDIT)
            pe.sem_inc(m_ready, CREDIT)
            pe.sem_inc(o_ready, CREDIT)

            def second_product(c, g):
                G = c * GROUPS + g
                pe.wait_ge(relu_done, G + (CREDIT + 1))
                pe.wait_ge(scan_done, G + (CREDIT - 1))
                nc.tensor.matmul(ps[0:CH, 2 + g % 2, :], w2s[:], R[:, g % 2, :], start=True, stop=True).then_inc(m_ready, 1)

            def rows_back(c, g, before, bank, banks):
                G = (before + c) * GROUPS + g
                hold(pe, (scan_done, G + (CREDIT + 1)), (out_copied, G + (CREDIT + 1 - banks)))
                for t in range(4):
                    last = nc.tensor.transpose(ps[:, bank, t * CH:(t + 1) * CH], S[:, g % 2, t * P:(t + 1) * P],
                                               ident[0:CH, 0:CH])
                last.then_inc(o_ready, 1)

            pe.wait_ge(flag_ready, 1)
            general = pe.value_load(flag[0:1, 0:1])
            with pe.If(general > 0):
                with pe.Fori(0, NCH // 2, 1) as i:
                    for k in range(2):
                        c = i * 2 + k
                        for g in range(PHASES):
                            if g in (0, GROUPS // 2):
                                pe.wait_ge(gath[k][g * 2 // GROUPS], i * (32 * HALF) + 32 * HALF)
                            if g < GROUPS:
                                pe.wait_ge(relu_done, c * GROUPS + (g + CREDIT - 1))
                                for t in range(4):
                                    o = ps[:, g % 2, t * P:(t + 1) * P]
                                    for n in range(2):
                                        a = (k * 2 + n) * TILES * HID + (4 * g + t) * HID
                                        last = nc.tensor.matmul(o, arena[:, a:a + HID], ident[:], start=n == 0, stop=n == 1)
                                last.then_inc(t_ready, 1)
                            if 0 <= g - 1 < GROUPS:
                                second_product(c, g - 1)
                            if g >= 2:
                                rows_back(c, g - 2, 0, 4 + g % 2, 2)
            with pe.Else():
                nc.tensor.matmul(ps[:, 7, 0:NBLK], zrow[:], orow[:, 0:NBLK], start=True, stop=False)
                with pe.Fori(0, NDB, 1) as d:
                    for n in range(FUSED):
                        c, k = d * FUSED + n, n % 2
                        for g in range(PHASES):
                            if g < GROUPS:
                                G = c * GROUPS + g
                                pe.wait_ge(relu_done, G + (CREDIT - 1))
                                if g == 0:
                                    pe.wait_ge(win_in[k], d * (FUSED * 16) + (n // 2 + 1) * 32)
                                if g in (0, GROUPS // 2):
                                    hold(pe, (gath[k][g * 2 // GROUPS], d * (FUSED * 8 * HALF) + (n // 2 + 1) * 16 * HALF))
                                for t in range(4):
                                    nc.tensor.matmul(ps[:, g % 2, t * P:(t + 1) * P], rows_b[:, k, 4 * g + t, :],
                                                     ident[:], start=t == 0, stop=False, is_transpose=True)
                                hold(pe, (one_a_ready, G + 1))
                                nc.tensor.matmul(ps[:, g % 2, :], window[k], one_a[g % 2],
                                                 start=False, stop=True).then_inc(t_ready, 1)
                            if 0 <= g - 1 < GROUPS:
                                second_product(c, g - 1)
                            if g >= 2:
                                rows_back(c, g - 2, 0, 4, 1)
                            for m in share(n, g):
                                pe.wait_ge(hot_ready, d * BPAIRS + (m + 1))
                                hold(pe, (count_copied, d * BPAIRS + (CREDIT + max(m - 1, 0))))
                                for u in range(2):
                                    for half in range(2):
                                        nc.tensor.matmul(ps[:, 7, bass.ds(d * 2 + half, 1)],
                                                         one_d[:, m % 7, u, half * P:(half + 1) * P],
                                                         ones_b[:], start=False, stop=False)
                                    last = nc.tensor.matmul(ps[:, 5 + m % 2, u * DB:(u + 1) * DB], one_s[:, m % 7, u, :],
                                                            one_d[:, m % 7, u, :], start=True, stop=True)
                                last.then_inc(count_ready, 1)
                nc.tensor.matmul(ps[:, 7, 0:NBLK], zrow[:], orow[:, 0:NBLK], start=False, stop=True).then_inc(deg_summed, 1)

            pe.wait_ge(ld_cw, 144)

            def project(r):
                with pe.Fori(0, STEPS, 1) as k:
                    pe.wait_ge(h_staged, r * STEPS + k + 1)
                    for j in range(PPI):
                        last = nc.tensor.transpose(psf[:, j * P:(j + 1) * P], stage[:, j * P:(j + 1) * P], ident[:])
                    last.then_inc(t_turned, 1)
                    pe.wait_ge(t_evac, r * STEPS + k + (STEPS + 1))
                    for j in range(PPI):
                        last = nc.tensor.matmul(psf[:, 1024 + j * P:1024 + (j + 1) * P], stageT[:, j * P:(j + 1) * P],
                                                w_cv[:, bass.ds(r * P, P)], start=True, stop=True)
                    last.then_inc(t_proj, 1)

            with pe.If(general > 0):
                turns(2)
                pe.wait_ge(order_done, 3)
                with pe.Fori(0, 3, 1) as r:
                    project(r)
                    with pe.Fori(0, NCH // 2, 1) as i:
                        for k in range(2):
                            c = i * 2 + k
                            for g in range(GROUPS + 1):
                                if g in (0, GROUPS // 2):
                                    pe.wait_ge(gath_cv[k][g * 2 // GROUPS], (r * (NCH // 2) + i) * (16 * HALF) + 16 * HALF)
                                if g < GROUPS:
                                    G = ((r + 1) * NCH + c) * GROUPS + g
                                    hold(pe, (scan_done, G + (CREDIT - 1)))
                                    for t in range(4):
                                        a = k * TILES * CH + (4 * g + t) * CH
                                        last = nc.tensor.transpose(ps[0:CH, 2 + g % 2, t * P:(t + 1) * P],
                                                                   arena[:, a:a + CH], ident[:])
                                    last.then_inc(m_ready, 1)
                                if g >= 1:
                                    rows_back(c, g - 1, (r + 1) * NCH, 4 + (g - 1) % 2, 2)
            with pe.Else():
                pe.sem_inc(ct_used, CREDIT)
                BANKS = [(b * 512, min(512, SB * DB - b * 512)) for b in range(-(-SB * DB // 512))]
                with pe.Fori(0, 3, 1) as r:
                    project(r)
                    pe.wait_ge(top_ready, r + 1)
                    nc.tensor.transpose(ps[0:1, 4, 0:P], top[:], ident[:]).then_inc(top_row, 1)
                    pe.wait_ge(top_one, r + 1)
                    nc.tensor.matmul(ps[:, 4, 0:1], ones1[:], one1[:], start=True, stop=True).then_inc(top_all, 1)
                    hold(pe, (parts_ready, r + 1))
                    with pe.Fori(0, NDB // SB, 1) as n:
                        m = r * SB + n
                        for b, (c0, width) in enumerate(BANKS):
                            nc.tensor.matmul(ps[:, b, 0:width], zrow[:], orow[:, 0:width], start=True, stop=False)
                        for a, lot in enumerate(PARTS):
                            hold(pe, (ct_in[a % 3], m * (16 * len(PARTS) // 3) + 16 * (a // 3 + 1)))
                            cv = ct[a % 3][:, 0:SB * lot * DB].rearrange("p (d n) -> p d n", d=SB)
                            for s0 in range(lot):
                                for b, (c0, width) in enumerate(BANKS):
                                    dsts = cv[:, c0 // DB:(c0 + width) // DB, s0 * DB:(s0 + 1) * DB]
                                    last = nc.tensor.matmul(ps[:, b, 0:width].rearrange("p (d n) -> p d n", n=DB),
                                                            parts[:, sum(PARTS[:a]) + s0, :], dsts, start=False, stop=False)
                            last.then_inc(ct_used, 1)
                        for b, (c0, width) in enumerate(BANKS):
                            last = nc.tensor.matmul(ps[:, b, 0:width], zrow[:], orow[:, 0:width], start=False, stop=True)
                        last.then_inc(acc_ready, 1)
                        pe.wait_ge(acc_copied, m + 1)
                        hold(pe, (sb_done, m + CREDIT))
                        for c in range(SB * DB // P):
                            last = nc.tensor.matmul(psf[:, 2048 + c * CH:2048 + (c + 1) * CH], sums[:, c * P:(c + 1) * P],
                                                    join[:], start=True, stop=True)
                        last.then_inc(joined, 1)

        @block.vector
        def _(dve):
            def bc_in(t, n=CH):
                return t[:, :, None].to_broadcast([P, NBLK, n])

            def bc_out(t):
                return t[:, None, :].to_broadcast([P, NBLK, CH])

            def nodes(t):
                return t[:, :].rearrange("p (c d) -> p c d", d=CH)

            for t in (X[:, (NBLK - 1) * CH:NC], w_ab[:], w_cv[:], b1r[:], ident[:], shift[:], wrap[:], cle[:],
                      prevk[:], S[:], join[:], zrow[:], fl[:]):
                nc.vector.memset(t, 0.0)
            for t in (orow, ones_b, ones_c):
                nc.vector.memset(t[:], 1.0)
            nc.vector.memset(ones1[:], 1.0).then_inc(cleared, 1)
            nc.vector.memset(low_cv[:], -2.0 * BIG)
            nc.vector.memset(sgn[:], 1.0)
            dve.drain()
            nc.vector.memset(low_cv[:, 1:2], 0.0)
            dve.wait_ge(made, 9)
            nc.vector.tensor_scalar(qi[:], qi[:], NODE_BITS, REAL | LOW, ALU.logical_shift_left, ALU.bitwise_or)
            nc.vector.tensor_scalar(qbi[:], qbi[:], 15, REAL, ALU.logical_shift_left, ALU.bitwise_or)
            nc.vector.tensor_copy(iota_r[:], iota_i[:])
            nc.vector.tensor_copy(pcolf[:], pcol[:])
            for j in range(SIGNS - 1):
                nc.vector.tensor_scalar(bit[:, j:j + 1], pcol[:], j, 1, ALU.logical_shift_right, ALU.bitwise_and)
            dve.drain()
            nc.vector.tensor_scalar(sgn[:, 0:SIGNS - 1], bit[:, 0:SIGNS - 1], -2.0, 1.0, ALU.mult, ALU.add)
            dve.drain()
            nc.vector.tensor_copy(flip[:, 0:1], sgn[:, 0:1])
            nc.vector.tensor_tensor(flip[:, 1:SIGNS], sgn[:, 0:SIGNS - 1], sgn[:, 1:SIGNS], ALU.mult)
            dve.wait_ge(ld_w, 128)
            for h in range(2):
                hs = slice(h * CH, (h + 1) * CH)
                nc.vector.tensor_copy(w_ab[hs, (2 + h) * P:(3 + h) * P], w1b[hs, :])
                last = nc.vector.tensor_tensor(w_ab[hs, h * P:(h + 1) * P], w_ab[hs, h * P:(h + 1) * P], w1b[hs, :],
                                               ALU.subtract)
            last.then_inc(setup_done, 1)

            def in_use(kind, L):
                unit = 2 << L
                return min(W, -(-NE // unit) * unit) if kind == "both" else W

            def network_step(kind, L, d, a, b):
                if kind == "flip":
                    return nc.vector.tensor_scalar(b, a, flip[:, L - LOGW:L - LOGW + 1], None, ALU.mult)
                if kind == "up":
                    av, bv = (t.rearrange("p (m h d) -> p m h d", h=2, d=d) for t in (a, b))
                    nc.vector.tensor_tensor(bv[:, :, 0, :], av[:, :, 0, :], av[:, :, 1, :], ALU.min)
                    return nc.vector.tensor_tensor(bv[:, :, 1, :], av[:, :, 0, :], av[:, :, 1, :], ALU.max)
                av, bv = (t[:, 0:in_use(kind, L)].rearrange("p (n r m h d) -> p n r m h d", r=2, h=2, d=d, m=(1 << L) // (2 * d)) for t in (a, b))
                for way in range(2):
                    lo, hi = av[:, :, way, :, 0, :], av[:, :, way, :, 1, :]
                    nc.vector.tensor_tensor(bv[:, :, way, :, way, :], lo, hi, ALU.min)
                    last = nc.vector.tensor_tensor(bv[:, :, way, :, 1 - way, :], lo, hi, ALU.max)
                return last

            kb_i = [t.bitcast(i32) for t in keyb]
            e_src, e_dst = (EX[:, n * NE:(n + 1) * NE].bitcast(i32) for n in range(2))

            def pair_keys(k, upper, lower):
                key = kb_i[0]
                nc.vector.memset(key[:, NE:], PAD)
                nc.vector.memset(kb_i[1][:, NE:], PAD)
                dve.wait_ge(ld_e, k * 32 + 32)
                nc.vector.tensor_scalar(key[:, 0:NE], upper, NODE_BITS, REAL, ALU.logical_shift_left, ALU.bitwise_or)
                dve.drain()
                nc.vector.tensor_tensor(key[:, 0:NE], key[:, 0:NE], lower, ALU.bitwise_or)
                dve.drain()

            def bucket_keys():
                key, tmp = kb_i[0], kb_i[1]
                nc.vector.memset(key[:, NE:], PAD)
                nc.vector.memset(tmp[:, NE:], PAD)
                dve.wait_ge(ld_e, 64)
                nc.vector.tensor_scalar(key[:, 0:NE], e_dst, 8, None, ALU.logical_shift_right)
                nc.vector.tensor_scalar(tmp[:, 0:NE], e_src, 7, None, ALU.logical_shift_right)
                dve.drain()
                nc.vector.scalar_tensor_tensor(key[:, 0:NE], key[:, 0:NE], float(NBLK), tmp[:, 0:NE], ALU.mult, ALU.add)
                dve.drain()
                nc.vector.tensor_scalar(key[:, 0:NE], key[:, 0:NE], 15, REAL, ALU.logical_shift_left, ALU.bitwise_or)
                nc.vector.tensor_scalar(tmp[:, 0:NE], e_src, P - 1, 8, ALU.bitwise_and, ALU.logical_shift_left)
                dve.drain()
                nc.vector.tensor_tensor(key[:, 0:NE], key[:, 0:NE], tmp[:, 0:NE], ALU.bitwise_or)
                dve.drain()
                nc.vector.tensor_scalar(tmp[:, 0:NE], e_dst, DB - 1, None, ALU.bitwise_and)
                dve.drain()
                nc.vector.tensor_tensor(key[:, 0:NE], key[:, 0:NE], tmp[:, 0:NE], ALU.bitwise_or)
                dve.drain()

            def network(k, steps=range(len(plan))):
                turn = sum(kind == "turn" for kind, L, d in plan[:steps[0]])
                for n in steps:
                    kind, L, d = plan[n]
                    if kind == "turn":
                        for b in range(0, 8, 2):
                            dve.wait_ge(turned, 8 * (TURNS[k] + turn) + b + 1)
                            nc.vector.tensor_copy(keyb[(n + 1) % 2][:, b * 512:(b + 1) * 512], ps[:, b, :])
                        turn += 1
                        dve.wait_ge(odd_copied, 4 * (TURNS[k] + turn))
                    else:
                        last = network_step(kind, L, d, keyb[n % 2], keyb[(n + 1) % 2])
                        if n + 1 < len(plan) and plan[n + 1][0] == "turn":
                            last.then_inc(turn_in, 1)
                    dve.drain()
                if steps[-1] == len(plan) - 1:
                    nc.vector.tensor_copy(subh[:], keyb[KEY_BUF].rearrange("p (a b) -> p a b", b=CH)[:, :, 0]).then_inc(heads_ready, 1)

            def segments(k):
                ks, kf = keyb[KEY_BUF], kb_i[1 - KEY_BUF]
                nc.vector.tensor_scalar(kf, kb_i[KEY_BUF], NODE_BITS, None, ALU.logical_shift_right)
                dve.wait_ge(back_in, k * 32 + 32)
                nc.vector.tensor_scalar(prevh[:], prevk[:].bitcast(i32), NODE_BITS, None, ALU.logical_shift_right)
                dve.drain()
                hi = EX[:, 0:W].bitcast(i32)
                if k == 0:
                    nc.vector.tensor_scalar(hi, kf, LOW, None, ALU.bitwise_and)
                nc.vector.tensor_tensor(keep[:, 1:W], kf[:, 1:W], kf[:, 0:W - 1], ALU.is_equal)
                nc.vector.tensor_tensor(keep[:, 0:1], kf[:, 0:1], prevh[:], ALU.is_equal).then_inc(turn_in, 1)
                dve.drain()
                if k == 0:
                    half = W // 2
                    assert half == TILES * P
                    hi2 = hi.rearrange("p (c n) -> p c n", n=half)
                    nc.vector.tensor_scalar(win[:], hi2[:, :, 0], WINDOW_END, None, ALU.min)
                    nc.vector.tensor_reduce(win_top[:], hi2, AX.X, ALU.max)
                    dve.drain()
                    nc.vector.tensor_tensor(local.rearrange("p (c n) -> p c n", n=half), hi2,
                                            win[:, :, None].to_broadcast([P, 2, half]), ALU.subtract)
                    nc.vector.tensor_tensor(win_top[:], win_top[:], win[:], ALU.subtract)
                    dve.drain()
                    nc.vector.tensor_reduce(fl[:, 3:4], win_top[:], AX.X, ALU.max)
                    dve.drain()
                    nc.vector.tensor_scalar(fl[:, 3:4], fl[:, 3:4], float(P - 1), None, ALU.is_gt)
                nc.vector.tensor_scalar(pen[:, :], keep[:, :], 2 * BIG, -BIG, ALU.mult, ALU.add).then_inc(masks_ready, 1)
                for b in range(0, 8, 2):
                    dve.wait_ge(turned, 8 * (TURNS[k] + NTURN) + b + 1)
                    nc.vector.tensor_copy(by_tile[:, :, 4 * b:4 * b + 4], ps[:, b, :].rearrange("p (j q) -> p q j", j=4))
                dve.wait_ge(odd_copied, 4 * (TURNS[k] + NTURN + 1))
                dve.drain()
                nc.vector.tensor_scalar(idx_lo, kf[:, 0:NT], LOW, None, ALU.bitwise_and)
                nc.vector.tensor_scalar(idx_hi, kf[:, 0:NT], NODE_BITS, LOW, ALU.logical_shift_right, ALU.bitwise_and)

            def search(k, queries, op, stages=range(3)):
                n = QCOLS[k]
                less = EX[:, :].bitcast(bf16)
                less1 = less[:, 0:n * P].rearrange("p (c d) -> p c d", d=P)
                less2 = less[:, 0:n * CH].rearrange("p (c d) -> p c d", d=CH)
                rows = HP[:, 0:n * CH].rearrange("p (c d) -> p c d", d=CH)

                def bc(width):
                    return queries[:, :, None].to_broadcast([P, n, width])

                if 0 in stages:
                    nc.vector.tensor_tensor(less1, headb[:, None, :].to_broadcast([P, n, P]), bc(P), op)
                    dve.drain()
                    nc.vector.tensor_reduce(r1[:, 0:n], less1, AX.X, ALU.add)
                    dve.drain()
                    nc.vector.tensor_scalar(r1[:, 0:n], r1[:, 0:n], -1.0, 0.0, ALU.add, ALU.max)
                    dve.drain()
                    nc.vector.tensor_copy(i1[:, 0:n], r1[:, 0:n]).then_inc(rows1_chosen, 1)
                if 1 in stages:
                    dve.wait_ge(g_sub, 16 * (QUERIED[k] + n))
                    nc.vector.tensor_tensor(less2, rows, bc(CH), op)
                    dve.drain()
                    nc.vector.tensor_reduce(sd[:, 0:n], less2, AX.X, ALU.add)
                    dve.drain()
                    nc.vector.tensor_scalar(sd[:, 0:n], sd[:, 0:n], -1.0, 0.0, ALU.add, ALU.max)
                    dve.drain()
                    nc.vector.scalar_tensor_tensor(r1[:, 0:n], r1[:, 0:n], float(CH), sd[:, 0:n], ALU.mult, ALU.add)
                    dve.drain()
                    nc.vector.tensor_copy(i2[:, 0:n], r1[:, 0:n]).then_inc(rows2_chosen, 1)
                if 2 in stages:
                    dve.wait_ge(g_key, 16 * (QUERIED[k] + n))
                    nc.vector.tensor_tensor(less2, rows, bc(CH), op)
                    dve.drain()
                    nc.vector.tensor_reduce(sd[:, 0:n], less2, AX.X, ALU.add)
                    dve.drain()
                    nc.vector.scalar_tensor_tensor(cle[:, 1:n + 1], r1[:, 0:n], float(CH), sd[:, 0:n],
                                                   ALU.mult, ALU.add).then_inc(counts_ready, 1)
                dve.drain()

            def ends(k):
                nc.vector.tensor_scalar(mu[:], cle[:, 1:], -1.0, 0.0, ALU.add, ALU.max)
                dve.drain()
                nc.vector.tensor_copy(e0[:], mu[:])
                dve.drain()
                nc.vector.tensor_scalar(e1[:], e0[:], (SORTED - 1) // (TILES * P) * (TILES * P), None, ALU.bitwise_and)
                nc.vector.tensor_scalar(e2[:], e0[:], P - 1, 4, ALU.bitwise_and, ALU.logical_shift_left)
                nc.vector.tensor_scalar(e3[:], e0[:], 7, TILES - 1, ALU.logical_shift_right, ALU.bitwise_and)
                dve.drain()
                nc.vector.tensor_tensor(e1[:], e1[:], e2[:], ALU.bitwise_or)
                dve.drain()
                nc.vector.tensor_tensor(endr[:], e1[:], e3[:], ALU.bitwise_or)
                dve.wait_ge(shifted, k + 1)
                nc.vector.tensor_tensor(cnt[:], cle[:, 1:], ps[:, 0, 0:NBLK], ALU.subtract)
                dve.drain()
                nc.vector.tensor_scalar(some[:], cnt[:], 0.0, None, ALU.is_gt).then_inc(order_done, 1)
                dve.drain()

            pair_keys(0, e_src, e_dst)
            network(0)
            segments(0)
            search(0, q, ALU.is_le, [0])
            dve.drain().then_inc(edges_wanted, 1)
            bucket_keys()
            quiet = plan.index(("flip", LOGW, 0))
            network(1, range(0, quiet // 2))
            search(0, q, ALU.is_le, [1])
            network(1, range(quiet // 2, quiet))
            search(0, q, ALU.is_le, [2])
            ends(0)
            network(1, range(quiet, len(plan)))
            dve.wait_ge(back_in, 64)
            same, later = HP[0:P - 1, 0:W], keyb[1 - KEY_BUF][0:P - 1, :]
            nc.vector.tensor_tensor(same, keyb[KEY_BUF][0:P - 1, :], later, ALU.is_equal)
            dve.drain()
            nc.vector.scalar_tensor_tensor(same, later, PAD_VALUE, same, ALU.is_lt, ALU.mult)
            dve.drain()
            nc.vector.tensor_reduce(fl[0:P - 1, 0:1], same, AX.X, ALU.max)
            dve.drain()
            search(1, qb, ALU.is_lt)
            dve.wait_ge(shifted, 2)
            nc.vector.tensor_tensor(mu[:, 0:BCOLS], cle[:, 1:BCOLS + 1], ps[:, 0, 0:BCOLS], ALU.subtract)
            dve.drain()
            nc.vector.tensor_reduce(fl[:, 1:2], mu[:, 0:BCOLS], AX.X, ALU.max)
            dve.drain()
            nc.vector.tensor_scalar(fl[:, 1:2], fl[:, 1:2], float(MOST), None, ALU.is_gt)
            dve.drain()
            nc.vector.tensor_reduce(fl[:, 2:3], fl[:, :], AX.X, ALU.max).then_inc(flag_in, 1)
            nc.vector.tensor_copy(e0[:, 0:BCOLS], cle[:, 1:BCOLS + 1])
            dve.drain()
            dve.wait_ge(flag_in, 2)
            nc.vector.tensor_copy(flag[:], ps[0:1, 1, 0:1]).then_inc(flag_ready, 1)
            nc.vector.tensor_scalar(i1[:, 0:BCOLS], e0[:, 0:BCOLS], 7, None, ALU.logical_shift_right)
            for bn in range(7):
                nc.vector.tensor_scalar(bit_on[:, bn, :], e0[:, 0:BCOLS], bn, 1, ALU.logical_shift_right, ALU.bitwise_and)
            dve.drain()
            nc.vector.tensor_scalar(i2[:, 0:BCOLS], i1[:, 0:BCOLS], 1.0, None, ALU.add).then_inc(starts_ready, 1)
            H = BCOLS // 2
            for h in range(2):
                dve.wait_ge(g_pairs, 32 * H * (h + 1))
                if h:
                    dve.wait_ge(b_turned, h)
                bufs = [t[:, 0:H * 2 * P].rearrange("p (c n) -> p c n", n=2 * P) for t in (EX, HP)]
                left = 2 * P
                for n, bn in enumerate(range(6, -1, -1)):
                    a, b = bufs[n % 2], bufs[(n + 1) % 2]
                    left = P + (1 << bn) - 1
                    nc.vector.tensor_copy(b[:, :, 0:left], a[:, :, 0:left])
                    dve.drain()
                    mask = bit_on[:, bn, h * H:(h + 1) * H][:, :, None].to_broadcast([P, H, left])
                    moved = nc.vector.copy_predicated(b[:, :, 0:left], mask, a[:, :, (1 << bn):(1 << bn) + left])
                    if n == 6:
                        moved.then_inc(b_shifted, 1)
                    dve.drain()
                if h == 0:
                    dve.drain().then_inc(starts_ready, 1)
            dve.drain().then_inc(cols_made, 1)
            dve.wait_ge(b_copied, 2)
            NBC = BCOLS * P
            turned_keys, nums = arena[:, 0:NBC].bitcast(i32), HP[:, 0:NBC].bitcast(i32)
            nc.vector.tensor_scalar(nums, turned_keys, 8, P - 1, ALU.logical_shift_right, ALU.bitwise_and)
            dve.drain()
            nc.vector.tensor_copy(vS, nums)
            dve.drain()
            nc.vector.tensor_scalar(nums, turned_keys, 15, None, ALU.logical_shift_right)
            dve.wait_ge(cols_made, 2)
            dve.drain()
            nc.vector.tensor_tensor(EX[:, 0:NBC], nums, EX[:, 0:NBC].bitcast(i32), ALU.is_equal)
            dve.drain()
            nc.vector.tensor_scalar(nums, turned_keys, DB - 1, None, ALU.bitwise_and)
            dve.drain()
            nc.vector.scalar_tensor_tensor(HP[:, 0:NBC], nums, 1.0, EX[:, 0:NBC], ALU.add, ALU.mult)
            dve.drain()
            nc.vector.tensor_scalar(vD, HP[:, 0:NBC], -1.0, None, ALU.add).then_inc(b_ready, 1)
            dve.drain().then_inc(order_done, 1)

            def scan(G, k, g, op0, op1):
                dve.wait_ge(m_ready, G + (CREDIT + 1))
                dve.wait_ge(o_ready, G + (CREDIT - 1))
                dve.wait_ge(scan_done, G + CREDIT)
                nc.vector.tensor_tensor_scan(S[:, g % 2, :], msk[k][:, g * 512:(g + 1) * 512],
                                             ps[0:CH, 2 + g % 2, :], S[:, 1 - g % 2, 511:512],
                                             op0, op1).then_inc(scan_done, 1)

            def scans(before, op0, op1):
                with dve.Fori(0, NCH // 2, 1) as i:
                    for k in range(2):
                        dve.wait_ge(msk_in[k], (i * 2 + before + 2) * 8 + before // NCH * 16)
                        for g in range(GROUPS):
                            scan((i * 2 + before + k) * GROUPS + g, k, g, op0, op1)

            def layer_norm(t, n):
                tv = nodes(t)
                nc.vector.tensor_reduce(mu[:], tv, AX.X, ALU.add)
                dve.drain()
                nc.vector.tensor_scalar(mu[:], mu[:], 1.0 / CH, None, ALU.mult)
                dve.drain()
                nc.vector.tensor_tensor(tv, tv, bc_in(mu), ALU.subtract)
                dve.drain()
                nc.vector.tensor_tensor(TMP, t[:, :], t[:, :], ALU.mult)
                dve.drain()
                nc.vector.tensor_reduce(sd[:], nodes(TMP), AX.X, ALU.add)
                dve.drain()
                nc.vector.tensor_scalar(mu[:], sd[:], 1.0 / CH, EPS, ALU.mult, ALU.add).then_inc(var_ready, 1)
                dve.wait_ge(rooted, n)
                nc.vector.reciprocal(mu[:], sd[:])
                dve.drain()
                return nc.vector.tensor_tensor(tv, tv, bc_in(mu), ALU.mult)

            dve.sem_inc(scan_done, CREDIT)
            dve.wait_ge(flag_ready, 1)
            general = dve.value_load(flag[0:1, 0:1])
            with dve.If(general > 0):
                scans(0, ALU.min, ALU.max)
            with dve.Else():
                with dve.Fori(0, NDB, 1) as d:
                    for n in range(FUSED):
                        c, k = d * FUSED + n, n % 2
                        dve.wait_ge(msk_in[k], d * (FUSED * 8) + (n // 2 + 1) * 16)
                        dve.wait_ge(win_in[k], d * (FUSED * 16) + (n // 2 + 1) * 32)
                        for g in range(PHASES):
                            if g < GROUPS:
                                dve.wait_ge(t_ready, c * GROUPS + (g + CREDIT - 1))
                                nc.vector.tensor_scalar(one_a[g % 2], loc[k][:, g * 512:(g + 1) * 512], pcolf[:], None,
                                                        ALU.is_equal).then_inc(one_a_ready, 1)
                            for m in share(n, g):
                                dve.wait_ge(count_ready, d * BPAIRS + (m + 1 + CREDIT - 7))
                                for u in range(2):
                                    b = d * NBLK + (2 * m + u)
                                    nc.vector.tensor_scalar(one_s[:, m % 7, u, :], iota_r[:, 0:P], vS[:, bass.ds(b, 1)],
                                                            None, ALU.is_equal)
                                    last = nc.vector.tensor_scalar(one_d[:, m % 7, u, :], iota_r[:], vD[:, bass.ds(b, 1)],
                                                                   None, ALU.is_equal)
                                last.then_inc(hot_ready, 1)
                            if 0 <= g - 1 < GROUPS:
                                scan(c * GROUPS + (g - 1), k, g - 1, ALU.min, ALU.max)
                dve.wait_ge(deg_summed, 1)
                nc.vector.tensor_copy(deg[:], ps[:, 7, 0:NBLK])
                dve.wait_ge(count_free, NDB * 7 + CREDIT)
            dve.wait_ge(g_end, 16 * NBLK)
            nc.vector.tensor_tensor(nodes(EX), nodes(EX), bc_out(b2b), ALU.add)
            dve.drain()
            nc.vector.tensor_tensor(TMP, EX[:], EX[:], ALU.subtract)
            nc.vector.memset(HP[:], 0.0)
            dve.drain()
            nc.vector.tensor_scalar(TMP, TMP, 0.0, None, ALU.is_equal)
            dve.drain()
            nc.vector.tensor_tensor(nodes(TMP), nodes(TMP), bc_in(some), ALU.mult)
            dve.drain()
            nc.vector.copy_predicated(HP[:], TMP.bitcast(i32), EX[:])
            dve.drain()
            nc.vector.tensor_tensor(X[:], X[:], HP[:], ALU.add)
            dve.drain()
            layer_norm(X, 1)
            dve.drain()
            nc.vector.tensor_copy(EX[:], X[:])
            dve.drain()
            n2 = 2 * PPI

            def inverse_roots(degrees):
                nc.vector.tensor_scalar(e_deg[:], degrees[:], 1.0, 1e-12, ALU.add, ALU.max).then_inc(deg_ready, 1)
                dve.wait_ge(rooted, 2)
                nc.vector.reciprocal(dinv[:], dinv[:])
                dve.drain()

            def project(r):
                with dve.Fori(0, STEPS, 1) as k:
                    nc.vector.tensor_copy(stage[:], EX[:, bass.ds(k * (PPI * P), PPI * P)]).then_inc(h_staged, 1)
                    dve.wait_ge(t_proj, r * STEPS + k + (2 * STEPS + 1))
                    nc.vector.tensor_tensor(HP[:, bass.ds(k * (PPI * P), PPI * P)].rearrange("p (c d) -> p c d", d=CH),
                                            psf[:, 1024:1024 + PPI * P].rearrange("p (c d) -> p c d", d=CH),
                                            dinv[:, bass.ds(k * n2, n2)][:, :, None].to_broadcast([P, n2, CH]),
                                            ALU.mult)
                    dve.drain()

            def out_of(r, t, tv, n, inv):
                nc.vector.tensor_tensor(tv, tv, inv, ALU.mult)
                dve.drain()
                nc.vector.tensor_tensor(tv, tv, b_cv[:, bass.ds(r * CH, CH)][:, None, :].to_broadcast([P, n, CH]), ALU.add)
                dve.drain()
                nc.vector.tensor_scalar(t, t, low_cv[:, bass.ds(r, 1)], None, ALU.max)
                dve.drain()

            with dve.If(general > 0):
                dve.drain().then_inc(ex_free, 1)
                pair_keys(2, e_dst, e_src)
                network(2)
                segments(2)
                search(2, q, ALU.is_le)
                ends(2)
                nc.vector.tensor_copy(EX[:], X[:])
                inverse_roots(cnt)
                with dve.Fori(0, 3, 1) as r:
                    project(r)
                    dve.drain().then_inc(h_ready, 1)
                    scans((r + 1) * NCH, ALU.mult, ALU.add)
                    dve.wait_ge(g_end, r * (16 * NBLK) + 32 * NBLK)
                    nc.vector.tensor_tensor(nodes(EX), nodes(EX), bc_in(some), ALU.mult)
                    dve.drain()
                    nc.vector.tensor_tensor(EX[:], EX[:], HP[:], ALU.add)
                    dve.drain()
                    out_of(r, EX[:], nodes(EX), NBLK, bc_in(dinv))
            with dve.Else():
                inverse_roots(deg)
                dve.sem_inc(sb_done, CREDIT)
                dve.drain().then_inc(degrees_done, 1)
                with dve.Fori(0, 3, 1) as r:
                    project(r)
                    nc.vector.tensor_reduce(top[:], HP[:], AX.X, ALU.max, apply_absolute_value=True).then_inc(top_ready, 1)
                    dve.wait_ge(top_row, r + 1)
                    nc.vector.tensor_reduce(one1[:], ps[0:1, 4, 0:P], AX.X, ALU.max).then_inc(top_one, 1)
                    dve.wait_ge(top_all, r + 1)
                    nc.vector.tensor_scalar(top[:], ps[:, 4, 0:1], 2.0 ** -100, None, ALU.max)
                    dve.drain()
                    nc.vector.tensor_scalar(expo[:], top[:].bitcast(i32), 0x7F800000, None, ALU.bitwise_and)
                    dve.drain()
                    nc.vector.tensor_scalar(scale[:].bitcast(i32), expo[:], -1.0, float((2 * 127 + 13) << 23), ALU.mult, ALU.add)
                    nc.vector.tensor_scalar(unscale[:].bitcast(i32), expo[:], float(-(13 << 23)), None, ALU.add)
                    dve.drain()
                    nc.vector.tensor_scalar(EX[:], HP[:], scale[:], None, ALU.mult)
                    dve.drain()
                    nc.vector.tensor_copy(parts[:, :, 0:CH], nodes(EX))
                    dve.drain()
                    nc.vector.tensor_tensor(nodes(EX), nodes(EX), parts[:, :, 0:CH], ALU.subtract)
                    dve.drain()
                    nc.vector.tensor_scalar(parts[:, :, CH:P], nodes(EX), SPLIT, None, ALU.mult).then_inc(parts_ready, 1)
                    dve.drain()
                    with dve.Fori(0, NDB // SB, 1) as n:
                        dve.wait_ge(joined, r * SB + n + 1)
                        wide = SB * DB // P
                        o = EX[:, bass.ds(n * (wide * CH), wide * CH)]
                        ov = o.rearrange("p (c d) -> p c d", d=CH)
                        nc.vector.scalar_tensor_tensor(o, psf[:, 2048:2048 + wide * CH], unscale[:],
                                                       HP[:, bass.ds(n * (wide * CH), wide * CH)], ALU.mult,
                                                       ALU.add).then_inc(sb_done, 1)
                        dve.drain()
                        out_of(r, o, ov, wide, dinv[:, bass.ds(n * wide, wide)][:, :, None].to_broadcast([P, wide, CH]))
            nc.vector.tensor_reduce(mu[:], nodes(EX), AX.X, ALU.max)
            dve.drain()
            nc.vector.tensor_tensor(nodes(EX), nodes(EX), bc_in(mu), ALU.subtract).then_inc(shifted_down, 1)
            dve.wait_ge(exped, 1)
            nc.vector.tensor_reduce(sd[:], nodes(TMP), AX.X, ALU.add).then_inc(sum_ready, 1)
            dve.wait_ge(logged, 1)
            nc.vector.tensor_tensor(nodes(EX), nodes(EX), bc_in(mu), ALU.subtract)
            dve.drain()
            nc.vector.tensor_tensor(X[:], X[:], EX[:], ALU.add)
            dve.drain()
            layer_norm(X, 3).then_inc(out_ready, 1)


_INS = ['x', 'src', 'dst', 'L0_gnn_W1', 'L0_gnn_b1', 'L0_gnn_W2', 'L0_gnn_b2',
        'L1_gnn_W1', 'L1_gnn_b1', 'L1_gnn_W2', 'L1_gnn_b2']
_OUTS = [((N_NODES, CH), 'float32')]


def kernel(**inputs):
    import numpy as _np
    import concourse.bacc as _bacc
    from concourse import mybir as _mybir
    from concourse.bass_utils import run_bass_kernel_spmd as _run

    nc = _bacc.Bacc("TRN2", target_bir_lowering=False, num_devices=1)
    arrays, args = {}, []
    for name in _INS:
        a = _np.ascontiguousarray(inputs[name])
        arrays[f"in_{name}_dram"] = a
        args.append(nc.dram_tensor(f"in_{name}_dram", a.shape, _mybir.dt.from_np(a.dtype), kind="ExternalInput").ap())
    for i, (shape, dtype) in enumerate(_OUTS):
        dt = _mybir.dt.from_np(_np.dtype(dtype))
        args.append(nc.dram_tensor(f"out_{i}_dram", shape, dt, kind="ExternalOutput").ap())
    gnn(nc, *args)
    r = _run(nc, [arrays], core_ids=[0])
    return r.results[0]["out_0_dram"]
```

```python
import concourse.bass as bass
from concourse import mybir
from contextlib import ExitStack

P = 128
N_NODES, CH, HID = 12500, 64, 128
N_EDGES = 400000
NBLK = -(-N_NODES // P)
LAST = N_NODES - (NBLK - 1) * P
NC = NBLK * CH
LOGW = 12
W = 1 << LOGW
SORTED = P * W
NODE_BITS = 14
LOW = (1 << NODE_BITS) - 1
REAL = 0x20000000
PAD = 0x30000000
TILES = 16
NCH = -(-N_EDGES // (P * TILES))
NCH += NCH % 2
NT = NCH * TILES
HALF = TILES // 2
GROUPS = TILES // 4
CREDIT = 8
BIG = 1.5e38
PAD_VALUE = 2.0 ** -31
EPS = 1e-5
DB = 256
NDB = NBLK * P // DB
BUCKETS = NBLK * NDB
BCOLS = -(-BUCKETS // P)
MOST = P
MOST_SAME = 16
SB = 7
SRC_GROUP = 14
PARTS = [9, 9] + [8] * 10
SPLIT = 2048.0
PAIRS = NBLK // 2
PPI = 7
SIGNS = 8
WINDOW_END = NBLK * P - P


def gnn(nc, x, src, dst, w1, b1, w2, b2, cw1, cb1, cw2, cb2, out):
    f32, bf16, i32, f16 = mybir.dt.float32, mybir.dt.bfloat16, mybir.dt.int32, mybir.dt.float16
    ALU, ACT, AX = mybir.AluOpType, mybir.ActivationFunctionType, mybir.AxisListType

    ctx = ExitStack()
    with ctx:
        def sb(name, shape, dt):
            return ctx.enter_context(nc.sbuf_tensor(name, shape, dt))

        def sem(name):
            return ctx.enter_context(nc.semaphore(name))

        def dram(name, shape, dt):
            return nc.dram_tensor(name, shape, dt, kind="Internal").ap()

        d_a = dram("table_a", (NBLK * P, HID), f32)
        d_b = dram("table_b", (NBLK * P, HID), f32)
        d_h = dram("table_h", (NBLK * P, CH), f32)
        d_keys = dram("sorted_keys", (SORTED // CH, CH), f32)
        d_sub = dram("sub_heads", (P, CH), f32)
        d_head = dram("heads", (P, 1), f32)
        d_last = dram("last_keys", (P, 1), f32)
        d_keep = dram("keep", (1, SORTED), bf16)
        d_local = dram("local_sources", (1, SORTED), bf16)
        d_first = dram("window_firsts", (P, 2), i32)
        d_early = dram("early_rows", (NDB, P, TILES * HID), f32)
        d_pen = dram("penalty", (1, SORTED), bf16)
        d_rows = dram("scan_rows", (NT * P, CH), f32)

        d_count = dram("edge_counts", (NDB, P, NBLK * DB // 2), bf16)

        X = sb("X", [P, NC], f32)
        NE = N_EDGES // P
        EX = sb("EX", [P, NC], f32)
        HP = sb("HP", [P, NC], f32)
        arena = sb("arena", [P, 2 * W], f32)
        keyb = [arena[:, 0:W], arena[:, W:2 * W]]
        TMP = arena[:, 0:NC]
        U = sb("U", [P, 15872], f32)
        idx_lo = U[:, 0:NT].bitcast(i32)
        idx_hi = U[:, NT:2 * NT].bitcast(i32)
        loc = [U[:, NT + k * TILES * P // 2:NT + (k + 1) * TILES * P // 2].bitcast(bf16) for k in range(2)]
        one_a = [U[:, NT + TILES * P + k * 512:NT + TILES * P + (k + 1) * 512] for k in range(2)]
        at = 2 * NT
        msk_all = U[:, at:at + TILES * P].bitcast(bf16)
        msk = [msk_all[0:CH, k * TILES * P:(k + 1) * TILES * P] for k in range(2)]
        at += TILES * P
        keep = U[:, at:at + W // 2].bitcast(bf16)
        pen = U[:, at + W // 2:at + W].bitcast(bf16)
        local = U[:, at + W:at + W + W // 2].bitcast(bf16)
        early = U[:, at:at + 2 * TILES * HID].rearrange("p (k n) -> p k n", k=2)
        vS = U[:, at:at + BCOLS * P // 2].bitcast(bf16)
        at += BCOLS * P // 2
        vD = U[:, at:at + BCOLS * P // 2].bitcast(bf16)
        at += BCOLS * P // 2
        one_s = U[:, at:at + 7 * P].bitcast(bf16).rearrange("p (j u n) -> p j u n", j=7, u=2)
        at += 7 * P
        one_d = U[:, at:at + 7 * DB].bitcast(bf16).rearrange("p (j u n) -> p j u n", j=7, u=2)
        assert at + 7 * DB <= 15872
        CT = max(PARTS) * SB * DB // 4
        ct = [U[:, k * CT:(k + 1) * CT].bitcast(mybir.dt.float8e4) for k in range(3)]
        ct_load = [U[:, k * CT:(k + 1) * CT].bitcast(bf16) for k in range(3)]
        ctile = arena[:, 0:7 * SRC_GROUP * DB // 4].bitcast(mybir.dt.float8e4).rearrange("p (g n) -> p g n", g=7)
        ctile_out = arena[:, 0:7 * SRC_GROUP * DB // 4].bitcast(bf16).rearrange("p (g n) -> p g n", g=7)
        rows_b = HP[:, 0:2 * TILES * HID].rearrange("p (k t d) -> p k t d", k=2, t=TILES)
        window = [HP[:, (2 * TILES + k) * HID:(2 * TILES + k + 1) * HID] for k in range(2)]
        parts = arena[:, 0:NC].bitcast(f16).rearrange("p (c n) -> p c n", n=P)
        room = sb("room", [P, 2 * TILES * CH], f32)
        outr = room[:, :].rearrange("p (k n) -> p k n", k=2)
        stage = room[:, 0:PPI * P]
        stageT = room[:, PPI * P:2 * PPI * P]
        sums = room[:, 0:2 * PPI * P]
        R = sb("R", [P, 2, 512], f32)
        S = sb("S", [CH, 2, 512], f32)
        stg = sb("stg", [P, 2, 2 * TILES], i32)
        ident = sb("ident", [P, P], f32)
        shift = sb("shift", [P, P], f32)
        wrap = sb("wrap", [P, P], f32)
        w_ab = sb("w_ab", [P, 4 * P], f32)
        w1b = sb("w1b", [P, HID], f32)
        w2s = sb("w2s", [HID, CH], f32)
        b1r = sb("b1r", [1, 4 * P], f32)
        ones1 = sb("ones1", [1, P], f32)
        b2b = sb("b2b", [P, CH], f32)
        w_cv = sb("w_cv", [P, 3 * P], f32)
        b_cv = sb("b_cv", [P, 3 * CH], f32)
        low_cv = sb("low_cv", [P, 3], f32)
        pcol = sb("pcol", [P, 1], i32)
        pcolf = sb("pcolf", [P, 1], f32)
        bit = sb("bit", [P, SIGNS], i32)
        sgn = sb("sgn", [P, SIGNS], f32)
        flip = sb("flip", [P, SIGNS], f32)
        qi = sb("qi", [P, NBLK], i32)
        q = qi[:, :].bitcast(f32)
        subh = sb("subh", [P, CH], f32)
        headb = sb("headb", [P, P], f32)
        prevk = sb("prevk", [P, 1], f32)
        prevh = sb("prevh", [P, 1], i32)
        r1 = sb("r1", [P, NBLK], f32)
        i1 = sb("i1", [P, NBLK], i32)
        i2 = sb("i2", [P, NBLK], i32)
        cle = sb("cle", [P, NBLK + 1], f32)
        cnt = sb("cnt", [P, NBLK], f32)
        some = sb("some", [P, NBLK], f32)
        endr = sb("endr", [P, NBLK], i32)
        e0 = sb("e0", [P, NBLK], i32)
        e1 = sb("e1", [P, NBLK], i32)
        e2 = sb("e2", [P, NBLK], i32)
        e3 = sb("e3", [P, NBLK], i32)
        dinv = sb("dinv", [P, NBLK], f32)
        deg = sb("deg", [P, NBLK], f32)
        e_deg = sb("e_deg", [P, NBLK], f32)
        qbi = sb("qbi", [P, BCOLS], i32)
        qb = qbi[:, :].bitcast(f32)
        bit_on = sb("bit_on", [P, 7, BCOLS], i32)
        iota_i = sb("iota_i", [P, DB], i32)
        iota_r = sb("iota_r", [P, DB], bf16)
        ones_b = sb("ones_b", [P, 1], bf16)
        ones_c = sb("ones_c", [P, 1], f32)
        zrow = sb("zrow", [1, P], bf16)
        orow = sb("orow", [1, 512], bf16)
        join = sb("join", [P, CH], f32)
        fl = sb("fl", [P, 4], f32)
        win = sb("win", [P, 2], i32)
        win_top = sb("win_top", [P, 2], i32)
        firsts = iota_i[0:1, :]
        flag = sb("flag", [1, 1], i32)
        top = sb("top", [P, 1], f32)
        one1 = sb("one1", [1, 1], f32)
        expo = sb("expo", [P, 1], i32)
        scale = sb("scale", [P, 1], f32)
        unscale = sb("unscale", [P, 1], f32)
        mu = sb("mu", [P, NBLK], f32)
        sd = sb("sd", [P, NBLK], f32)

        ps = ctx.enter_context(nc.psum_tensor("ps", [P, 8, 512], f32))
        psf = ps[:, :, :].rearrange("p b n -> p (b n)")

        cleared, made, setup_done = sem("cleared"), sem("constants_made"), sem("setup_done")
        ld_x, ld_e, ld_w, ld_cw = sem("x_loaded"), sem("edges_loaded"), sem("weights_loaded"), sem("conv_weights_loaded")

        staged, t_turned, t_evac, t_proj, t_copied, t_stored = (sem(n) for n in (
            "nodes_staged", "nodes_turned", "turned_copied", "projected", "projection_copied", "tables_stored"))
        turn_in, turned, odd_copied = sem("keys_to_turn"), sem("keys_turned"), sem("odd_banks_copied")
        heads_ready, masks_ready = sem("heads_ready"), sem("masks_ready")
        keys_out, back_in, masks_out = sem("keys_stored"), sem("heads_loaded"), sem("masks_stored")
        rows1_chosen, rows2_chosen, counts_ready, shifted = (sem(n) for n in (
            "sub_head_rows_chosen", "key_rows_chosen", "counts_ready", "counts_shifted"))
        g_sub, g_key, order_done = sem("sub_heads_gathered"), sem("key_rows_gathered"), sem("order_done")
        gath = [[sem(f"message_rows_gathered_{k}_{h}") for h in range(2)] for k in range(2)]
        gath_cv = [[sem(f"feature_rows_gathered_{k}_{h}") for h in range(2)] for k in range(2)]
        staged_idx = sem("indices_staged")
        t_ready, relu_done, m_ready, scan_done, o_ready, out_copied, out_free = (sem(n) for n in (
            "messages_summed", "relu_done", "columns_ready", "scanned", "rows_turned", "rows_copied", "rows_stored"))
        msk_in = [sem("mask_loaded_0"), sem("mask_loaded_1")]
        outd = [sem("rows_out_0"), sem("rows_out_1")]
        h_staged = sem("conv_nodes_staged")
        g_end, h_ready, h_out = sem("ends_gathered"), sem("features_ready"), sem("features_stored")
        var_ready, deg_ready, rooted = sem("variance_ready"), sem("degree_ready"), sem("rooted")
        shifted_down, exped, sum_ready, logged, out_ready = (sem(n) for n in (
            "logits_shifted", "exponentiated", "sum_ready", "logarithm_done", "output_ready"))
        stored = sem("output_stored")
        ex_free, edges_wanted = sem("ex_free"), sem("edges_wanted")
        early_in = [sem("early_rows_gathered_0"), sem("early_rows_gathered_1")]
        early_out = [sem("early_rows_out_0"), sem("early_rows_out_1")]
        early_staged, early_free, early_back = sem("early_indices_staged"), sem("early_rows_stored"), sem("early_rows_loaded")
        firsts_in, one_a_ready = sem("window_firsts_loaded"), sem("one_hot_sources_ready")
        win_in = [sem("window_loaded_0"), sem("window_loaded_1")]
        flag_in, flag_ready = sem("overflows_found"), sem("path_chosen")
        starts_ready, g_pairs, b_shifted, b_turned, b_copied, b_ready = (sem(n) for n in (
            "bucket_rows_chosen", "bucket_rows_gathered", "buckets_aligned", "buckets_turned", "buckets_copied", "bucket_columns_ready"))
        cols_made = sem("bucket_numbers_made")
        hot_ready, count_ready, count_copied, count_free = (sem(n) for n in (
            "one_hots_ready", "counts_summed", "counts_copied", "counts_stored"))
        c_out = [sem(f"counts_out_{g}") for g in range(7)]
        deg_summed, degrees_done = sem("degrees_summed"), sem("degrees_done")
        top_ready, top_row, top_one, top_all = (sem(n) for n in (
            "partition_maxima", "maxima_turned", "maximum_found", "maximum_spread"))
        parts_ready, acc_ready, acc_copied, joined, sb_done = (sem(n) for n in (
            "parts_ready", "block_summed", "block_sums_copied", "block_joined", "block_done"))
        ct_in = [sem(f"counts_in_{k}") for k in range(3)]
        ct_used = sem("counts_used")
        passed = {e.engine: sem(f"passed_{n}") for n, e in (("sp", nc.sync), ("pool", nc.gpsimd), ("pe", nc.tensor), ("act", nc.scalar))}

        plan = [("both", L, 1 << d) for L in range(1, LOGW) for d in range(L - 1, -1, -1)]
        plan.append(("flip", LOGW, 0))
        plan += [("up", LOGW, 1 << d) for d in range(LOGW - 1, -1, -1)]
        for L in range(LOGW + 1, LOGW + 8):
            plan += [("flip", L, 0), ("turn", L, 0)]
            plan += [("up", L, 1 << d) for d in range(L - LOGW - 1, -1, -1)]
            plan.append(("turn", L, 0))
            plan += [("up", L, 1 << d) for d in range(LOGW - 1, -1, -1)]
        turn_from = [n % 2 for n, e in enumerate(plan) if e[0] == "turn"]
        KEY_BUF = len(plan) % 2
        NTURN = len(turn_from)
        TURNS = [0, NTURN + 1, 2 * NTURN + 1]
        QCOLS = [NBLK, BCOLS, NBLK]
        QUERIED = [0, NBLK, NBLK + BCOLS]
        STEPS = PAIRS // PPI
        FUSED = NCH // NDB
        FGROUPS = FUSED * GROUPS
        PHASES = FGROUPS + 2
        BPAIRS = NBLK // 2

        EARLY_PAIRS = NDB // 2 - 2

        def share(f):
            return range(f * BPAIRS // PHASES, (f + 1) * BPAIRS // PHASES)

        def place(f):
            return f // GROUPS, f // GROUPS % 2, f % GROUPS

        by_tile = keyb[1 - KEY_BUF].rearrange("p (q f) -> p q f", q=P)
        def hold(eng, *waits):
            for signal, value in waits:
                eng.wait_ge(signal, value)
            eng.sem_inc(passed[eng.engine], 1)

        block = ctx.enter_context(nc.Block())

        @block.sync
        def _(sp):
            sp.wait_ge(cleared, 1)
            sp.dma_start(X[:, 0:(NBLK - 1) * CH].rearrange("p (c d) -> p c d", d=CH),
                         x[0:(NBLK - 1) * P, :].rearrange("(c p) d -> p c d", p=P)).then_inc(ld_x, 16)
            sp.dma_start(X[0:LAST, (NBLK - 1) * CH:NC], x[(NBLK - 1) * P:, :]).then_inc(ld_x, 16)
            for h in range(2):
                sp.dma_start(w_ab[h * CH:(h + 1) * CH, h * P:(h + 1) * P], w1[0:CH, :]).then_inc(ld_w, 16)
                sp.dma_start(w1b[h * CH:(h + 1) * CH, :], w1[CH:2 * CH, :]).then_inc(ld_w, 16)
                sp.dma_start(b1r[0:1, h * P:(h + 1) * P], b1[None, :]).then_inc(ld_w, 16)
            sp.dma_start(w2s[:], w2).then_inc(ld_w, 16)
            sp.dma_start(b2b[:], b2.partition_broadcast(P)).then_inc(ld_w, 16)
            for k, (w, b) in enumerate(((cw1, cb1), (cw1, cb1), (cw2, cb2))):
                for h in range(2):
                    sp.dma_start(w_cv[h * CH:(h + 1) * CH, k * P + h * CH:k * P + (h + 1) * CH], w).then_inc(ld_cw, 16)
                sp.dma_start(b_cv[:, k * CH:(k + 1) * CH], b.partition_broadcast(P)).then_inc(ld_cw, 16)

            def load_edges():
                for n, e in enumerate((src, dst)):
                    sp.dma_start(EX[:, n * NE:(n + 1) * NE], e.rearrange("(p w) -> p w", p=P).bitcast(f32)).then_inc(ld_e, 16)

            load_edges()
            A_v = d_a.rearrange("(k c p) d -> k p c d", p=P, c=2 * PPI)
            B_v = d_b.rearrange("(k c p) d -> k p c d", p=P, c=2 * PPI)
            nA = 2 * PPI * HID
            with sp.Fori(0, STEPS, 1) as k:
                for n, table in enumerate((A_v, B_v)):
                    sp.wait_ge(t_copied, k * 2 + (n + 1))
                    sp.dma_start(table[bass.ds(k, 1)].rearrange("o p c d -> (o p) c d"),
                                 HP[:, n * nA:(n + 1) * nA].rearrange("p (c d) -> p c d", d=HID)).then_inc(t_stored, 16)
            def sort_io(k):
                sp.wait_ge(heads_ready, k + 1)
                sp.dma_start(d_keys.rearrange("(p a) b -> p (a b)", p=P), keyb[KEY_BUF]).then_inc(keys_out, 16)
                sp.dma_start(d_sub, subh[:]).then_inc(keys_out, 16)
                sp.dma_start(d_head, subh[:, 0:1]).then_inc(keys_out, 16)
                sp.dma_start(d_last, keyb[KEY_BUF][:, W - 1:W]).then_inc(keys_out, 16)
                sp.wait_ge(keys_out, k * 64 + 64)
                sp.dma_start(headb[:], d_head.rearrange("p o -> (p o)").partition_broadcast(P)).then_inc(back_in, 16)
                if k == 1:
                    later = d_keys.rearrange("a b -> (a b)")[MOST_SAME:MOST_SAME + (P - 1) * W]
                    sp.dma_start(keyb[1 - KEY_BUF][0:P - 1, :], later.rearrange("(p w) -> p w", w=W)).then_inc(back_in, 16)
                else:
                    sp.dma_start(prevk[1:P, :], d_last[0:P - 1, :]).then_inc(back_in, 16)
                    sp.wait_ge(masks_ready, k // 2 + 1)
                    rows, t = (d_pen, pen) if k == 0 else (d_keep, keep)
                    sp.dma_start(rows.rearrange("o (p w) -> (o p) w", p=P), t).then_inc(masks_out, 16)
                    if k == 0:
                        sp.dma_start(d_local.rearrange("o (p w) -> (o p) w", p=P), local).then_inc(masks_out, 16)
                        sp.dma_start(d_first, win[:]).then_inc(masks_out, 16)
                    sp.wait_ge(masks_out, 48 + k // 2 * 16)
                    if k == 0:
                        sp.dma_start(firsts, d_first.rearrange("(o p) k -> o (p k)", o=1)).then_inc(firsts_in, 16)

            sort_io(0)
            sp.wait_ge(edges_wanted, 1)
            load_edges()
            sp.sem_inc(early_free, CREDIT)

            def store_early(i, k):
                lot = i * 2 + k
                hold(sp, (early_in[k], i * (16 * TILES) + 16 * TILES))
                row = d_early[bass.ds(lot, 1)].rearrange("o p n -> (o p) n")
                sp.dma_start(row, early[:, k, :]).then_inc(early_out[k], 16)

            def store_early_pairs(first, end):
                with sp.Fori(first, end, 1) as i:
                    for k in range(2):
                        store_early(i, k)
                    for k in range(2):
                        sp.wait_ge(early_out[k], i * 16 + 16)
                        sp.sem_inc(early_free, 1)

            store_early_pairs(0, EARLY_PAIRS)
            sort_io(1)
            store_early_pairs(EARLY_PAIRS, NDB // 2)
            store_early(NDB // 2, 0)
            sp.wait_ge(early_out[0], (NDB // 2 + 1) * 16)
            sp.sem_inc(early_free, 1)
            def pass_io(mask_row, chunks_before):
                def load(c, k):
                    cols = mask_row[bass.ds(c * (TILES * P), TILES * P)]
                    sp.dma_start(msk[k], cols.partition_broadcast(CH)).then_inc(msk_in[k], 16)
                load(0, 0)
                load(1, 1)
                rows = d_rows.rearrange("(c p k) d -> c p (k d)", p=P, k=TILES)
                with sp.Fori(0, NCH // 2, 1) as i:
                    for k in range(2):
                        c = i * 2 + k
                        g = (chunks_before + c) * GROUPS
                        sp.wait_ge(scan_done, g + (CREDIT + GROUPS))
                        load(c + 2, k)
                        if k == 1:
                            sp.wait_ge(outd[0], (chunks_before + c + 1) * 8)
                            sp.sem_inc(out_free, 1)
                        sp.wait_ge(out_copied, g + (CREDIT + GROUPS))
                        sp.dma_start(rows[bass.ds(c, 1)].rearrange("o p n -> (o p) n"), outr[:, k, :]).then_inc(outd[k], 16)
                    sp.wait_ge(outd[1], (i * 2 + (chunks_before + 2)) * 8)
                    sp.sem_inc(out_free, 1)
                landed = (chunks_before + NCH) * 8 + (chunks_before + NCH) // NCH * 16
                if isinstance(landed, int):
                    sp.wait_ge(msk_in[0], landed)
                    sp.wait_ge(msk_in[1], landed)
                else:
                    hold(sp, (msk_in[0], landed), (msk_in[1], landed))

            sp.sem_inc(out_free, CREDIT)
            sp.sem_inc(count_free, CREDIT)
            sp.wait_ge(firsts_in, 16)
            sp.wait_ge(flag_ready, 1)
            sp.wait_ge(order_done, 2)
            general = sp.value_load(flag[0:1, 0:1])
            with sp.If(general > 0):
                pass_io(d_pen[0, :], 0)
            with sp.Else():
                rows = d_rows.rearrange("(c p k) d -> c p (k d)", p=P, k=TILES)

                def load(c, k):
                    edges = bass.ds(c * (TILES * P), TILES * P)
                    first = sp.value_load(firsts[:, bass.ds(c, 1)], min_val=0, max_val=WINDOW_END)
                    sp.dma_start(msk[k], d_pen[0, edges].partition_broadcast(CH)).then_inc(msk_in[k], 16)
                    sp.dma_start(loc[k], d_local[0, edges].partition_broadcast(P)).then_inc(win_in[k], 16)
                    sp.dma_start(window[k], d_a[bass.ds(first, P), :]).then_inc(win_in[k], 16)

                load(0, 0)
                load(1, 1)
                with sp.Fori(0, NDB, 1) as d:
                    stored_lots = 0
                    for n in range(FUSED):
                        c, k = d * FUSED + n, n % 2
                        g = c * GROUPS
                        sp.wait_ge(t_ready, g + (CREDIT + GROUPS))
                        sp.wait_ge(scan_done, g + (CREDIT + GROUPS))
                        load(c + 2, k)
                        if n == FUSED - 3:
                            row = d_early[bass.ds(d, 1)].rearrange("o p n -> (o p) n")
                            sp.dma_start(rows_b[:, k, :, :].rearrange("p t d -> p (t d)"), row).then_inc(early_back, 16)
                        if n:
                            sp.wait_ge(outd[1 - k], d * (FUSED * 8) + (n + 1) // 2 * 16)
                            sp.sem_inc(out_free, 1)
                        hold(sp, (out_copied, g + (CREDIT + GROUPS)))
                        sp.dma_start(rows[bass.ds(c, 1)].rearrange("o p n -> (o p) n"), outr[:, k, :]).then_inc(outd[k], 16)
                        for lot in range(stored_lots, share((n + 1) * GROUPS + 1).stop // 7):
                            hold(sp, (count_copied, d * BPAIRS + (lot * 7 + 7 + CREDIT)))
                            half = SRC_GROUP * DB // 2
                            sp.dma_start(d_count[bass.ds(d, 1), :, lot * half:(lot + 1) * half].rearrange("o p n -> (o p) n"),
                                         ctile_out[:, lot, :]).then_inc(c_out[lot], 16)
                            if lot:
                                sp.wait_ge(c_out[lot - 1], d * 16 + 16)
                                sp.sem_inc(count_free, 1)
                            stored_lots = lot + 1
                    sp.wait_ge(outd[1], d * (FUSED * 8) + FUSED * 8)
                    sp.sem_inc(out_free, 1)
                    sp.wait_ge(c_out[6], d * 16 + 16)
                    sp.sem_inc(count_free, 1)
                for k in range(2):
                    sp.wait_ge(msk_in[k], NCH * 8 + 16)
                    sp.wait_ge(win_in[k], NCH * 16 + 32)
            with sp.If(general > 0):
                sp.wait_ge(ex_free, 1)
                load_edges()
                sort_io(2)
                with sp.Fori(0, 3, 1) as r:
                    sp.wait_ge(h_ready, r + 1)
                    sp.dma_start(d_h.rearrange("(c p) d -> p c d", p=P),
                                 HP[:, :].rearrange("p (c d) -> p c d", d=CH)).then_inc(h_out, 16)
                    pass_io(d_keep[0, :], (r + 1) * NCH)
            with sp.Else():
                sp.wait_ge(degrees_done, 1)
                NP = len(PARTS)
                with sp.Fori(0, 3, 1) as r, sp.Fori(0, NDB // SB, 1) as nb:
                    n = r * SB + nb
                    for a, width in enumerate(PARTS):
                        s0 = sum(PARTS[:a])
                        sp.wait_ge(ct_used, n * NP + (a - 2 + CREDIT))
                        row = d_count[bass.ds(nb * SB, SB), :, s0 * DB // 2:(s0 + width) * DB // 2]
                        sp.dma_start(ct_load[a % 3][:, 0:SB * width * DB // 2].rearrange("p (d n) -> p d n", d=SB),
                                     row.rearrange("d p n -> p d n")).then_inc(ct_in[a % 3], 16)
            sp.wait_ge(stored, 32)

        @block.gpsimd
        def _(pool):
            pool.wait_ge(cleared, 1)
            nc.gpsimd.iota(pcol[:], [[0, 1]], base=0, channel_multiplier=1).then_inc(made, 1)
            nc.gpsimd.iota(qi[:], [[P, NBLK]], base=0, channel_multiplier=1).then_inc(made, 1)
            nc.gpsimd.iota(qbi[:], [[P, BCOLS]], base=0, channel_multiplier=1).then_inc(made, 1)
            nc.gpsimd.iota(iota_i[:], [[1, DB]], base=0, channel_multiplier=0).then_inc(made, 1)
            for t, base, step in ((ident, 0, -1), (shift, 1, -1)):
                nc.gpsimd.affine_select(out=t[:], in_=t[:], compare_op=ALU.not_equal, fill=1.0, base=base,
                                        pattern=[[step, P]], channel_multiplier=1).then_inc(made, 1)
            nc.gpsimd.affine_select(out=wrap[:], in_=wrap[:], compare_op=ALU.not_equal, fill=1.0, base=-(P - 1),
                                    pattern=[[P, P]], channel_multiplier=1).then_inc(made, 1)
            for half, fill in ((0, 1.0), (1, 1.0 / SPLIT)):
                pool.wait_ge(made, 7 + half)
                nc.gpsimd.affine_select(out=join[:], in_=join[:], compare_op=ALU.not_equal, fill=fill, base=-half * CH,
                                        pattern=[[-1, CH]], channel_multiplier=1).then_inc(made, 1)

            def gather(dst, table, index, signal):
                nc.gpsimd.indirect_dma_start(dst, None, table, bass.IndirectOffsetOnAxis(ap=index, axis=0)).then_inc(signal, 16)

            def sub_head_rows(k):
                pool.wait_ge(rows1_chosen, k + 1)
                pool.wait_ge(keys_out, k * 64 + 64)
                for c in range(QCOLS[k]):
                    gather(HP[:, c * CH:(c + 1) * CH], d_sub, i1[:, c:c + 1], g_sub)

            def key_row_rows(k):
                pool.wait_ge(rows2_chosen, k + 1)
                for c in range(QCOLS[k]):
                    gather(HP[:, c * CH:(c + 1) * CH], d_keys, i2[:, c:c + 1], g_key)

            def search_rows(k):
                sub_head_rows(k)
                key_row_rows(k)

            pool.wait_ge(t_stored, 32 * STEPS)
            sub_head_rows(0)
            def gather_early(i, k):
                lot = i * 2 + k
                pool.wait_ge(early_free, lot + (CREDIT - 1))
                cols = bass.ds(lot * (FUSED * TILES) + (FUSED - 1) * TILES, TILES)
                nc.gpsimd.tensor_copy(stg[:, k, 0:TILES], idx_lo[:, cols]).then_inc(early_staged, 1)
                hold(pool, (early_staged, lot + 1))
                for t in range(TILES):
                    gather(early[:, k, t * HID:(t + 1) * HID], d_b, stg[:, k, t:t + 1], early_in[k])

            pool.wait_ge(masks_out, 48)
            BEFORE = 2
            with pool.Fori(0, BEFORE, 1) as i:
                for k in range(2):
                    gather_early(i, k)
            key_row_rows(0)
            with pool.Fori(BEFORE, EARLY_PAIRS, 1) as i:
                for k in range(2):
                    gather_early(i, k)
            sub_head_rows(1)
            gather_early(EARLY_PAIRS, 0)
            key_row_rows(1)
            gather_early(EARLY_PAIRS, 1)
            key_rows = d_keys.rearrange("(a t) b -> a (t b)", t=2)
            for h in range(2):
                pool.wait_ge(starts_ready, h + 1)
                for c in range(BCOLS // 2):
                    for n, index in enumerate((i1, i2)):
                        o = c * 2 * P + n * P
                        gather(EX[:, o:o + P], key_rows, index[:, h * BCOLS // 2 + c:h * BCOLS // 2 + c + 1], g_pairs)
                if h == 0:
                    for k in range(2):
                        gather_early(EARLY_PAIRS + 1, k)
            gather_early(NDB // 2, 0)
            pool.wait_ge(cols_made, 1)
            nc.gpsimd.iota(EX[:, 0:BCOLS * P].bitcast(i32), [[1, BCOLS * P]], base=REAL >> 15,
                           channel_multiplier=0).then_inc(cols_made, 1)

            def pass_gather(chunks_before, lots, width, per):
                with pool.Fori(0, NCH // 2, 1) as i:
                    for k in range(2):
                        c = i * 2 + k
                        used = t_ready if lots == 2 else m_ready
                        pool.wait_ge(used, (chunks_before + c) * GROUPS + (CREDIT - GROUPS))
                        for n in range(lots):
                            lst = (idx_lo[:, bass.ds(c * TILES, TILES)], idx_hi[:, bass.ds(c * TILES, TILES)])[n] \
                                if lots == 2 else idx_lo[:, bass.ds(c * TILES, TILES)]
                            nc.gpsimd.tensor_copy(stg[:, k, n * TILES:(n + 1) * TILES], lst).then_inc(staged_idx, 1)
                        hold(pool, (staged_idx, c * lots + (lots if lots == 2 else per)))
                        for t in range(TILES):
                            for n in range(lots):
                                at = (k * lots + n) * TILES * width + t * width
                                gather(arena[:, at:at + width], ((d_b, d_a)[n] if lots == 2 else d_h),
                                       stg[:, k, n * TILES + t:n * TILES + t + 1],
                                       (gath if lots == 2 else gath_cv)[k][t // HALF])

            def ends(passes):
                stored_rows = passes * NCH + CREDIT
                if isinstance(stored_rows, int):
                    pool.wait_ge(out_free, stored_rows)
                else:
                    hold(pool, (out_free, stored_rows))
                for c in range(NBLK):
                    gather(EX[:, c * CH:(c + 1) * CH], d_rows, endr[:, c:c + 1], g_end)

            pool.wait_ge(order_done, 2)
            pool.wait_ge(flag_ready, 1)
            general = pool.value_load(flag[0:1, 0:1])
            with pool.If(general > 0):
                pass_gather(0, 2, HID, 0)
            with pool.Else():
                with pool.Fori(0, NDB, 1) as d:
                    for n in range(FUSED - 1):
                        c, k = d * FUSED + n, n % 2
                        for h in range(2):
                            pool.wait_ge(t_ready, c * GROUPS + (CREDIT - 2 * GROUPS + (h + 1) * GROUPS // 2))
                            tiles = slice(h * HALF, (h + 1) * HALF)
                            nc.gpsimd.tensor_copy(stg[:, k, tiles], idx_lo[:, bass.ds(c * TILES + h * HALF, HALF)]
                                                  ).then_inc(staged_idx, 1)
                            hold(pool, (staged_idx, d * (2 * (FUSED - 1)) + (2 * n + h + 1)))
                            for t in range(h * HALF, (h + 1) * HALF):
                                gather(rows_b[:, k, t, :], d_b, stg[:, k, t:t + 1], gath[k][h])
            ends(1)
            with pool.If(general > 0):
                search_rows(2)
                pool.wait_ge(order_done, 3)
                with pool.Fori(0, 3, 1) as r:
                    hold(pool, (h_out, r * 16 + 16))
                    pass_gather((r + 1) * NCH, 1, CH, r * NCH + (2 * NCH + 1))
                    ends(r + 2)
            with pool.Else():
                pool.wait_ge(flag_ready, 1)

        @block.scalar
        def _(act):
            act.wait_ge(ld_x, 32)
            nA = 2 * PPI * HID
            with act.Fori(0, STEPS, 1) as k:
                nc.scalar.copy(stage[:], X[:, bass.ds(k * (PPI * P), PPI * P)]).then_inc(staged, 1)
                act.wait_ge(t_turned, k + 1)
                nc.scalar.copy(stageT[:], psf[:, 0:PPI * P]).then_inc(t_evac, 1)
                for h in range(2):
                    act.wait_ge(t_proj, k * 2 + (h + 1))
                    nc.scalar.copy(HP[:, h * nA:(h + 1) * nA], psf[:, h * 2048:h * 2048 + nA]).then_inc(t_copied, 1)
                act.wait_ge(t_stored, k * 32 + 32)
            def odd_banks(k):
                for n in range(NTURN + (k != 1)):
                    for b in range(1, 8, 2):
                        act.wait_ge(turned, 8 * (TURNS[k] + n) + b + 1)
                        if n < NTURN:
                            dst_cols = keyb[1 - turn_from[n]][:, b * 512:(b + 1) * 512]
                            nc.scalar.copy(dst_cols, ps[:, b, :]).then_inc(odd_copied, 1)
                        else:
                            dst_cols = by_tile[:, :, 4 * b:4 * b + 4]
                            nc.scalar.copy(dst_cols, ps[:, b, :].rearrange("p (j q) -> p q j", j=4)).then_inc(odd_copied, 1)

            odd_banks(0)
            odd_banks(1)
            for h in range(2):
                act.wait_ge(b_turned, h + 1)
                half = BCOLS // 2 * P
                nc.scalar.copy(arena[:, h * half:(h + 1) * half], psf[:, 0:half]).then_inc(b_copied, 1)
            def copy_rows(c, k, g, before, bank):
                G = (before + c) * GROUPS + g
                act.wait_ge(o_ready, G + (CREDIT + 1))
                if g == 0:
                    act.wait_ge(out_free, before + c + (CREDIT - 1))
                nc.scalar.copy(outr[:, k, g * 4 * CH:(g + 1) * 4 * CH], ps[:, bank, 0:4 * CH]).then_inc(out_copied, 1)

            act.sem_inc(relu_done, CREDIT)
            act.sem_inc(out_copied, CREDIT)
            act.sem_inc(count_copied, CREDIT)

            def relu(c, g):
                G = c * GROUPS + g
                act.wait_ge(t_ready, G + (CREDIT + 1))
                act.wait_ge(m_ready, G + (CREDIT - 1))
                nc.scalar.activation(R[:, g % 2, :], ps[:, g % 2, :], ACT.Relu).then_inc(relu_done, 1)

            def copy_counts(d, pairs):
                for m in pairs:
                    if m % 7 == 0:
                        act.wait_ge(count_free, d * 7 + (m // 7 + 1 + CREDIT - 7))
                    hold(act, (count_ready, d * BPAIRS + (m + 1 + CREDIT)))
                    nc.scalar.copy(ctile[:, m // 7, m % 7 * 512:(m % 7 + 1) * 512], ps[:, 5 + m % 2, :],
                                   saturate=False).then_inc(count_copied, 1)

            act.wait_ge(b_ready, 1)
            act.wait_ge(flag_ready, 1)
            general = act.value_load(flag[0:1, 0:1])
            with act.If(general > 0):
                with act.Fori(0, NCH // 2, 1) as i:
                    for k in range(2):
                        for g in range(GROUPS + 2):
                            if g < GROUPS:
                                relu(i * 2 + k, g)
                            if g >= 2:
                                copy_rows(i * 2 + k, k, g - 2, 0, 4 + g % 2)
            with act.Else():
                with act.Fori(0, NDB, 1) as d:
                    for f in range(PHASES):
                        if f < FGROUPS:
                            n, k, g = place(f)
                            relu(d * FUSED + n, g)
                        copy_counts(d, share(f)[0:2])
                        if f >= 2:
                            n, k, g = place(f - 2)
                            copy_rows(d * FUSED + n, k, g, 0, 4)
                        copy_counts(d, share(f)[2:])
            act.wait_ge(var_ready, 1)
            nc.scalar.activation(sd[:], mu[:], ACT.Sqrt).then_inc(rooted, 1)

            def copy_turned(r):
                with act.Fori(0, STEPS, 1) as k:
                    act.wait_ge(t_turned, r * STEPS + k + (STEPS + 1))
                    nc.scalar.copy(stageT[:], psf[:, 0:PPI * P]).then_inc(t_evac, 1)

            with act.If(general > 0):
                odd_banks(2)
                act.wait_ge(deg_ready, 1)
                nc.scalar.activation(dinv[:], e_deg[:], ACT.Sqrt).then_inc(rooted, 1)
                with act.Fori(0, 3, 1) as r:
                    copy_turned(r)
                    with act.Fori(0, NCH // 2, 1) as i:
                        for k in range(2):
                            for g in range(GROUPS):
                                copy_rows(i * 2 + k, k, g, (r + 1) * NCH, 4 + g % 2)
            with act.Else():
                act.wait_ge(deg_ready, 1)
                nc.scalar.activation(dinv[:], e_deg[:], ACT.Sqrt).then_inc(rooted, 1)
                def copy_sums(r, n):
                    act.wait_ge(acc_ready, r * SB + n + 1)
                    nc.scalar.copy(sums, psf[:, 0:SB * DB]).then_inc(acc_copied, 1)

                def copy_turned_next(r, n):
                    act.wait_ge(t_turned, r * STEPS + n + (2 * STEPS + 1))
                    nc.scalar.copy(stageT[:], psf[:, 3072:3072 + PPI * P]).then_inc(t_evac, 1)

                copy_turned(0)
                with act.Fori(0, 2, 1) as r:
                    copy_sums(r, 0)
                    with act.Fori(1, NDB // SB, 1) as n:
                        copy_turned_next(r, n - 1)
                        copy_sums(r, n)
                    copy_turned_next(r, NDB // SB - 1)
                with act.Fori(0, NDB // SB, 1) as n:
                    copy_sums(2, n)
            act.wait_ge(shifted_down, 1)
            nc.scalar.activation(TMP, EX[:], ACT.Exp).then_inc(exped, 1)
            act.wait_ge(sum_ready, 1)
            nc.scalar.activation(mu[:], sd[:], ACT.Ln).then_inc(logged, 1)
            act.wait_ge(var_ready, 2)
            nc.scalar.activation(sd[:], mu[:], ACT.Sqrt).then_inc(rooted, 1)
            act.wait_ge(out_ready, 1)
            act.dma_start(out[0:(NBLK - 1) * P, :].rearrange("(c p) d -> p c d", p=P),
                          X[:, 0:(NBLK - 1) * CH].rearrange("p (c d) -> p c d", d=CH)).then_inc(stored, 16)
            act.dma_start(out[(NBLK - 1) * P:, :], X[0:LAST, (NBLK - 1) * CH:NC]).then_inc(stored, 16)
            act.wait_ge(stored, 32)

        @block.tensor
        def _(pe):
            pe.wait_ge(made, 9)
            pe.wait_ge(setup_done, 1)
            nA = 2 * PPI * HID
            with pe.Fori(0, STEPS, 1) as k:
                pe.wait_ge(staged, k + 1)
                for j in range(PPI):
                    last = nc.tensor.transpose(psf[:, j * P:(j + 1) * P], stage[:, j * P:(j + 1) * P], ident[:])
                last.then_inc(t_turned, 1)
                pe.wait_ge(t_evac, k + 1)
                for h in range(2):
                    for j in range(PPI):
                        o = psf[:, h * 2048 + j * 2 * P:h * 2048 + (j + 1) * 2 * P]
                        nc.tensor.matmul(o, ones1[:], b1r[:, h * 2 * P:(h + 1) * 2 * P], start=True, stop=False)
                        last = nc.tensor.matmul(o, stageT[:, j * P:(j + 1) * P], w_ab[:, h * 2 * P:(h + 1) * 2 * P],
                                                start=False, stop=True)
                    last.then_inc(t_proj, 1)
            pe.wait_ge(t_copied, 2 * STEPS)
            def turns(k):
                for n in range(NTURN + (k != 1)):
                    pe.wait_ge(turn_in, TURNS[k] + n + 1)
                    from_buf = keyb[turn_from[n] if n < NTURN else KEY_BUF]
                    for b in range(8):
                        for j in range(4):
                            f = 4 * b + j
                            last = nc.tensor.transpose(ps[:, b, j * P:(j + 1) * P], from_buf[:, f * P:(f + 1) * P], ident[:])
                        last.then_inc(turned, 1)
                pe.wait_ge(counts_ready, k + 1)
                n = QCOLS[k]
                nc.tensor.matmul(ps[:, 0, 0:n], shift[:], cle[:, 1:n + 1], start=True, stop=False)
                nc.tensor.matmul(ps[:, 0, 0:n], wrap[:], cle[:, 0:n], start=False, stop=True).then_inc(shifted, 1)

            turns(0)
            turns(1)
            pe.wait_ge(flag_in, 1)
            nc.tensor.matmul(ps[0:1, 1, 0:1], fl[:, 2:3], ones_c[:], start=True, stop=True).then_inc(flag_in, 1)
            for h in range(2):
                pe.wait_ge(b_shifted, h + 1)
                if h:
                    pe.wait_ge(b_copied, h)
                for c in range(BCOLS // 2):
                    last = nc.tensor.transpose(psf[:, c * P:(c + 1) * P], HP[:, c * 2 * P:c * 2 * P + P], ident[:])
                last.then_inc(b_turned, 1)
            pe.wait_ge(order_done, 2)
            pe.sem_inc(count_ready, CREDIT)
            pe.sem_inc(t_ready, CREDIT)
            pe.sem_inc(m_ready, CREDIT)
            pe.sem_inc(o_ready, CREDIT)

            def second_product(c, g):
                G = c * GROUPS + g
                pe.wait_ge(relu_done, G + (CREDIT + 1))
                pe.wait_ge(scan_done, G + (CREDIT - 1))
                nc.tensor.matmul(ps[0:CH, 2 + g % 2, :], w2s[:], R[:, g % 2, :], start=True, stop=True).then_inc(m_ready, 1)

            def rows_back(c, g, before, bank, banks):
                G = (before + c) * GROUPS + g
                hold(pe, (scan_done, G + (CREDIT + 1)), (out_copied, G + (CREDIT + 1 - banks)))
                for t in range(4):
                    last = nc.tensor.transpose(ps[:, bank, t * CH:(t + 1) * CH], S[:, g % 2, t * P:(t + 1) * P],
                                               ident[0:CH, 0:CH])
                last.then_inc(o_ready, 1)

            def count(d, pairs):
                for m in pairs:
                    pe.wait_ge(hot_ready, d * BPAIRS + (m + 1))
                    hold(pe, (count_copied, d * BPAIRS + (CREDIT + max(m - 1, 0))))
                    for u in range(2):
                        for half in range(2):
                            nc.tensor.matmul(ps[:, 7, bass.ds(d * 2 + half, 1)],
                                             one_d[:, m % 7, u, half * P:(half + 1) * P],
                                             ones_b[:], start=False, stop=False)
                        last = nc.tensor.matmul(ps[:, 5 + m % 2, u * DB:(u + 1) * DB], one_s[:, m % 7, u, :],
                                                one_d[:, m % 7, u, :], start=True, stop=True)
                    last.then_inc(count_ready, 1)

            pe.wait_ge(flag_ready, 1)
            general = pe.value_load(flag[0:1, 0:1])
            with pe.If(general > 0):
                with pe.Fori(0, NCH // 2, 1) as i:
                    for k in range(2):
                        c = i * 2 + k
                        for g in range(GROUPS + 2):
                            if g in (0, GROUPS // 2):
                                pe.wait_ge(gath[k][g * 2 // GROUPS], i * (32 * HALF) + 32 * HALF)
                            if g < GROUPS:
                                pe.wait_ge(relu_done, c * GROUPS + (g + CREDIT - 1))
                                for t in range(4):
                                    o = ps[:, g % 2, t * P:(t + 1) * P]
                                    for n in range(2):
                                        a = (k * 2 + n) * TILES * HID + (4 * g + t) * HID
                                        last = nc.tensor.matmul(o, arena[:, a:a + HID], ident[:], start=n == 0, stop=n == 1)
                                last.then_inc(t_ready, 1)
                            if 0 <= g - 1 < GROUPS:
                                second_product(c, g - 1)
                            if g >= 2:
                                rows_back(c, g - 2, 0, 4 + g % 2, 2)
            with pe.Else():
                nc.tensor.matmul(ps[:, 7, 0:NBLK], zrow[:], orow[:, 0:NBLK], start=True, stop=False)
                with pe.Fori(0, NDB, 1) as d:
                    for f in range(PHASES):
                        if f < FGROUPS:
                            n, k, g = place(f)
                            G = d * FGROUPS + f
                            pe.wait_ge(relu_done, G + (CREDIT - 1))
                            if g == 0:
                                pe.wait_ge(win_in[k], d * (FUSED * 16) + (n // 2 + 1) * 32)
                            if n < FUSED - 1 and g in (0, GROUPS // 2):
                                hold(pe, (gath[k][g * 2 // GROUPS], d * ((2 - k) * 16 * HALF) + (n // 2 + 1) * 16 * HALF))
                            elif g == 0:
                                hold(pe, (early_back, d * 16 + 16))
                            for t in range(4):
                                nc.tensor.matmul(ps[:, g % 2, t * P:(t + 1) * P], rows_b[:, k, 4 * g + t, :],
                                                 ident[:], start=t == 0, stop=False, is_transpose=True)
                            hold(pe, (one_a_ready, G + 1))
                            nc.tensor.matmul(ps[:, g % 2, :], window[k], one_a[g % 2],
                                             start=False, stop=True).then_inc(t_ready, 1)
                        count(d, share(f)[0:1])
                        if 0 <= f - 1 < FGROUPS:
                            n, k, g = place(f - 1)
                            second_product(d * FUSED + n, g)
                        count(d, share(f)[1:2])
                        if f >= 2:
                            n, k, g = place(f - 2)
                            rows_back(d * FUSED + n, g, 0, 4, 1)
                        count(d, share(f)[2:])
                nc.tensor.matmul(ps[:, 7, 0:NBLK], zrow[:], orow[:, 0:NBLK], start=False, stop=True).then_inc(deg_summed, 1)

            pe.wait_ge(ld_cw, 144)

            def project(r):
                with pe.Fori(0, STEPS, 1) as k:
                    pe.wait_ge(h_staged, r * STEPS + k + 1)
                    for j in range(PPI):
                        last = nc.tensor.transpose(psf[:, j * P:(j + 1) * P], stage[:, j * P:(j + 1) * P], ident[:])
                    last.then_inc(t_turned, 1)
                    pe.wait_ge(t_evac, r * STEPS + k + (STEPS + 1))
                    for j in range(PPI):
                        last = nc.tensor.matmul(psf[:, 1024 + j * P:1024 + (j + 1) * P], stageT[:, j * P:(j + 1) * P],
                                                w_cv[:, bass.ds(r * P, P)], start=True, stop=True)
                    last.then_inc(t_proj, 1)

            with pe.If(general > 0):
                turns(2)
                pe.wait_ge(order_done, 3)
                with pe.Fori(0, 3, 1) as r:
                    project(r)
                    with pe.Fori(0, NCH // 2, 1) as i:
                        for k in range(2):
                            c = i * 2 + k
                            for g in range(GROUPS + 1):
                                if g in (0, GROUPS // 2):
                                    pe.wait_ge(gath_cv[k][g * 2 // GROUPS], (r * (NCH // 2) + i) * (16 * HALF) + 16 * HALF)
                                if g < GROUPS:
                                    G = ((r + 1) * NCH + c) * GROUPS + g
                                    hold(pe, (scan_done, G + (CREDIT - 1)))
                                    for t in range(4):
                                        a = k * TILES * CH + (4 * g + t) * CH
                                        last = nc.tensor.transpose(ps[0:CH, 2 + g % 2, t * P:(t + 1) * P],
                                                                   arena[:, a:a + CH], ident[:])
                                    last.then_inc(m_ready, 1)
                                if g >= 1:
                                    rows_back(c, g - 1, (r + 1) * NCH, 4 + (g - 1) % 2, 2)
            with pe.Else():
                pe.sem_inc(ct_used, CREDIT)
                BANKS = [(b * 512, min(512, SB * DB - b * 512)) for b in range(-(-SB * DB // 512))]

                def spread_top(r):
                    pe.wait_ge(top_ready, r + 1)
                    nc.tensor.transpose(ps[0:1, 4, 0:P], top[:], ident[:]).then_inc(top_row, 1)
                    pe.wait_ge(top_one, r + 1)
                    nc.tensor.matmul(ps[:, 4, 0:1], ones1[:], one1[:], start=True, stop=True).then_inc(top_all, 1)
                    hold(pe, (parts_ready, r + 1))

                def turn_next(r, n):
                    hold(pe, (h_staged, r * STEPS + n + (STEPS + 1)))
                    for j in range(PPI):
                        last = nc.tensor.transpose(psf[:, 3072 + j * P:3072 + (j + 1) * P], stage[:, j * P:(j + 1) * P],
                                                   ident[:])
                    last.then_inc(t_turned, 1)

                def project_next(r, n):
                    hold(pe, (t_evac, r * STEPS + n + (2 * STEPS + 1)))
                    for j in range(PPI):
                        last = nc.tensor.matmul(psf[:, 3072 + j * P:3072 + (j + 1) * P], stageT[:, j * P:(j + 1) * P],
                                                w_cv[:, bass.ds(r * P + P, P)], start=True, stop=True)
                    last.then_inc(t_proj, 1)

                def sum_block(r, n, also):
                    m = r * SB + n
                    for b, (c0, width) in enumerate(BANKS):
                        nc.tensor.matmul(ps[:, b, 0:width], zrow[:], orow[:, 0:width], start=True, stop=False)
                    for a, lot in enumerate(PARTS):
                        if also and a == 3:
                            turn_next(r, n - 1)
                        if also and a == 6:
                            project_next(r, n - 1)
                        counts_here = m * (16 * len(PARTS) // 3) + 16 * (a // 3 + 1)
                        if isinstance(m, int):
                            pe.wait_ge(ct_in[a % 3], counts_here)
                        else:
                            hold(pe, (ct_in[a % 3], counts_here))
                        cv = ct[a % 3][:, 0:SB * lot * DB].rearrange("p (d n) -> p d n", d=SB)
                        for s0 in range(lot):
                            for b, (c0, width) in enumerate(BANKS):
                                dsts = cv[:, c0 // DB:(c0 + width) // DB, s0 * DB:(s0 + 1) * DB]
                                last = nc.tensor.matmul(ps[:, b, 0:width].rearrange("p (d n) -> p d n", n=DB),
                                                        parts[:, sum(PARTS[:a]) + s0, :], dsts, start=False, stop=False)
                        last.then_inc(ct_used, 1)
                    for b, (c0, width) in enumerate(BANKS):
                        last = nc.tensor.matmul(ps[:, b, 0:width], zrow[:], orow[:, 0:width], start=False, stop=True)
                    last.then_inc(acc_ready, 1)
                    pe.wait_ge(acc_copied, m + 1)
                    hold(pe, (sb_done, m + CREDIT))
                    for c in range(SB * DB // P):
                        last = nc.tensor.matmul(psf[:, 2048 + c * CH:2048 + (c + 1) * CH], sums[:, c * P:(c + 1) * P],
                                                join[:], start=True, stop=True)
                    last.then_inc(joined, 1)

                project(0)
                with pe.Fori(0, 2, 1) as r:
                    spread_top(r)
                    sum_block(r, 0, False)
                    with pe.Fori(1, NDB // SB, 1) as n:
                        sum_block(r, n, True)
                    turn_next(r, NDB // SB - 1)
                    project_next(r, NDB // SB - 1)
                spread_top(2)
                with pe.Fori(0, NDB // SB, 1) as n:
                    sum_block(2, n, False)

        @block.vector
        def _(dve):
            def bc_in(t, n=CH):
                return t[:, :, None].to_broadcast([P, NBLK, n])

            def bc_out(t):
                return t[:, None, :].to_broadcast([P, NBLK, CH])

            def nodes(t):
                return t[:, :].rearrange("p (c d) -> p c d", d=CH)

            for t in (X[:, (NBLK - 1) * CH:NC], w_ab[:], w_cv[:], b1r[:], ident[:], shift[:], wrap[:], cle[:],
                      prevk[:], S[:], join[:], zrow[:], fl[:]):
                nc.vector.memset(t, 0.0)
            for t in (orow, ones_b, ones_c):
                nc.vector.memset(t[:], 1.0)
            nc.vector.memset(ones1[:], 1.0).then_inc(cleared, 1)
            nc.vector.memset(low_cv[:], -2.0 * BIG)
            nc.vector.memset(sgn[:], 1.0)
            dve.drain()
            nc.vector.memset(low_cv[:, 1:2], 0.0)
            dve.wait_ge(made, 9)
            nc.vector.tensor_scalar(qi[:], qi[:], NODE_BITS, REAL | LOW, ALU.logical_shift_left, ALU.bitwise_or)
            nc.vector.tensor_scalar(qbi[:], qbi[:], 15, REAL, ALU.logical_shift_left, ALU.bitwise_or)
            nc.vector.tensor_copy(iota_r[:], iota_i[:])
            nc.vector.tensor_copy(pcolf[:], pcol[:])
            for j in range(SIGNS - 1):
                nc.vector.tensor_scalar(bit[:, j:j + 1], pcol[:], j, 1, ALU.logical_shift_right, ALU.bitwise_and)
            dve.drain()
            nc.vector.tensor_scalar(sgn[:, 0:SIGNS - 1], bit[:, 0:SIGNS - 1], -2.0, 1.0, ALU.mult, ALU.add)
            dve.drain()
            nc.vector.tensor_copy(flip[:, 0:1], sgn[:, 0:1])
            nc.vector.tensor_tensor(flip[:, 1:SIGNS], sgn[:, 0:SIGNS - 1], sgn[:, 1:SIGNS], ALU.mult)
            dve.wait_ge(ld_w, 128)
            for h in range(2):
                hs = slice(h * CH, (h + 1) * CH)
                nc.vector.tensor_copy(w_ab[hs, (2 + h) * P:(3 + h) * P], w1b[hs, :])
                last = nc.vector.tensor_tensor(w_ab[hs, h * P:(h + 1) * P], w_ab[hs, h * P:(h + 1) * P], w1b[hs, :],
                                               ALU.subtract)
            last.then_inc(setup_done, 1)

            def in_use(kind, L):
                unit = 2 << L
                return min(W, -(-NE // unit) * unit) if kind == "both" else W

            def network_step(kind, L, d, a, b):
                if kind == "flip":
                    return nc.vector.tensor_scalar(b, a, flip[:, L - LOGW:L - LOGW + 1], None, ALU.mult)
                if kind == "up":
                    av, bv = (t.rearrange("p (m h d) -> p m h d", h=2, d=d) for t in (a, b))
                    nc.vector.tensor_tensor(bv[:, :, 0, :], av[:, :, 0, :], av[:, :, 1, :], ALU.min)
                    return nc.vector.tensor_tensor(bv[:, :, 1, :], av[:, :, 0, :], av[:, :, 1, :], ALU.max)
                av, bv = (t[:, 0:in_use(kind, L)].rearrange("p (n r m h d) -> p n r m h d", r=2, h=2, d=d, m=(1 << L) // (2 * d)) for t in (a, b))
                for way in range(2):
                    lo, hi = av[:, :, way, :, 0, :], av[:, :, way, :, 1, :]
                    nc.vector.tensor_tensor(bv[:, :, way, :, way, :], lo, hi, ALU.min)
                    last = nc.vector.tensor_tensor(bv[:, :, way, :, 1 - way, :], lo, hi, ALU.max)
                return last

            kb_i = [t.bitcast(i32) for t in keyb]
            e_src, e_dst = (EX[:, n * NE:(n + 1) * NE].bitcast(i32) for n in range(2))

            def pair_keys(k, upper, lower):
                key = kb_i[0]
                nc.vector.memset(key[:, NE:], PAD)
                nc.vector.memset(kb_i[1][:, NE:], PAD)
                dve.wait_ge(ld_e, k * 32 + 32)
                nc.vector.tensor_scalar(key[:, 0:NE], upper, NODE_BITS, REAL, ALU.logical_shift_left, ALU.bitwise_or)
                dve.drain()
                nc.vector.tensor_tensor(key[:, 0:NE], key[:, 0:NE], lower, ALU.bitwise_or)
                dve.drain()

            def bucket_keys():
                key, tmp = kb_i[0], kb_i[1]
                nc.vector.memset(key[:, NE:], PAD)
                nc.vector.memset(tmp[:, NE:], PAD)
                dve.wait_ge(ld_e, 64)
                nc.vector.tensor_scalar(key[:, 0:NE], e_dst, 8, None, ALU.logical_shift_right)
                nc.vector.tensor_scalar(tmp[:, 0:NE], e_src, 7, None, ALU.logical_shift_right)
                dve.drain()
                nc.vector.scalar_tensor_tensor(key[:, 0:NE], key[:, 0:NE], float(NBLK), tmp[:, 0:NE], ALU.mult, ALU.add)
                dve.drain()
                nc.vector.tensor_scalar(key[:, 0:NE], key[:, 0:NE], 15, REAL, ALU.logical_shift_left, ALU.bitwise_or)
                nc.vector.tensor_scalar(tmp[:, 0:NE], e_src, P - 1, 8, ALU.bitwise_and, ALU.logical_shift_left)
                dve.drain()
                nc.vector.tensor_tensor(key[:, 0:NE], key[:, 0:NE], tmp[:, 0:NE], ALU.bitwise_or)
                dve.drain()
                nc.vector.tensor_scalar(tmp[:, 0:NE], e_dst, DB - 1, None, ALU.bitwise_and)
                dve.drain()
                nc.vector.tensor_tensor(key[:, 0:NE], key[:, 0:NE], tmp[:, 0:NE], ALU.bitwise_or)
                dve.drain()

            def network(k, steps=range(len(plan))):
                turn = sum(kind == "turn" for kind, L, d in plan[:steps[0]])
                for n in steps:
                    kind, L, d = plan[n]
                    if kind == "turn":
                        for b in range(0, 8, 2):
                            dve.wait_ge(turned, 8 * (TURNS[k] + turn) + b + 1)
                            nc.vector.tensor_copy(keyb[(n + 1) % 2][:, b * 512:(b + 1) * 512], ps[:, b, :])
                        turn += 1
                        dve.wait_ge(odd_copied, 4 * (TURNS[k] + turn))
                    else:
                        last = network_step(kind, L, d, keyb[n % 2], keyb[(n + 1) % 2])
                        if n + 1 < len(plan) and plan[n + 1][0] == "turn":
                            last.then_inc(turn_in, 1)
                    dve.drain()
                if steps[-1] == len(plan) - 1:
                    nc.vector.tensor_copy(subh[:], keyb[KEY_BUF].rearrange("p (a b) -> p a b", b=CH)[:, :, 0]).then_inc(heads_ready, 1)

            def segments(k):
                kf = kb_i[1 - KEY_BUF]
                nc.vector.tensor_scalar(kf, kb_i[KEY_BUF], NODE_BITS, None, ALU.logical_shift_right)
                dve.wait_ge(back_in, k * 32 + 32)
                nc.vector.tensor_scalar(prevh[:], prevk[:].bitcast(i32), NODE_BITS, None, ALU.logical_shift_right)
                dve.drain()
                hi = EX[:, 0:W].bitcast(i32)
                if k == 0:
                    nc.vector.tensor_scalar(hi, kf, LOW, None, ALU.bitwise_and)
                nc.vector.tensor_tensor(keep[:, 1:W], kf[:, 1:W], kf[:, 0:W - 1], ALU.is_equal)
                nc.vector.tensor_tensor(keep[:, 0:1], kf[:, 0:1], prevh[:], ALU.is_equal).then_inc(turn_in, 1)
                dve.drain()
                if k == 0:
                    half = W // 2
                    assert half == TILES * P
                    hi2 = hi.rearrange("p (c n) -> p c n", n=half)
                    nc.vector.tensor_scalar(win[:], hi2[:, :, 0], WINDOW_END, None, ALU.min)
                    nc.vector.tensor_reduce(win_top[:], hi2, AX.X, ALU.max)
                    dve.drain()
                    nc.vector.tensor_tensor(local.rearrange("p (c n) -> p c n", n=half), hi2,
                                            win[:, :, None].to_broadcast([P, 2, half]), ALU.subtract)
                    nc.vector.tensor_tensor(win_top[:], win_top[:], win[:], ALU.subtract)
                    dve.drain()
                    nc.vector.tensor_reduce(fl[:, 3:4], win_top[:], AX.X, ALU.max)
                    dve.drain()
                    nc.vector.tensor_scalar(fl[:, 3:4], fl[:, 3:4], float(P - 1), None, ALU.is_gt)
                nc.vector.tensor_scalar(pen[:, :], keep[:, :], 2 * BIG, -BIG, ALU.mult, ALU.add).then_inc(masks_ready, 1)
                for b in range(0, 8, 2):
                    dve.wait_ge(turned, 8 * (TURNS[k] + NTURN) + b + 1)
                    nc.vector.tensor_copy(by_tile[:, :, 4 * b:4 * b + 4], ps[:, b, :].rearrange("p (j q) -> p q j", j=4))
                dve.wait_ge(odd_copied, 4 * (TURNS[k] + NTURN + 1))
                dve.drain()
                nc.vector.tensor_scalar(idx_lo, kf[:, 0:NT], LOW, None, ALU.bitwise_and)
                nc.vector.tensor_scalar(idx_hi, kf[:, 0:NT], NODE_BITS, LOW, ALU.logical_shift_right, ALU.bitwise_and)

            def search(k, queries, op, stages=range(3)):
                n = QCOLS[k]
                less = EX[:, :].bitcast(bf16)
                less1 = less[:, 0:n * P].rearrange("p (c d) -> p c d", d=P)
                less2 = less[:, 0:n * CH].rearrange("p (c d) -> p c d", d=CH)
                rows = HP[:, 0:n * CH].rearrange("p (c d) -> p c d", d=CH)

                def bc(width):
                    return queries[:, :, None].to_broadcast([P, n, width])

                if 0 in stages:
                    nc.vector.tensor_tensor(less1, headb[:, None, :].to_broadcast([P, n, P]), bc(P), op)
                    dve.drain()
                    nc.vector.tensor_reduce(r1[:, 0:n], less1, AX.X, ALU.add)
                    dve.drain()
                    nc.vector.tensor_scalar(r1[:, 0:n], r1[:, 0:n], -1.0, 0.0, ALU.add, ALU.max)
                    dve.drain()
                    nc.vector.tensor_copy(i1[:, 0:n], r1[:, 0:n]).then_inc(rows1_chosen, 1)
                if 1 in stages:
                    dve.wait_ge(g_sub, 16 * (QUERIED[k] + n))
                    nc.vector.tensor_tensor(less2, rows, bc(CH), op)
                    dve.drain()
                    nc.vector.tensor_reduce(sd[:, 0:n], less2, AX.X, ALU.add)
                    dve.drain()
                    nc.vector.tensor_scalar(sd[:, 0:n], sd[:, 0:n], -1.0, 0.0, ALU.add, ALU.max)
                    dve.drain()
                    nc.vector.scalar_tensor_tensor(r1[:, 0:n], r1[:, 0:n], float(CH), sd[:, 0:n], ALU.mult, ALU.add)
                    dve.drain()
                    nc.vector.tensor_copy(i2[:, 0:n], r1[:, 0:n]).then_inc(rows2_chosen, 1)
                if 2 in stages:
                    dve.wait_ge(g_key, 16 * (QUERIED[k] + n))
                    nc.vector.tensor_tensor(less2, rows, bc(CH), op)
                    dve.drain()
                    nc.vector.tensor_reduce(sd[:, 0:n], less2, AX.X, ALU.add)
                    dve.drain()
                    nc.vector.scalar_tensor_tensor(cle[:, 1:n + 1], r1[:, 0:n], float(CH), sd[:, 0:n],
                                                   ALU.mult, ALU.add).then_inc(counts_ready, 1)
                dve.drain()

            def ends(k):
                nc.vector.tensor_scalar(mu[:], cle[:, 1:], -1.0, 0.0, ALU.add, ALU.max)
                dve.drain()
                nc.vector.tensor_copy(e0[:], mu[:])
                dve.drain()
                nc.vector.tensor_scalar(e1[:], e0[:], (SORTED - 1) // (TILES * P) * (TILES * P), None, ALU.bitwise_and)
                nc.vector.tensor_scalar(e2[:], e0[:], P - 1, 4, ALU.bitwise_and, ALU.logical_shift_left)
                nc.vector.tensor_scalar(e3[:], e0[:], 7, TILES - 1, ALU.logical_shift_right, ALU.bitwise_and)
                dve.drain()
                nc.vector.tensor_tensor(e1[:], e1[:], e2[:], ALU.bitwise_or)
                dve.drain()
                nc.vector.tensor_tensor(endr[:], e1[:], e3[:], ALU.bitwise_or)
                dve.wait_ge(shifted, k + 1)
                nc.vector.tensor_tensor(cnt[:], cle[:, 1:], ps[:, 0, 0:NBLK], ALU.subtract)
                dve.drain()
                nc.vector.tensor_scalar(some[:], cnt[:], 0.0, None, ALU.is_gt).then_inc(order_done, 1)
                dve.drain()

            pair_keys(0, e_src, e_dst)
            network(0)
            segments(0)
            search(0, q, ALU.is_le, [0])
            dve.drain().then_inc(edges_wanted, 1)
            bucket_keys()
            quiet = plan.index(("flip", LOGW, 0))
            network(1, range(0, quiet // 3))
            search(0, q, ALU.is_le, [1])
            network(1, range(quiet // 3, quiet))
            search(0, q, ALU.is_le, [2])
            ends(0)
            network(1, range(quiet, len(plan)))
            dve.wait_ge(back_in, 64)
            search(1, qb, ALU.is_lt, [0])
            same = EX[0:P - 1, NC - W // 2:NC].bitcast(bf16)
            later = keyb[1 - KEY_BUF][0:P - 1, :]
            nc.vector.tensor_tensor(same, keyb[KEY_BUF][0:P - 1, :], later, ALU.is_equal)
            dve.drain()
            nc.vector.scalar_tensor_tensor(same, later, PAD_VALUE, same, ALU.is_lt, ALU.mult)
            dve.drain()
            nc.vector.tensor_reduce(fl[0:P - 1, 0:1], same, AX.X, ALU.max)
            dve.drain()
            search(1, qb, ALU.is_lt, [1, 2])
            dve.wait_ge(shifted, 2)
            nc.vector.tensor_tensor(mu[:, 0:BCOLS], cle[:, 1:BCOLS + 1], ps[:, 0, 0:BCOLS], ALU.subtract)
            dve.drain()
            nc.vector.tensor_reduce(fl[:, 1:2], mu[:, 0:BCOLS], AX.X, ALU.max)
            dve.drain()
            nc.vector.tensor_scalar(fl[:, 1:2], fl[:, 1:2], float(MOST), None, ALU.is_gt)
            dve.drain()
            nc.vector.tensor_reduce(fl[:, 2:3], fl[:, :], AX.X, ALU.max).then_inc(flag_in, 1)
            nc.vector.tensor_copy(e0[:, 0:BCOLS], cle[:, 1:BCOLS + 1])
            dve.drain()
            dve.wait_ge(flag_in, 2)
            nc.vector.tensor_copy(flag[:], ps[0:1, 1, 0:1]).then_inc(flag_ready, 1)
            nc.vector.tensor_scalar(i1[:, 0:BCOLS], e0[:, 0:BCOLS], 7, None, ALU.logical_shift_right)
            for bn in range(7):
                nc.vector.tensor_scalar(bit_on[:, bn, :], e0[:, 0:BCOLS], bn, 1, ALU.logical_shift_right, ALU.bitwise_and)
            dve.drain()
            nc.vector.tensor_scalar(i2[:, 0:BCOLS], i1[:, 0:BCOLS], 1.0, None, ALU.add).then_inc(starts_ready, 1)
            H = BCOLS // 2
            for h in range(2):
                dve.wait_ge(g_pairs, 32 * H * (h + 1))
                if h:
                    dve.wait_ge(b_turned, h)
                bufs = [t[:, 0:H * 2 * P].rearrange("p (c n) -> p c n", n=2 * P) for t in (EX, HP)]
                left = 2 * P
                for n, bn in enumerate(range(6, -1, -1)):
                    a, b = bufs[n % 2], bufs[(n + 1) % 2]
                    left = P + (1 << bn) - 1
                    nc.vector.tensor_copy(b[:, :, 0:left], a[:, :, 0:left])
                    dve.drain()
                    mask = bit_on[:, bn, h * H:(h + 1) * H][:, :, None].to_broadcast([P, H, left])
                    moved = nc.vector.copy_predicated(b[:, :, 0:left], mask, a[:, :, (1 << bn):(1 << bn) + left])
                    if n == 6:
                        moved.then_inc(b_shifted, 1)
                    dve.drain()
                if h == 0:
                    dve.drain().then_inc(starts_ready, 1)
            dve.drain().then_inc(cols_made, 1)
            dve.wait_ge(b_copied, 2)
            NBC = BCOLS * P
            turned_keys, nums = arena[:, 0:NBC].bitcast(i32), HP[:, 0:NBC].bitcast(i32)
            nc.vector.tensor_scalar(nums, turned_keys, 8, P - 1, ALU.logical_shift_right, ALU.bitwise_and)
            dve.drain()
            dve.wait_ge(early_free, NDB + CREDIT)
            nc.vector.tensor_copy(vS, nums)
            dve.drain()
            nc.vector.tensor_scalar(nums, turned_keys, 15, None, ALU.logical_shift_right)
            dve.wait_ge(cols_made, 2)
            dve.drain()
            nc.vector.tensor_tensor(EX[:, 0:NBC], nums, EX[:, 0:NBC].bitcast(i32), ALU.is_equal)
            dve.drain()
            nc.vector.tensor_scalar(nums, turned_keys, DB - 1, None, ALU.bitwise_and)
            dve.drain()
            nc.vector.scalar_tensor_tensor(HP[:, 0:NBC], nums, 1.0, EX[:, 0:NBC], ALU.add, ALU.mult)
            dve.drain()
            nc.vector.tensor_scalar(vD, HP[:, 0:NBC], -1.0, None, ALU.add).then_inc(b_ready, 1)
            dve.drain().then_inc(order_done, 1)

            def scan(G, k, g, op0, op1):
                dve.wait_ge(m_ready, G + (CREDIT + 1))
                dve.wait_ge(o_ready, G + (CREDIT - 1))
                dve.wait_ge(scan_done, G + CREDIT)
                nc.vector.tensor_tensor_scan(S[:, g % 2, :], msk[k][:, g * 512:(g + 1) * 512],
                                             ps[0:CH, 2 + g % 2, :], S[:, 1 - g % 2, 511:512],
                                             op0, op1).then_inc(scan_done, 1)

            def scans(before, op0, op1):
                with dve.Fori(0, NCH // 2, 1) as i:
                    for k in range(2):
                        dve.wait_ge(msk_in[k], (i * 2 + before + 2) * 8 + before // NCH * 16)
                        for g in range(GROUPS):
                            scan((i * 2 + before + k) * GROUPS + g, k, g, op0, op1)

            def layer_norm(t, n):
                tv = nodes(t)
                nc.vector.tensor_reduce(mu[:], tv, AX.X, ALU.add)
                dve.drain()
                nc.vector.tensor_scalar(mu[:], mu[:], 1.0 / CH, None, ALU.mult)
                dve.drain()
                nc.vector.tensor_tensor(tv, tv, bc_in(mu), ALU.subtract)
                dve.drain()
                nc.vector.tensor_tensor(TMP, t[:, :], t[:, :], ALU.mult)
                dve.drain()
                nc.vector.tensor_reduce(sd[:], nodes(TMP), AX.X, ALU.add)
                dve.drain()
                nc.vector.tensor_scalar(mu[:], sd[:], 1.0 / CH, EPS, ALU.mult, ALU.add).then_inc(var_ready, 1)
                dve.wait_ge(rooted, n)
                nc.vector.reciprocal(mu[:], sd[:])
                dve.drain()
                return nc.vector.tensor_tensor(tv, tv, bc_in(mu), ALU.mult)

            def one_hot_sources(d, f):
                n, k, g = place(f)
                if g == 0:
                    dve.wait_ge(win_in[k], d * (FUSED * 16) + (n // 2 + 1) * 32)
                dve.wait_ge(t_ready, d * FGROUPS + (f + CREDIT - 1))
                nc.vector.tensor_scalar(one_a[g % 2], loc[k][:, g * 512:(g + 1) * 512], pcolf[:], None,
                                        ALU.is_equal).then_inc(one_a_ready, 1)

            dve.sem_inc(scan_done, CREDIT)
            dve.wait_ge(flag_ready, 1)
            general = dve.value_load(flag[0:1, 0:1])
            with dve.If(general > 0):
                scans(0, ALU.min, ALU.max)
            with dve.Else():
                with dve.Fori(0, NDB, 1) as d:
                    one_hot_sources(d, 0)
                    for f in range(PHASES):
                        for m in share(f):
                            dve.wait_ge(count_ready, d * BPAIRS + (m + 1 + CREDIT - 7))
                            for u in range(2):
                                b = d * NBLK + (2 * m + u)
                                nc.vector.tensor_scalar(one_s[:, m % 7, u, :], iota_r[:, 0:P], vS[:, bass.ds(b, 1)],
                                                        None, ALU.is_equal)
                                last = nc.vector.tensor_scalar(one_d[:, m % 7, u, :], iota_r[:], vD[:, bass.ds(b, 1)],
                                                               None, ALU.is_equal)
                            last.then_inc(hot_ready, 1)
                        if f + 1 < FGROUPS:
                            one_hot_sources(d, f + 1)
                        if 0 <= f - 1 < FGROUPS:
                            n, k, g = place(f - 1)
                            if g == 0:
                                dve.wait_ge(msk_in[k], d * (FUSED * 8) + (n // 2 + 1) * 16)
                            scan(d * FGROUPS + (f - 1), k, g, ALU.min, ALU.max)
                dve.wait_ge(deg_summed, 1)
                nc.vector.tensor_copy(deg[:], ps[:, 7, 0:NBLK])
                dve.wait_ge(count_free, NDB * 7 + CREDIT)
            dve.wait_ge(g_end, 16 * NBLK)
            nc.vector.tensor_tensor(nodes(EX), nodes(EX), bc_out(b2b), ALU.add)
            dve.drain()
            nc.vector.tensor_tensor(TMP, EX[:], EX[:], ALU.subtract)
            nc.vector.memset(HP[:], 0.0)
            dve.drain()
            nc.vector.tensor_scalar(TMP, TMP, 0.0, None, ALU.is_equal)
            dve.drain()
            nc.vector.tensor_tensor(nodes(TMP), nodes(TMP), bc_in(some), ALU.mult)
            dve.drain()
            nc.vector.copy_predicated(HP[:], TMP.bitcast(i32), EX[:])
            dve.drain()
            nc.vector.tensor_tensor(X[:], X[:], HP[:], ALU.add)
            dve.drain()
            layer_norm(X, 1)
            dve.drain()
            nc.vector.tensor_copy(EX[:], X[:])
            dve.drain()
            n2 = 2 * PPI

            def inverse_roots(degrees):
                nc.vector.tensor_scalar(e_deg[:], degrees[:], 1.0, 1e-12, ALU.add, ALU.max).then_inc(deg_ready, 1)
                dve.wait_ge(rooted, 2)
                nc.vector.reciprocal(dinv[:], dinv[:])
                dve.drain()

            def project(r):
                with dve.Fori(0, STEPS, 1) as k:
                    nc.vector.tensor_copy(stage[:], EX[:, bass.ds(k * (PPI * P), PPI * P)]).then_inc(h_staged, 1)
                    dve.wait_ge(t_proj, r * STEPS + k + (2 * STEPS + 1))
                    nc.vector.tensor_tensor(HP[:, bass.ds(k * (PPI * P), PPI * P)].rearrange("p (c d) -> p c d", d=CH),
                                            psf[:, 1024:1024 + PPI * P].rearrange("p (c d) -> p c d", d=CH),
                                            dinv[:, bass.ds(k * n2, n2)][:, :, None].to_broadcast([P, n2, CH]),
                                            ALU.mult)
                    dve.drain()

            def out_of(r, t, tv, n, inv):
                nc.vector.tensor_tensor(tv, tv, inv, ALU.mult)
                dve.drain()
                nc.vector.tensor_tensor(tv, tv, b_cv[:, bass.ds(r * CH, CH)][:, None, :].to_broadcast([P, n, CH]), ALU.add)
                dve.drain()
                nc.vector.tensor_scalar(t, t, low_cv[:, bass.ds(r, 1)], None, ALU.max)
                dve.drain()

            with dve.If(general > 0):
                dve.drain().then_inc(ex_free, 1)
                pair_keys(2, e_dst, e_src)
                network(2)
                segments(2)
                search(2, q, ALU.is_le)
                ends(2)
                nc.vector.tensor_copy(EX[:], X[:])
                inverse_roots(cnt)
                with dve.Fori(0, 3, 1) as r:
                    project(r)
                    dve.drain().then_inc(h_ready, 1)
                    scans((r + 1) * NCH, ALU.mult, ALU.add)
                    dve.wait_ge(g_end, r * (16 * NBLK) + 32 * NBLK)
                    nc.vector.tensor_tensor(nodes(EX), nodes(EX), bc_in(some), ALU.mult)
                    dve.drain()
                    nc.vector.tensor_tensor(EX[:], EX[:], HP[:], ALU.add)
                    dve.drain()
                    out_of(r, EX[:], nodes(EX), NBLK, bc_in(dinv))
            with dve.Else():
                inverse_roots(deg)
                dve.sem_inc(sb_done, CREDIT)
                dve.drain().then_inc(degrees_done, 1)
                wide = SB * DB // P

                def split(r):
                    nc.vector.tensor_reduce(top[:], HP[:], AX.X, ALU.max, apply_absolute_value=True).then_inc(top_ready, 1)
                    dve.wait_ge(top_row, r + 1)
                    nc.vector.tensor_reduce(one1[:], ps[0:1, 4, 0:P], AX.X, ALU.max).then_inc(top_one, 1)
                    dve.wait_ge(top_all, r + 1)
                    nc.vector.tensor_scalar(top[:], ps[:, 4, 0:1], 2.0 ** -100, None, ALU.max)
                    dve.drain()
                    nc.vector.tensor_scalar(expo[:], top[:].bitcast(i32), 0x7F800000, None, ALU.bitwise_and)
                    dve.drain()
                    nc.vector.tensor_scalar(scale[:].bitcast(i32), expo[:], -1.0, float((2 * 127 + 13) << 23), ALU.mult, ALU.add)
                    nc.vector.tensor_scalar(unscale[:].bitcast(i32), expo[:], float(-(13 << 23)), None, ALU.add)
                    dve.drain()
                    nc.vector.tensor_scalar(EX[:], HP[:], scale[:], None, ALU.mult)
                    dve.drain()
                    nc.vector.tensor_copy(parts[:, :, 0:CH], nodes(EX))
                    dve.drain()
                    nc.vector.tensor_tensor(nodes(EX), nodes(EX), parts[:, :, 0:CH], ALU.subtract)
                    dve.drain()
                    nc.vector.tensor_scalar(parts[:, :, CH:P], nodes(EX), SPLIT, None, ALU.mult).then_inc(parts_ready, 1)
                    dve.drain()

                def features(n):
                    return slice_of(EX, n), slice_of(HP, n)

                def slice_of(t, n):
                    return t[:, bass.ds(n * (wide * CH), wide * CH)]

                def epilogue(r, n):
                    dve.wait_ge(joined, r * SB + n + 1)
                    o, own = features(n)
                    nc.vector.scalar_tensor_tensor(o, psf[:, 2048:2048 + wide * CH], unscale[:], own, ALU.mult,
                                                   ALU.add).then_inc(sb_done, 1)
                    dve.drain()
                    out_of(r, o, o.rearrange("p (c d) -> p c d", d=CH), wide,
                           dinv[:, bass.ds(n * wide, wide)][:, :, None].to_broadcast([P, wide, CH]))

                def project_next(r, n):
                    o, own = features(n)
                    nc.vector.tensor_copy(stage[:], o).then_inc(h_staged, 1)
                    dve.wait_ge(t_proj, r * STEPS + n + (3 * STEPS + 1))
                    nc.vector.tensor_tensor(own.rearrange("p (c d) -> p c d", d=CH),
                                            psf[:, 3072:3072 + PPI * P].rearrange("p (c d) -> p c d", d=CH),
                                            dinv[:, bass.ds(n * wide, wide)][:, :, None].to_broadcast([P, wide, CH]),
                                            ALU.mult)
                    dve.drain()

                project(0)
                with dve.Fori(0, 2, 1) as r:
                    split(r)
                    with dve.Fori(0, NDB // SB, 1) as n:
                        epilogue(r, n)
                        project_next(r, n)
                split(2)
                with dve.Fori(0, NDB // SB, 1) as n:
                    epilogue(2, n)
            nc.vector.tensor_reduce(mu[:], nodes(EX), AX.X, ALU.max)
            dve.drain()
            nc.vector.tensor_tensor(nodes(EX), nodes(EX), bc_in(mu), ALU.subtract).then_inc(shifted_down, 1)
            dve.wait_ge(exped, 1)
            nc.vector.tensor_reduce(sd[:], nodes(TMP), AX.X, ALU.add).then_inc(sum_ready, 1)
            dve.wait_ge(logged, 1)
            nc.vector.tensor_tensor(nodes(EX), nodes(EX), bc_in(mu), ALU.subtract)
            dve.drain()
            nc.vector.tensor_tensor(X[:], X[:], EX[:], ALU.add)
            dve.drain()
            layer_norm(X, 3).then_inc(out_ready, 1)


_INS = ['x', 'src', 'dst', 'L0_gnn_W1', 'L0_gnn_b1', 'L0_gnn_W2', 'L0_gnn_b2',
        'L1_gnn_W1', 'L1_gnn_b1', 'L1_gnn_W2', 'L1_gnn_b2']
_OUTS = [((N_NODES, CH), 'float32')]


def kernel(**inputs):
    import numpy as _np
    import concourse.bacc as _bacc
    from concourse import mybir as _mybir
    from concourse.bass_utils import run_bass_kernel_spmd as _run

    nc = _bacc.Bacc("TRN2", target_bir_lowering=False, num_devices=1)
    arrays, args = {}, []
    for name in _INS:
        a = _np.ascontiguousarray(inputs[name])
        arrays[f"in_{name}_dram"] = a
        args.append(nc.dram_tensor(f"in_{name}_dram", a.shape, _mybir.dt.from_np(a.dtype), kind="ExternalInput").ap())
    for i, (shape, dtype) in enumerate(_OUTS):
        dt = _mybir.dt.from_np(_np.dtype(dtype))
        args.append(nc.dram_tensor(f"out_{i}_dram", shape, dt, kind="ExternalOutput").ap())
    gnn(nc, *args)
    r = _run(nc, [arrays], core_ids=[0])
    return r.results[0]["out_0_dram"]
```
